# Optimizing a Trainium2 kernel written in Bass

```python
import numpy as np
import jax
import jax.numpy as jnp

def _softmax(x, axis=-1):
    return jax.nn.softmax(x, axis=axis)

def _gelu(x):
    return jax.nn.gelu(x, approximate=True)

def _silu(x):
    return jax.nn.silu(x)

def _sigmoid(x):
    return jax.nn.sigmoid(x)

def _layernorm(x, axis=-1, eps=1e-05):
    m = jnp.mean(x, axis=axis, keepdims=True)
    v = jnp.var(x, axis=axis, keepdims=True)
    return (x - m) / jnp.sqrt(v + eps)

def _scatter_add(tgt, idx, src, axis=0):
    return tgt.at[idx].add(src)

def _segment_sum(src, seg, n):
    return jax.ops.segment_sum(src, seg, n)
kernel_name = 'mk_decoder_postln_d1_seqx_r4_6172a6'

def setup_inputs(seed: int=0):
    np.random.seed(seed)
    _w = jnp.asarray

    def _rec_inputs():
        import jax
        import jax.numpy as jnp
        _rk = jax.random.key(seed)
        x = -9.806e-05 + 1 * jax.random.normal(jax.random.fold_in(_rk, 1), (1, 2048, 256), jnp.float32)
        _lenS = 2048 - jax.random.randint(jax.random.fold_in(_rk, 7), (1,), 0, max(1, 2048 // 4) + 1, jnp.int32)
        _lenS2 = 1601 - jax.random.randint(jax.random.fold_in(_rk, 8), (1,), 0, max(1, 1601 // 4) + 1, jnp.int32)
        _ctx_1024P = jax.random.normal(jax.random.fold_in(_rk, 11), (1, 16, 256), jnp.float32)
        _ctx_1024c = jax.random.dirichlet(jax.random.fold_in(_rk, 511), 0.3 * jnp.ones((16,), jnp.float32), (1, 1601))
        _ctx_1024t = jnp.einsum('bsk,bkd->bsd', _ctx_1024c, _ctx_1024P)
        _ctx_1024t = _ctx_1024t * jax.lax.rsqrt(jnp.mean(jnp.square(_ctx_1024t)) + 1e-12) * 0.953939
        ctx_1024 = -1.52775e-05 + 0.999936 * (_ctx_1024t + 0.3 * jax.random.normal(jax.random.fold_in(_rk, 611), (1, 1601, 256), jnp.float32))
        return (x, ctx_1024)
    x, ctx_1024 = _rec_inputs()

    def _L0_attn_setup():
        import jax, jax.numpy as jnp
        import numpy as np
        GAMMA_MIN, GAMMA_MAX = (0.15, 1.0)
        ALPHA_CAP = 1.0
        EPS_L2 = 1e-08
        EPS_RMS = 1e-06

        def _rmsnorm(x, w):
            return x * jax.lax.rsqrt(jnp.mean(x * x, axis=-1, keepdims=True) + EPS_RMS) * w

        def _l2norm(x):
            n = jnp.linalg.norm(x, axis=-1, keepdims=True)
            return x / jnp.maximum(n, EPS_L2)

        def _causal_conv(h, kernel):
            K = kernel.shape[0]
            S = h.shape[1]
            hp = jnp.pad(h, ((0, 0), (K - 1, 0), (0, 0)))
            out = jnp.zeros_like(h)
            for j in range(K):
                out = out + kernel[j] * hp[:, K - 1 - j:K - 1 - j + S, :]
            return out
        B, S, D, R, K = (8, 256, 256, 16, 4)
        key = jax.random.key(seed)
        ks = jax.random.split(key, 8)
        return {'h': jax.random.normal(ks[0], (B, S, D), dtype=jnp.float32), 'u': jax.random.normal(ks[1], (D, R), dtype=jnp.float32) * 0.05, 'v': jax.random.normal(ks[2], (D, R), dtype=jnp.float32) * 0.05, 'decay_logit': jnp.zeros((R,), jnp.float32), 'alpha_logit': jnp.zeros((R,), jnp.float32), 'k_base_gate_logit': jnp.float32(0.0), 'k_base_kernel': jax.random.normal(ks[3], (K,), dtype=jnp.float32) * 0.05, 'proj_w': jax.random.normal(ks[4], (D, D), dtype=jnp.float32) * 0.02, 'proj_b': jnp.zeros((D,), jnp.float32), 'norm1_w': jnp.ones((D,), jnp.float32), 'norm2_w': jnp.ones((D,), jnp.float32), 'mlp_w1': jax.random.normal(ks[5], (D, 4 * D), dtype=jnp.float32) * 0.02, 'mlp_b1': jnp.zeros((4 * D,), jnp.float32), 'mlp_w2': jax.random.normal(ks[6], (4 * D, D), dtype=jnp.float32) * 0.02, 'mlp_b2': jnp.zeros((D,), jnp.float32)}
    _L0_attn_all = _L0_attn_setup()
    _L0_attn_in = {k: v for k, v in _L0_attn_all.items() if k in ('u', 'v', 'decay_logit', 'alpha_logit', 'k_base_gate_logit', 'k_base_kernel', 'proj_w', 'proj_b', 'norm1_w', 'norm2_w', 'mlp_w1', 'mlp_b1', 'mlp_w2', 'mlp_b2')}
    del _L0_attn_all

    def _L0_xattn_setup():
        import jax, jax.numpy as jnp
        import numpy as np
        EPS = 1e-06
        NUM_ITERS = 3

        def rmsnorm(x, w, eps=EPS):
            return x * jax.lax.rsqrt(jnp.mean(x * x, axis=-1, keepdims=True) + eps) * w

        def gru_cell(x, h, wi, wh, bi, bh):
            d = h.shape[-1]
            gi = jnp.einsum('...d,ed->...e', x, wi) + bi
            gh = jnp.einsum('...d,ed->...e', h, wh) + bh
            ir, iz, inn = (gi[..., :d], gi[..., d:2 * d], gi[..., 2 * d:])
            hr, hz, hn = (gh[..., :d], gh[..., d:2 * d], gh[..., 2 * d:])
            r = jax.nn.sigmoid(ir + hr)
            z = jax.nn.sigmoid(iz + hz)
            n = jnp.tanh(inn + r * hn)
            return (1.0 - z) * n + z * h
        key = jax.random.key(seed)
        ks = jax.random.split(key, 12)
        B, K, M, d = (8, 64, 1024, 256)
        s = 0.02
        return {'slots': jax.random.normal(ks[0], (B, K, d), jnp.float32), 'P': jax.random.normal(ks[1], (B, M, d), jnp.float32), 'Wq': jax.random.normal(ks[2], (d, d), jnp.float32) * s, 'Wk': jax.random.normal(ks[3], (d, d), jnp.float32) * s, 'Wv': jax.random.normal(ks[4], (d, d), jnp.float32) * s, 'gru_wi': jax.random.normal(ks[5], (3 * d, d), jnp.float32) * s, 'gru_wh': jax.random.normal(ks[6], (3 * d, d), jnp.float32) * s, 'gru_bi': jax.random.normal(ks[7], (3 * d,), jnp.float32) * s, 'gru_bh': jax.random.normal(ks[8], (3 * d,), jnp.float32) * s, 'slot_norm_w': jnp.ones((d,), jnp.float32), 'input_norm_w': jnp.ones((d,), jnp.float32)}
    _L0_xattn_all = _L0_xattn_setup()
    _L0_xattn_in = {k: v for k, v in _L0_xattn_all.items() if k in ('Wq', 'Wk', 'Wv', 'gru_wi', 'gru_wh', 'gru_bi', 'gru_bh', 'slot_norm_w', 'input_norm_w')}
    del _L0_xattn_all

    def _L0_ffn_setup():
        import jax, jax.numpy as jnp
        import numpy as np
        EMBED_DIM = 256
        MLP_DIM = 1024
        NUM_EXPERTS = 8
        TOP_K = 2
        BATCH, SEQ = (4, 512)
        key = jax.random.key(seed)
        ks = jax.random.split(key, 8)
        scale = 0.02
        hidden_states = jax.random.normal(ks[0], (BATCH, SEQ, EMBED_DIM), dtype=jnp.float32)
        router_w = jax.random.normal(ks[1], (EMBED_DIM, NUM_EXPERTS), dtype=jnp.float32) * scale
        router_b = jnp.zeros((NUM_EXPERTS,), dtype=jnp.float32)
        expert_bias = jnp.zeros((NUM_EXPERTS,), dtype=jnp.float32)
        w1 = jax.random.normal(ks[2], (NUM_EXPERTS, EMBED_DIM, MLP_DIM), dtype=jnp.float32) * scale
        b1 = jnp.zeros((NUM_EXPERTS, MLP_DIM), dtype=jnp.float32)
        w2 = jax.random.normal(ks[3], (NUM_EXPERTS, MLP_DIM, EMBED_DIM), dtype=jnp.float32) * scale
        b2 = jnp.zeros((NUM_EXPERTS, EMBED_DIM), dtype=jnp.float32)
        return {'hidden_states': hidden_states, 'router_w': router_w, 'router_b': router_b, 'expert_bias': expert_bias, 'w1': w1, 'b1': b1, 'w2': w2, 'b2': b2}
    _L0_ffn_all = _L0_ffn_setup()
    _L0_ffn_in = {k: v for k, v in _L0_ffn_all.items() if k in ('router_w', 'router_b', 'expert_bias', 'w1', 'b1', 'w2', 'b2')}
    del _L0_ffn_all
    return {'x': x, 'ctx_1024': ctx_1024, 'L0_attn_u': _L0_attn_in['u'], 'L0_attn_v': _L0_attn_in['v'], 'L0_attn_decay_logit': _L0_attn_in['decay_logit'], 'L0_attn_alpha_logit': _L0_attn_in['alpha_logit'], 'L0_attn_k_base_gate_logit': _L0_attn_in['k_base_gate_logit'], 'L0_attn_k_base_kernel': _L0_attn_in['k_base_kernel'], 'L0_attn_proj_w': _L0_attn_in['proj_w'], 'L0_attn_proj_b': _L0_attn_in['proj_b'], 'L0_attn_norm1_w': _L0_attn_in['norm1_w'], 'L0_attn_norm2_w': _L0_attn_in['norm2_w'], 'L0_attn_mlp_w1': _L0_attn_in['mlp_w1'], 'L0_attn_mlp_b1': _L0_attn_in['mlp_b1'], 'L0_attn_mlp_w2': _L0_attn_in['mlp_w2'], 'L0_attn_mlp_b2': _L0_attn_in['mlp_b2'], 'L0_xattn_Wq': _L0_xattn_in['Wq'], 'L0_xattn_Wk': _L0_xattn_in['Wk'], 'L0_xattn_Wv': _L0_xattn_in['Wv'], 'L0_xattn_gru_wi': _L0_xattn_in['gru_wi'], 'L0_xattn_gru_wh': _L0_xattn_in['gru_wh'], 'L0_xattn_gru_bi': _L0_xattn_in['gru_bi'], 'L0_xattn_gru_bh': _L0_xattn_in['gru_bh'], 'L0_xattn_slot_norm_w': _L0_xattn_in['slot_norm_w'], 'L0_xattn_input_norm_w': _L0_xattn_in['input_norm_w'], 'L0_ffn_router_w': _L0_ffn_in['router_w'], 'L0_ffn_router_b': _L0_ffn_in['router_b'], 'L0_ffn_expert_bias': _L0_ffn_in['expert_bias'], 'L0_ffn_w1': _L0_ffn_in['w1'], 'L0_ffn_b1': _L0_ffn_in['b1'], 'L0_ffn_w2': _L0_ffn_in['w2'], 'L0_ffn_b2': _L0_ffn_in['b2']}

def reference(x, ctx_1024, L0_attn_u, L0_attn_v, L0_attn_decay_logit, L0_attn_alpha_logit, L0_attn_k_base_gate_logit, L0_attn_k_base_kernel, L0_attn_proj_w, L0_attn_proj_b, L0_attn_norm1_w, L0_attn_norm2_w, L0_attn_mlp_w1, L0_attn_mlp_b1, L0_attn_mlp_w2, L0_attn_mlp_b2, L0_xattn_Wq, L0_xattn_Wk, L0_xattn_Wv, L0_xattn_gru_wi, L0_xattn_gru_wh, L0_xattn_gru_bi, L0_xattn_gru_bh, L0_xattn_slot_norm_w, L0_xattn_input_norm_w, L0_ffn_router_w, L0_ffn_router_b, L0_ffn_expert_bias, L0_ffn_w1, L0_ffn_b1, L0_ffn_w2, L0_ffn_b2):
    import jax
    import jax.numpy as jnp

    def _L0_attn_ref(h, u, v, decay_logit, alpha_logit, k_base_gate_logit, k_base_kernel, proj_w, proj_b, norm1_w, norm2_w, mlp_w1, mlp_b1, mlp_w2, mlp_b2):
        import jax, jax.numpy as jnp
        import numpy as np
        GAMMA_MIN, GAMMA_MAX = (0.15, 1.0)
        ALPHA_CAP = 1.0
        EPS_L2 = 1e-08
        EPS_RMS = 1e-06

        def _rmsnorm(x, w):
            return x * jax.lax.rsqrt(jnp.mean(x * x, axis=-1, keepdims=True) + EPS_RMS) * w

        def _l2norm(x):
            n = jnp.linalg.norm(x, axis=-1, keepdims=True)
            return x / jnp.maximum(n, EPS_L2)

        def _causal_conv(h, kernel):
            K = kernel.shape[0]
            S = h.shape[1]
            hp = jnp.pad(h, ((0, 0), (K - 1, 0), (0, 0)))
            out = jnp.zeros_like(h)
            for j in range(K):
                out = out + kernel[j] * hp[:, K - 1 - j:K - 1 - j + S, :]
            return out
        B, S, D = h.shape
        R = u.shape[1]
        residual = h
        h_norm = _rmsnorm(h, norm1_w)
        gate = jax.nn.sigmoid(k_base_gate_logit)
        out = gate * _causal_conv(h_norm, k_base_kernel)
        alpha = ALPHA_CAP * jax.nn.sigmoid(alpha_logit)
        qk = h_norm @ jnp.concatenate((u, v), axis=1)
        q_raw, k_raw = (qk[..., :R], qk[..., R:])
        q = _l2norm(q_raw)
        k = _l2norm(k_raw)
        gamma = jnp.clip(jax.nn.sigmoid(decay_logit), GAMMA_MIN, GAMMA_MAX)
        pos = jnp.arange(S, dtype=h.dtype)
        diff = jnp.maximum(pos[:, None] - pos[None, :], 0.0)
        mask = jnp.tril(jnp.ones((S, S), dtype=h.dtype))
        w = gamma[:, None, None] ** diff * mask
        q_alpha = q * alpha
        A = jnp.einsum('bir,bjr,rij->bij', q_alpha, k, w)
        decay_out = jnp.einsum('bij,bjd->bid', A, h_norm)
        out = out + decay_out
        out = out @ proj_w.T + proj_b
        h2 = residual + out
        hn2 = _rmsnorm(h2, norm2_w)
        mlp_out = jax.nn.gelu(hn2 @ mlp_w1 + mlp_b1) @ mlp_w2 + mlp_b2
        return h2 + mlp_out

    def _L0_xattn_ref(slots, P, Wq, Wk, Wv, gru_wi, gru_wh, gru_bi, gru_bh, slot_norm_w, input_norm_w):
        import jax, jax.numpy as jnp
        import numpy as np
        EPS = 1e-06
        NUM_ITERS = 3

        def rmsnorm(x, w, eps=EPS):
            return x * jax.lax.rsqrt(jnp.mean(x * x, axis=-1, keepdims=True) + eps) * w

        def gru_cell(x, h, wi, wh, bi, bh):
            d = h.shape[-1]
            gi = jnp.einsum('...d,ed->...e', x, wi) + bi
            gh = jnp.einsum('...d,ed->...e', h, wh) + bh
            ir, iz, inn = (gi[..., :d], gi[..., d:2 * d], gi[..., 2 * d:])
            hr, hz, hn = (gh[..., :d], gh[..., d:2 * d], gh[..., 2 * d:])
            r = jax.nn.sigmoid(ir + hr)
            z = jax.nn.sigmoid(iz + hz)
            n = jnp.tanh(inn + r * hn)
            return (1.0 - z) * n + z * h
        d = slots.shape[-1]
        scale = d ** (-0.5)
        Pn = rmsnorm(P, input_norm_w)
        k_proj = jnp.einsum('bmd,ed->bme', Pn, Wk)
        v_proj = jnp.einsum('bmd,ed->bme', Pn, Wv)
        for _ in range(NUM_ITERS):
            sn = rmsnorm(slots, slot_norm_w)
            q = jnp.einsum('bkd,ed->bke', sn, Wq)
            scores = jnp.einsum('bkd,bmd->bkm', q, k_proj) * scale
            attn = jax.nn.softmax(scores, axis=-2)
            attn = attn / (jnp.sum(attn, axis=-1, keepdims=True) + EPS)
            updates = jnp.einsum('bkm,bmd->bkd', attn, v_proj)
            slots = gru_cell(updates, slots, gru_wi, gru_wh, gru_bi, gru_bh)
        return slots

    def _L0_ffn_ref(hidden_states, router_w, router_b, expert_bias, w1, b1, w2, b2):
        import jax, jax.numpy as jnp
        import numpy as np
        EMBED_DIM = 256
        MLP_DIM = 1024
        NUM_EXPERTS = 8
        TOP_K = 2
        BATCH, SEQ = (4, 512)
        B, S, D = hidden_states.shape
        E = w1.shape[0]
        x = hidden_states.reshape(-1, D)
        T = x.shape[0]
        logits = x @ router_w + router_b + expert_bias
        probs = jax.nn.softmax(logits, axis=-1)
        top_v, top_i = jax.lax.top_k(probs, TOP_K)
        top_v = top_v / (jnp.sum(top_v, axis=-1, keepdims=True) + 1e-09)
        gates = jnp.zeros((T, E), dtype=x.dtype).at[jnp.arange(T)[:, None], top_i].set(top_v)

        def body(acc, params):
            W1, B1, W2, B2, g = params
            h = jax.nn.gelu(x @ W1 + B1, approximate=False)
            y = h @ W2 + B2
            return (acc + g[:, None] * y, None)
        out, _ = jax.lax.scan(body, jnp.zeros_like(x), (w1, b1, w2, b2, gates.T))
        return out.reshape(B, S, D)
    x = _layernorm(x + _L0_attn_ref(x, L0_attn_u, L0_attn_v, L0_attn_decay_logit, L0_attn_alpha_logit, L0_attn_k_base_gate_logit, L0_attn_k_base_kernel, L0_attn_proj_w, L0_attn_proj_b, L0_attn_norm1_w, L0_attn_norm2_w, L0_attn_mlp_w1, L0_attn_mlp_b1, L0_attn_mlp_w2, L0_attn_mlp_b2), axis=-1)
    x = _layernorm(x + _L0_xattn_ref(x, ctx_1024, L0_xattn_Wq, L0_xattn_Wk, L0_xattn_Wv, L0_xattn_gru_wi, L0_xattn_gru_wh, L0_xattn_gru_bi, L0_xattn_gru_bh, L0_xattn_slot_norm_w, L0_xattn_input_norm_w), axis=-1)
    x = _layernorm(x + _L0_ffn_ref(x, L0_ffn_router_w, L0_ffn_router_b, L0_ffn_expert_bias, L0_ffn_w1, L0_ffn_b1, L0_ffn_w2, L0_ffn_b2), axis=-1)
    return x

_drawn_inputs = setup_inputs


def setup_inputs(seed=0):
    import zlib

    import numpy as np

    out = dict(_drawn_inputs(seed))
    spreads = {'L0_attn_decay_logit': (0.0, 2.0),
     'L0_attn_alpha_logit': (0.0, 2.0),
     'L0_attn_proj_b': (0.0, 0.1),
     'L0_attn_norm1_w': (1.0, 0.6),
     'L0_attn_norm2_w': (1.0, 0.6),
     'L0_attn_mlp_b1': (0.0, 0.345),
     'L0_attn_mlp_b2': (0.0, 0.1),
     'L0_xattn_slot_norm_w': (1.0, 0.6),
     'L0_xattn_input_norm_w': (1.0, 0.6),
     'L0_ffn_router_b': (0.0, 0.1),
     'L0_ffn_expert_bias': (0.0, 0.1),
     'L0_ffn_b1': (0.0, 0.309),
     'L0_ffn_b2': (0.0, 0.1)}
    factors = {'L0_attn_k_base_kernel': 3.777,
     'L0_xattn_Wq': 8.0,
     'L0_xattn_Wk': 8.0,
     'L0_xattn_gru_bi': 3.318,
     'L0_xattn_gru_bh': 4.959}
    for name, (base, spread) in spreads.items():
        noise = np.random.default_rng([zlib.crc32(name.encode()), seed]).standard_normal(out[name].shape)
        drawn = base * np.exp(spread * noise) if base else spread * noise
        out[name] = jnp.asarray(drawn.astype(out[name].dtype))
    for name, factor in factors.items():
        out[name] = (out[name] * factor).astype(out[name].dtype)
    return out
```

```python
from contextlib import ExitStack

import concourse.bass as bass
from concourse import mybir

F32 = mybir.dt.float32
F32R = mybir.dt.float32r
I32 = mybir.dt.int32
ALU = mybir.AluOpType
ACT = mybir.ActivationFunctionType
AX_X = mybir.AxisListType.X

P = 128
T = 2048
D = 256
DH = D // P
NT = T // P
CH = 512
NC = T // CH
TPC = CH // P
R = 16
SUB = 32
NSUB = P // SUB
KTAP = 4
F = 4 * D
FT = F // P
M = 1601
MT = -(-M // P)
MROWS = [min(P, M - m * P) for m in range(MT)]
ITERS = 3
NE = 8
EPS_LN = 1e-5
EPS_RMS = 1e-6
RSQRT_MAGIC = float(0x5F3759DF)
NEWTON = 3
RSQRT_STEPS = 2 + 3 * NEWTON


def bc(ap, axis, n):
    return ap.unsqueeze(axis).broadcast_to([*ap.shape[:axis], n, *ap.shape[axis:]])


class Chain:

    def __init__(self, eng, sem, base=0):
        self.eng, self.sem, self.n, self.base = eng, sem, 0, base

    def step(self, ins):
        self.n += 1
        ins.then_inc(self.sem, 1)
        self.eng.wait_ge(self.sem, self.base + self.n)

    def mark(self, ins):
        self.n += 1
        ins.then_inc(self.sem, 1)
        return self.base + self.n


def rsqrt_steps(v, chain, y, x, tmp):
    chain.step(v.tensor_scalar(tmp.bitcast(I32), x.bitcast(I32), 1, None, ALU.logical_shift_right))
    chain.step(v.tensor_scalar(y.bitcast(I32), tmp.bitcast(I32), -1.0, RSQRT_MAGIC, ALU.mult, ALU.add))
    for _ in range(NEWTON):
        chain.step(v.scalar_tensor_tensor(out=tmp, in0=y, scalar=-0.5, in1=y, op0=ALU.mult, op1=ALU.mult))
        chain.step(v.tensor_tensor(tmp, tmp, x, ALU.mult))
        chain.step(v.scalar_tensor_tensor(out=y, in0=tmp, scalar=1.5, in1=y, op0=ALU.add, op1=ALU.mult))


def three_pass(pe, out, w_hi, w_lo, x_hi, x_lo, start, stop):
    pe.matmul(out, w_hi, x_lo, start=start, stop=False)
    pe.matmul(out, w_lo, x_hi, start=False, stop=False)
    return pe.matmul(out, w_hi, x_hi, start=False, stop=stop)


def decay_attention_and_mlp(nc, io, shared):
    ident, ones, sT = shared["ident"], shared["ones"], shared["sT"]
    with ExitStack() as ctx:
        def sb(name, shape, dt=F32):
            return ctx.enter_context(nc.sbuf_tensor(name, shape, dt))

        def sem(name):
            return ctx.enter_context(nc.semaphore(name))

        bank = [ctx.enter_context(nc.psum_tensor(f"a_bank{i}", [P, CH], F32)) for i in range(8)]

        x = sb("a_x", [P, NT, D])
        hn = sb("a_hn", [P, NT, D])
        h2 = sb("a_h2", [P, NT, D])
        n2 = sb("a_n2", [P, 2, TPC, D])
        xT = oT = sT
        hT_hi = sb("a_hT_hi", [P, DH, 3 * CH], F32R)
        hT_lo = sb("a_hT_lo", [P, DH, 3 * CH], F32R)
        g32 = sb("a_g32", [P, 2, CH])
        g_hi = sb("a_g_hi", [P, FT, CH], F32R)
        g_lo = sb("a_g_lo", [P, FT, CH], F32R)
        w1_32 = sb("a_w1_32", [P, DH * F])
        w2_32 = n2[:].rearrange("p a t d -> p (a t d)")
        w1_hi = sb("a_w1_hi", [P, DH, F], F32R)
        w1_lo = sb("a_w1_lo", [P, DH, F], F32R)
        w2_hi = sb("a_w2_hi", [P, FT, D], F32R)
        w2_lo = sb("a_w2_lo", [P, FT, D], F32R)
        projT = sb("a_projT", [P, DH, D])
        uv = sb("a_uv", [P, DH, 2 * R])
        rows = sb("a_rows", [P, 3, D])
        cols = sb("a_cols", [P, 2 * DH + FT])
        sg = sb("a_sg", [P, 2 * R + 2])
        traw = sb("a_traw", [P, KTAP])
        lg = sb("a_lg", [P, R + 1])
        gk = sb("a_gk", [P, KTAP])
        expo = sb("a_expo", [P, 2, NSUB + 1], I32)
        expf = sb("a_expf", [P, 2, NSUB + 1])
        kw = sb("a_kw", [P, NSUB + 1, R])
        qw = sb("a_qw", [P, NSUB + 1, R])
        coef = sb("a_coef", [P, 1])
        taps = sb("a_taps", [P, KTAP, P + KTAP - 1])
        band = sb("a_band", [P, P + KTAP - 1])
        later = sb("a_later", [P, P])
        qk = sb("a_qk", [P, NT, 2, R])
        qkn = sb("a_qkn", [P, NT * 2])
        qkr = sb("a_qkr", [P, NT * 2])
        kcat = sb("a_kcat", [P, NT, 6, R])
        qcat = sb("a_qcat", [P, NT, 6, R])
        qkT = sb("a_qkT", [96, 3, 2 * P])
        AT = sb("a_AT", [P, 2, P])
        S = sb("a_S", [P, 4, D])
        ss = sb("a_ss", [P, NT])
        rs = sb("a_rs", [P, NT])
        tmp = sb("a_tmp", [P, 2 * NT])
        junk = sb("a_junk", [P, 2, D])
        qk_sq = junk[:].rearrange("p a (t b r) -> p (a t) b r", b=2, r=R)
        stats = sb("a_stats", [P, NT, 6])
        mv = sb("a_mv", [P, NT, 2])

        ld_x, ld_xT, ld_w, ld_mlp = sem("a_ld_x"), sem("a_ld_xT"), sem("a_ld_w"), sem("a_ld_mlp")
        consts, masked, hi_w = sem("a_consts"), sem("a_masked"), sem("a_hi_w")
        vchain, achain, gchain = sem("a_vchain"), sem("a_achain"), sem("a_gchain")
        squares, zeroed, gammas, expos, coef_ok = (sem(f"a_{n}") for n in ("squares", "zeroed", "gammas", "expos", "coef_ok"))
        hn_ok, uv_ok, qk_mm, cats = sem("a_hn_ok"), sem("a_uv_ok"), sem("a_qk_mm"), sem("a_cats")
        turned, turned_sb = sem("a_turned"), sem("a_turned_sb")
        A_mm, A_sb, o_mm, o_sb, S_mm, S_sb = (sem(f"a_{n}") for n in ("A_mm", "A_sb", "o_mm", "o_sb", "S_mm", "S_sb"))
        xb_ok, h2_mm, h2_sb, sq2, n2_ok = (sem(f"a_{n}") for n in ("xb_ok", "h2_mm", "h2_sb", "sq2", "n2_ok"))
        hT_mm, hT_hi_ok, hT_lo_ok, w_lo_ok = sem("a_hT_mm"), sem("a_hT_hi_ok"), sem("a_hT_lo_ok"), sem("a_w_lo_ok")
        up_mm, gelu_ok, g_ok, y_mm, z_ok, res_ok = (sem(f"a_{n}") for n in ("up_mm", "gelu_ok", "g_ok", "y_mm", "z_ok", "res_ok"))
        x1_ok, x1_mm, x1_sb, x1_out = (sem(f"a_{n}") for n in ("x1_ok", "x1_mm", "x1_sb", "x1_out"))

        zeros = sb("a_zeros", [P, 2 * D])
        zeros_ok, zero_out = sem("a_zeros_ok"), sem("a_zero_out")

        def tile(t):
            return slice(t * P, (t + 1) * P)

        def chunk(c):
            return slice(c * CH, (c + 1) * CH)

        block = ctx.enter_context(nc.Block())

        @block.sync
        def _(sp):
            sp.dma_start(x[:], io["x"].rearrange("(t p) d -> p t d", p=P)).then_inc(ld_x, 16)
            sp.dma_start(w1_32[:].rearrange("p (c f) -> p c f", c=DH),
                         io["mlp_w1"].rearrange("(c p) f -> p c f", p=P)).then_inc(ld_mlp, 16)
            sp.dma_start(w2_32.rearrange("p (c f) -> p c f", c=FT),
                         io["mlp_w2"].rearrange("(c p) f -> p c f", p=P)).then_inc(ld_mlp, 16)
            if "routed" in io:
                rows_of = io["routed"].rearrange("(i p s) d -> p i (s d)", p=P, s=2)
                n = rows_of.shape[1]
                sp.wait_ge(zeros_ok, 1)
                sp.dma_start(rows_of, bc(zeros[:], 1, n)).then_inc(zero_out, 16)
                sp.wait_ge(zero_out, 16)
            sp.wait_ge(x1_ok, NC)
            sp.dma_start(io["x1"].rearrange("(t p) d -> p t d", p=P), h2[:]).then_inc(x1_out, 16)
            sp.wait_ge(x1_out, 16)

        @block.gpsimd
        def _(pool):
            g = Chain(pool, gchain)
            pool.memset(zeros[:], 0.0).then_inc(zeros_ok, 1)
            g.step(pool.memset(ident[:], 0.0))
            g.step(pool.memset(later[:], 1.0))
            g.step(pool.memset(taps[:], 0.0))
            g.step(pool.affine_select(out=ident[:], in_=ident[:], compare_op=ALU.not_equal, fill=1.0,
                                      base=0, pattern=[[-1, P]], channel_multiplier=1))
            g.step(pool.affine_select(out=later[:], in_=later[:], compare_op=ALU.is_ge, fill=0.0,
                                      base=0, pattern=[[1, P]], channel_multiplier=-1))
            for t in range(KTAP):
                g.step(pool.affine_select(out=taps[:, t, 0:P], in_=taps[:, t, 0:P], compare_op=ALU.not_equal,
                                          fill=1.0, base=-t, pattern=[[1, P]], channel_multiplier=-1))
                g.step(pool.affine_select(out=taps[:, t, P:], in_=taps[:, t, P:], compare_op=ALU.not_equal,
                                          fill=1.0, base=KTAP - 1 - t, pattern=[[-1, KTAP - 1]],
                                          channel_multiplier=1))
            g.step(pool.iota(expo[:, 0, :], pattern=[[SUB, NSUB + 1]], base=0, channel_multiplier=-1))
            g.step(pool.iota(expo[:, 1, 0:NSUB], pattern=[[-SUB, NSUB]], base=0, channel_multiplier=1))
            g.step(pool.iota(expo[:, 1, NSUB:], pattern=[[0, 1]], base=0, channel_multiplier=1))
            g.step(pool.memset(coef[:], 1.0))
            g.step(pool.affine_select(out=coef[:], in_=coef[:], compare_op=ALU.is_ge, fill=0.0,
                                      base=64 + R - 1, pattern=[[0, 1]], channel_multiplier=-1))
            g.step(pool.memset(kcat[:], 0.0))
            g.step(pool.memset(qcat[:], 0.0))
            g.step(pool.affine_select(out=kcat[:, :, 5, 0:KTAP - 1], in_=kcat[:, :, 5, 0:KTAP - 1],
                                      compare_op=ALU.not_equal, fill=1.0, base=-(P - KTAP + 1),
                                      pattern=[[0, NT], [-1, KTAP - 1]], channel_multiplier=1))
            g.step(pool.memset(ones[:], 1.0))
            pool.memset(S[:], 0.0).then_inc(consts, 1)
            pool.wait_ge(gammas, 4)
            g.step(pool.affine_select(out=kw[:, 0:NSUB, :], in_=kw[:, 0:NSUB, :], compare_op=ALU.is_ge, fill=0.0,
                                      base=SUB - 1, pattern=[[SUB, NSUB], [0, R]], channel_multiplier=-1))
            g.step(pool.affine_select(out=qw[:, 0:NSUB, :], in_=qw[:, 0:NSUB, :], compare_op=ALU.is_ge, fill=0.0,
                                      base=SUB - 1, pattern=[[SUB, NSUB], [0, R]], channel_multiplier=-1))
            pool.affine_select(out=qw[:, 0:NSUB, :], in_=qw[:, 0:NSUB, :], compare_op=ALU.is_ge, fill=0.0,
                               base=0, pattern=[[-SUB, NSUB], [0, R]], channel_multiplier=1).then_inc(masked, 1)
            pool.wait_ge(ld_w, 16 * 9)
            pool.wait_ge(ld_x, 16)
            for t in range(NT):
                pool.tensor_tensor(h2[:, t], x[:, t], rows[:, 1], ALU.add).then_inc(xb_ok, 1)
            for t in range(NT):
                pool.wait_ge(h2_sb, t + 1)
                g.step(pool.tensor_tensor(hn[:, t], h2[:, t], x[:, t], ALU.add))
                pool.tensor_tensor(hn[:, t], hn[:, t], rows[:, 2], ALU.add).then_inc(res_ok, 1)

        @block.scalar
        def _(act):
            act.dma_start(xT[:], io["xT"].rearrange("(c p) t -> p c t", p=P)).then_inc(ld_xT, 16)
            act.dma_start(cols[:], io["a_cols"]).then_inc(ld_xT, 16)
            act.dma_start(uv[:, :, 0:R], io["u"].rearrange("(c p) r -> p c r", p=P)).then_inc(ld_xT, 16)
            act.dma_start(uv[:, :, R:], io["v"].rearrange("(c p) r -> p c r", p=P)).then_inc(ld_xT, 16)
            for i, name in enumerate(("norm1_w", "proj_b", "mlp_b2")):
                act.dma_start(rows[:, i], io[name].partition_broadcast(P)).then_inc(ld_w, 16)
            act.wait_ge(zeroed, 1)
            act.dma_start(sg[:, 0:R], io["decay"].partition_broadcast(P)).then_inc(ld_w, 16)
            act.dma_start(sg[:, R:2 * R], io["alpha"].partition_broadcast(P)).then_inc(ld_w, 16)
            act.dma_start(sg[64:64 + R, 2 * R:2 * R + 1], io["decay"].unsqueeze(1)).then_inc(ld_w, 16)
            act.dma_start(sg[:, 2 * R + 1:], io["gate"].partition_broadcast(P)).then_inc(ld_w, 16)
            act.dma_start(traw[:], io["taps"].partition_broadcast(P)).then_inc(ld_w, 16)
            act.dma_start(projT[:], io["projT"].rearrange("(c p) f -> p c f", p=P)).then_inc(ld_w, 16)
            act.wait_ge(ld_x, 16)
            for t in range(NT):
                if t >= 2:
                    act.wait_ge(squares, t - 1)
                act.activation(junk[:, t % 2], x[:, t], ACT.Square, accum_out=ss[:, t:t + 1]).then_inc(squares, 1)
            act.wait_ge(ld_w, 16 * 9)
            act.activation(sg[:], sg[:], ACT.Exp, scale=-1.0).then_inc(gammas, 1)
            act.wait_ge(expos, 1)
            act.activation(lg[:], lg[:], ACT.Ln).then_inc(gammas, 1)
            act.wait_ge(coef_ok, 1)
            act.activation(kw[:], kw[:], ACT.Exp).then_inc(gammas, 1)
            act.activation(qw[:], qw[:], ACT.Exp).then_inc(gammas, 1)
            act.activation(lg[:, R:], lg[:, R:], ACT.Exp, scale=float(P)).then_inc(gammas, 1)
            act.wait_ge(ld_mlp, 32)
            act.activation(w1_hi[:].rearrange("p c f -> p (c f)"), w1_32[:], ACT.Copy).then_inc(hi_w, 1)
            act.activation(w2_hi[:].rearrange("p c f -> p (c f)"), w2_32, ACT.Copy).then_inc(hi_w, 1)
            for t in range(NT + 2):
                if t < NT:
                    act.wait_ge(turned, t + 1)
                    if t >= 3:
                        act.wait_ge(o_mm, t - 2)
                    act.activation(qkT[:, t % 3], bank[t % 2][0:96, 0:2 * P], ACT.Copy).then_inc(turned_sb, 1)
                if t >= 2:
                    act.wait_ge(o_mm, t - 1)
                    act.activation(oT[:, :, tile(t - 2)], bank[4 + t % 2][:, 0:2 * P].rearrange("p (c t) -> p c t", c=DH),
                                   ACT.Copy).then_inc(o_sb, 1)
            for t in range(NT):
                act.wait_ge(h2_sb, t + 1)
                act.wait_ge(squares, NT + t - 1)
                act.activation(junk[:, t % 2], h2[:, t], ACT.Square, accum_out=ss[:, t:t + 1]).then_inc(squares, 1)

            def high_part(c):
                for h in range(DH):
                    act.wait_ge(hT_mm, DH * c + h + 1)
                    act.activation(hT_hi[:, h, chunk(c % 3)], bank[2 + (c % 2) * 2 + h][:], ACT.Copy,
                                   scale=cols[:, 2 + h:3 + h]).then_inc(hT_hi_ok, 1)

            high_part(0)
            high_part(1)
            for c in range(NC):
                for f in range(FT):
                    n = c * FT + f
                    act.wait_ge(up_mm, n + 1)
                    if n >= 2:
                        act.wait_ge(g_ok, n - 1)
                    act.activation(g32[:, f % 2], bank[6 + f % 2][:], ACT.Gelu_apprx_tanh,
                                   bias=cols[:, 4 + f:5 + f]).then_inc(gelu_ok, 1)
                    if f == 3 and c + 2 < NC:
                        high_part(c + 2)
            for c in range(NC):
                for h in range(DH):
                    act.wait_ge(x1_mm, DH * c + h + 1)
                    act.activation(sT[:, h, chunk(c)], bank[2 + (c % 2) * 2 + h][:], ACT.Copy).then_inc(x1_sb, 1)

        def low_part(v, c):
            for h in range(DH):
                v.wait_ge(hT_hi_ok, DH * c + h + 1)
                v.scalar_tensor_tensor(out=hT_lo[:, h, chunk(c % 3)], in0=bank[2 + (c % 2) * 2 + h][:],
                                       scalar=cols[:, 2 + h:3 + h], in1=hT_hi[:, h, chunk(c % 3)].bitcast(F32),
                                       op0=ALU.mult, op1=ALU.subtract).then_inc(hT_lo_ok, 1)

        @block.vector
        def _(v):
            k = Chain(v, vchain)
            v.memset(sg[:], 0.0).then_inc(zeroed, 1)
            v.wait_ge(ld_xT, 64)
            for h in range(DH):
                v.tensor_scalar(uv[:, h], uv[:, h], cols[:, h:h + 1], None, ALU.mult).then_inc(uv_ok, 1)
            v.wait_ge(squares, NT)
            k.step(v.tensor_scalar(ss[:], ss[:], 1.0 / D, EPS_RMS, ALU.mult, ALU.add))
            rsqrt_steps(v, k, rs[:], ss[:], tmp[:, 0:NT])
            v.wait_ge(ld_w, 16 * 9)
            for t in range(NT):
                v.scalar_tensor_tensor(out=hn[:, t], in0=x[:, t], scalar=rs[:, t:t + 1], in1=rows[:, 0],
                                       op0=ALU.mult, op1=ALU.mult).then_inc(hn_ok, 1)
            v.wait_ge(gammas, 1)
            k.step(v.tensor_scalar(sg[:], sg[:], 1.0, None, ALU.add))
            k.step(v.reciprocal(sg[:], sg[:]))
            k.step(v.tensor_scalar(lg[:, 0:R], sg[:, 0:R], 0.15, 1.0, ALU.max, ALU.min))
            v.tensor_scalar(lg[:, R:], sg[:, 2 * R:2 * R + 1], 0.15, 1.0, ALU.max, ALU.min).then_inc(expos, 1)
            v.wait_ge(consts, 1)
            k.step(v.tensor_copy(expf[:], expo[:]))
            k.step(v.tensor_scalar(expf[:], expf[:], 1.0 - SUB, None, ALU.max))
            v.wait_ge(gammas, 2)
            k.step(v.tensor_tensor(kw[:], bc(expf[:, 0], 2, R), bc(lg[:, 0:R], 1, NSUB + 1), ALU.mult))
            v.tensor_tensor(qw[:], bc(expf[:, 1], 2, R), bc(lg[:, 0:R], 1, NSUB + 1), ALU.mult).then_inc(coef_ok, 1)
            k.step(v.tensor_scalar(gk[:], traw[:], sg[:, 2 * R + 1:], None, ALU.mult))
            k.step(v.tensor_scalar(band[:], taps[:, 0], gk[:, 0:1], None, ALU.mult))
            for t in range(1, KTAP):
                k.step(v.scalar_tensor_tensor(out=band[:], in0=taps[:, t], scalar=gk[:, t:t + 1], in1=band[:],
                                              op0=ALU.mult, op1=ALU.add))
            k.step(v.tensor_copy(qcat[:, :, 5, 0:KTAP - 1], bc(band[:, P:], 1, NT)))
            v.wait_ge(gammas, 5)
            k.step(v.tensor_tensor(coef[:], coef[:], lg[:, R:], ALU.mult))
            v.wait_ge(masked, 1)
            k.step(v.tensor_tensor(qw[:], qw[:], bc(sg[:, R:2 * R], 1, NSUB + 1), ALU.mult))
            v.wait_ge(qk_mm, 1)
            k.step(v.tensor_tensor(qk[:].rearrange("p t a r -> p t (a r)"),
                                   bank[7][:].rearrange("p (t n) -> p t n", t=NT), bc(rs[:], 2, 2 * R), ALU.mult))
            k.step(v.tensor_tensor(qk_sq, qk[:], qk[:], ALU.mult))
            k.step(v.tensor_reduce(qkn[:], qk_sq.rearrange("p t a r -> p (t a) r"), AX_X, ALU.add))
            k.step(v.tensor_scalar(qkn[:], qkn[:], 1e-16, None, ALU.max))
            rsqrt_steps(v, k, qkr[:], qkn[:], tmp[:])
            k.step(v.tensor_tensor(qk[:].rearrange("p t a r -> p (t a) r"), qk[:].rearrange("p t a r -> p (t a) r"),
                                   bc(qkr[:], 2, R), ALU.mult))
            k.step(v.tensor_tensor(kcat[:, :, 0:NSUB + 1, :], bc(qk[:, :, 1], 2, NSUB + 1), bc(kw[:], 1, NT), ALU.mult))
            v.tensor_tensor(qcat[:, :, 0:NSUB + 1, :], bc(qk[:, :, 0], 2, NSUB + 1), bc(qw[:], 1, NT),
                            ALU.mult).then_inc(cats, 1)
            for t in range(NT + 1):
                if t < NT:
                    v.wait_ge(S_mm, t + 1)
                    if t >= 3:
                        v.wait_ge(o_mm, t - 2)
                    if t >= 1:
                        v.wait_ge(S_sb, t)
                    v.scalar_tensor_tensor(out=S[64:64 + R + KTAP - 1, (t + 1) % 4], in0=S[64:64 + R + KTAP - 1, t % 4],
                                           scalar=coef[64:64 + R + KTAP - 1, 0:1],
                                           in1=bank[6 + t % 2][64:64 + R + KTAP - 1, 0:D],
                                           op0=ALU.mult, op1=ALU.add).then_inc(S_sb, 1)
                if t >= 1:
                    v.wait_ge(A_mm, t)
                    if t >= 3:
                        v.wait_ge(o_mm, t - 2)
                    k.step(v.tensor_tensor(AT[:, (t - 1) % 2], bank[2 + (t - 1) % 2][:, 0:P], later[:], ALU.mult))
                    v.tensor_tensor(AT[:, (t - 1) % 2], AT[:, (t - 1) % 2], band[:, 0:P], ALU.add).then_inc(A_sb, 1)
            v.wait_ge(hi_w, 2)
            v.tensor_tensor(w1_lo[:].rearrange("p c f -> p (c f)"), w1_32[:],
                            w1_hi[:].bitcast(F32).rearrange("p c f -> p (c f)"), ALU.subtract).then_inc(w_lo_ok, 1)
            v.tensor_tensor(w2_lo[:].rearrange("p c f -> p (c f)"), w2_32,
                            w2_hi[:].bitcast(F32).rearrange("p c f -> p (c f)"), ALU.subtract).then_inc(w_lo_ok, 1)
            for c in range(NC):
                for t in range(c * TPC, (c + 1) * TPC):
                    v.wait_ge(h2_mm, t + 1)
                    v.wait_ge(xb_ok, t + 1)
                    v.tensor_tensor(h2[:, t], bank[t % 2][:, 0:D], h2[:, t], ALU.add).then_inc(h2_sb, 1)
            for c in range(NC):
                sl = slice(c * TPC, (c + 1) * TPC)
                v.wait_ge(squares, NT + (c + 1) * TPC)
                k.step(v.tensor_scalar(ss[:, sl], ss[:, sl], 1.0 / D, EPS_RMS, ALU.mult, ALU.add))
                rsqrt_steps(v, k, rs[:, sl], ss[:, sl], tmp[:, 0:TPC])
                if c >= 2:
                    v.wait_ge(hT_mm, DH * (c - 1))
                for j in range(TPC):
                    t = c * TPC + j
                    v.tensor_scalar(n2[:, c % 2, j], h2[:, t], rs[:, t:t + 1], None, ALU.mult).then_inc(n2_ok, 1)
                if 1 <= c <= 2:
                    low_part(v, c - 1)
            for c in range(NC):
                for f in range(FT):
                    n = c * FT + f
                    v.wait_ge(gelu_ok, n + 1)
                    if c >= 1:
                        v.wait_ge(y_mm, TPC * c)
                    k.step(v.tensor_copy(g_hi[:, f], g32[:, f % 2]))
                    v.tensor_tensor(g_lo[:, f], g32[:, f % 2], g_hi[:, f].bitcast(F32), ALU.subtract).then_inc(g_ok, 1)
                    if f == 4 and c + 2 < NC:
                        low_part(v, c + 2)
                for t in range(c * TPC, (c + 1) * TPC):
                    v.wait_ge(y_mm, t + 1)
                    v.wait_ge(res_ok, t + 1)
                    v.tensor_tensor(hn[:, t], bank[t % 2][:, 0:D], hn[:, t], ALU.add).then_inc(z_ok, 1)
                    v.wait_ge(z_ok, t + 1)
                    k.step(v.bn_stats(stats[:, t], hn[:, t]))
                    k.step(v.bn_aggr(mv[:, t], stats[:, t]))
                sl = slice(c * TPC, (c + 1) * TPC)
                k.step(v.tensor_scalar(ss[:, sl], mv[:, sl, 1], EPS_LN, None, ALU.add))
                rsqrt_steps(v, k, rs[:, sl], ss[:, sl], tmp[:, 0:TPC])
                for t in range(c * TPC, (c + 1) * TPC):
                    last = v.tensor_scalar(h2[:, t], hn[:, t], mv[:, t, 0:1], rs[:, t:t + 1], ALU.subtract, ALU.mult)
                last.then_inc(x1_ok, 1)

        @block.tensor
        def _(pe):
            pe.wait_ge(ld_xT, 64)
            pe.wait_ge(uv_ok, 2)
            for t in range(NT):
                for h in range(DH):
                    last = pe.matmul(bank[7][:, t * 2 * R:(t + 1) * 2 * R], xT[:, h, tile(t)], uv[:, h],
                                     start=(h == 0), stop=(h == DH - 1))
            last.then_inc(qk_mm, 1)
            pe.wait_ge(consts, 1)
            pe.wait_ge(cats, 1)
            for t in range(NT + 2):
                if t < NT:
                    if t >= 2:
                        pe.wait_ge(turned_sb, t - 1)
                    pe.transpose(bank[t % 2][0:96, 0:P], qcat[:, t].rearrange("p s r -> p (s r)"), ident[:])
                    pe.transpose(bank[t % 2][0:96, P:2 * P], kcat[:, t].rearrange("p s r -> p (s r)"),
                                 ident[:]).then_inc(turned, 1)
                    pe.wait_ge(hn_ok, t + 1)
                    if t >= 2:
                        pe.wait_ge(S_sb, t - 1)
                    pe.matmul(bank[6 + t % 2][64:64 + R + KTAP - 1, 0:D],
                              kcat[:, t].rearrange("p s r -> p (s r)")[:, 64:64 + R + KTAP - 1], hn[:, t],
                              start=True, stop=True).then_inc(S_mm, 1)
                if 1 <= t <= NT:
                    pe.wait_ge(turned_sb, t)
                    if t >= 3:
                        pe.wait_ge(A_sb, t - 2)
                    u = (t - 1) % 3
                    pe.matmul(bank[2 + (t - 1) % 2][:, 0:P], qkT[0:64, u, P:2 * P], qkT[0:64, u, 0:P],
                              start=True, stop=True).then_inc(A_mm, 1)
                if t >= 2:
                    u = t - 2
                    pe.wait_ge(A_sb, u + 1)
                    if u >= 1:
                        pe.wait_ge(S_sb, u)
                    if u >= 2:
                        pe.wait_ge(o_sb, u - 1)
                    for h in range(DH):
                        out = bank[4 + u % 2][:, h * P:(h + 1) * P]
                        pe.matmul(out, hn[:, u, h * P:(h + 1) * P], AT[:, u % 2], start=True, stop=False)
                        last = pe.matmul(out, S[64:64 + R + KTAP - 1, u % 4, h * P:(h + 1) * P],
                                         qkT[64:64 + R + KTAP - 1, u % 3, 0:P], start=False, stop=True)
                    last.then_inc(o_mm, 1)
            for t in range(NT):
                pe.wait_ge(o_sb, t + 1)
                if t >= 2:
                    pe.wait_ge(h2_sb, t - 1)
                for h in range(DH):
                    last = pe.matmul(bank[t % 2][:, 0:D], oT[:, h, tile(t)], projT[:, h], start=(h == 0), stop=(h == DH - 1))
                last.then_inc(h2_mm, 1)

            def turn_n2(c):
                if c >= 2:
                    pe.wait_ge(hT_lo_ok, DH * (c - 1))
                pe.wait_ge(n2_ok, (c + 1) * TPC)
                for h in range(DH):
                    for j in range(TPC):
                        last = pe.transpose(bank[2 + (c % 2) * 2 + h][:, j * P:(j + 1) * P],
                                            n2[:, c % 2, j, h * P:(h + 1) * P], ident[:])
                    last.then_inc(hT_mm, 1)

            def turn_x1(c):
                if c >= 2:
                    pe.wait_ge(x1_sb, DH * (c - 1))
                pe.wait_ge(x1_ok, c + 1)
                for h in range(DH):
                    for j in range(TPC):
                        last = pe.transpose(bank[2 + (c % 2) * 2 + h][:, j * P:(j + 1) * P],
                                            h2[:, c * TPC + j, h * P:(h + 1) * P], ident[:])
                    last.then_inc(x1_mm, 1)

            turn_n2(0)
            turn_n2(1)
            pe.wait_ge(w_lo_ok, 2)
            for c in range(NC):
                pe.wait_ge(hT_lo_ok, DH * (c + 1))
                for f in range(FT):
                    n = c * FT + f
                    if n >= 2:
                        pe.wait_ge(gelu_ok, n - 1)
                    fs = slice(f * P, (f + 1) * P)
                    for h in range(DH):
                        last = three_pass(pe, bank[6 + f % 2][:], w1_hi[:, h, fs], w1_lo[:, h, fs],
                                          hT_hi[:, h, chunk(c % 3)], hT_lo[:, h, chunk(c % 3)], h == 0, h == DH - 1)
                    last.then_inc(up_mm, 1)
                    if f == 1 and c + 2 < NC:
                        turn_n2(c + 2)
                for j in range(TPC):
                    t = c * TPC + j
                    if t >= 2:
                        pe.wait_ge(z_ok, t - 1)
                    for f in range(FT):
                        pe.wait_ge(g_ok, c * FT + f + 1)
                        last = three_pass(pe, bank[t % 2][:, 0:D], g_hi[:, f, j * P:(j + 1) * P], g_lo[:, f, j * P:(j + 1) * P],
                                          w2_hi[:, f], w2_lo[:, f], f == 0, f == FT - 1)
                    last.then_inc(y_mm, 1)
            for c in range(NC):
                turn_x1(c)


def cross_attention(nc, io, shared):
    ident, ones, sT = shared["ident"], shared["ones"], shared["sT"]
    HALF = T // 2
    G = 3 * D
    FIRST_STEPS = (NC - 1) * (1 + RSQRT_STEPS)
    V_STEPS, v_steps = NC * (1 + RSQRT_STEPS) + MT * (NC + 2) + 2 + NC * DH * 2, []
    with ExitStack() as ctx:
        def sb(name, shape, dt=F32, stack=ctx):
            return stack.enter_context(nc.sbuf_tensor(name, shape, dt))

        def sem(name, stack=ctx):
            return stack.enter_context(nc.semaphore("x_" + name))

        psum = ctx.enter_context(nc.psum_tensor("x_psum", [P, 8, CH], F32))
        bank = [psum[:, i] for i in range(8)]

        kq_hi = sb("x_kq_hi", [P, DH, M], F32R)
        kq_lo = sb("x_kq_lo", [P, DH, M], F32R)
        v_hi = sb("x_v_hi", [P, MT, D], F32R)
        v_lo = sb("x_v_lo", [P, MT, D], F32R)
        wi_hi = sb("x_wi_hi", [P, DH, G], F32R)
        wi_lo = sb("x_wi_lo", [P, DH, G], F32R)
        wh_hi = sb("x_wh_hi", [P, DH, G], F32R)
        wh_lo = sb("x_wh_lo", [P, DH, G], F32R)
        rs16 = sb("x_rs16", [P, MT])
        bias = sb("x_bias", [P, 4 * DH])

        def hs(h):
            return slice(h * P, (h + 1) * P)

        def chunk(c):
            return slice(c * CH, (c + 1) * CH)

        with ExitStack() as pre:
            prepare_context(nc, io, pre, bank, dict(kq_hi=kq_hi, kq_lo=kq_lo, v_hi=v_hi, v_lo=v_lo, wi_hi=wi_hi,
                                                    wi_lo=wi_lo, wh_hi=wh_hi, wh_lo=wh_lo, rs16=rs16, bias=bias))

        sn_hi = sb("x_sn_hi", [P, DH, T], F32R)
        sn_lo = sb("x_sn_lo", [P, DH, T], F32R)
        E = sb("x_E", [P, MT, HALF])
        e = sb("x_e", [P, 2, HALF])
        p_hi = sb("x_p_hi", [P, 2, HALF], F32R)
        p_lo = sb("x_p_lo", [P, 2, HALF], F32R)
        acc = sb("x_acc", [P, T])
        diag = sb("x_diag", [P, 2, CH])
        st = sb("x_st", [P, 3, NT])
        rw = sb("x_rw", [P, NT])
        mx = sb("x_mx", [P, 2, NC + 2])
        inv = sb("x_inv", [P, MT, 3])
        room = E[:].rearrange("p m (a n) -> p (m a) n", n=CH)
        gates = [room[:, 4 + 4 * i:8 + 4 * i] for i in range(2)]
        sq = [room[:, 12 + DH * i:12 + DH * (i + 1)] for i in range(2)]
        u32 = [room[:, 16 + DH * i:16 + DH * (i + 1)] for i in range(2)]
        U = [e[:, c].rearrange("p (h n) -> p h n", h=DH) for c in range(2)] + [room[:, DH * c:DH * (c + 1)] for c in range(2)]
        u_hi = [p_hi[:, i].rearrange("p (h n) -> p h n", h=DH) for i in range(2)]
        u_lo = [p_lo[:, i].rearrange("p (h n) -> p h n", h=DH) for i in range(2)]

        (sq_ok, sum_ok, stat_mm, diag_ok, bc_mm, prod_ok, sn_hi_ok, sn_lo_ok) = (
            sem(n) for n in ("sq_ok", "sum_ok", "stat_mm", "diag_ok", "bc_mm", "prod_ok", "sn_hi_ok", "sn_lo_ok"))
        (score_mm, neg_ok, exp_ok, inv_ok, p_hi_ok, p_lo_ok, acc_ok, upd_mm) = (
            sem(n) for n in ("score_mm", "neg_ok", "exp_ok", "inv_ok", "p_hi_ok", "p_lo_ok", "acc_ok", "upd_mm"))
        (U_ok, s_hi_ok, s_lo_ok, row_mm, rdiag_ok, rbc_mm, u_ok, u_hi_ok, u_lo_ok) = (
            sem(n) for n in ("U_ok", "s_hi_ok", "s_lo_ok", "row_mm", "rdiag_ok", "rbc_mm", "u_ok", "u_hi_ok", "u_lo_ok"))
        (r_mm, z_mm, hn_mm, in_mm, r_ok, z_ok, hr_ok, arg_ok, n_ok, s_ok, vchain) = (
            sem(n) for n in ("r_mm", "z_mm", "hn_mm", "in_mm", "r_ok", "z_ok", "hr_ok", "arg_ok", "n_ok", "s_ok", "vchain"))

        GH = NC * DH
        Q = 2 * MT
        block = ctx.enter_context(nc.Block())

        @block.scalar
        def _(act):
            def squares(g, c, first=False):
                if not (first and c < 2):
                    act.wait_ge(stat_mm, g - 1)
                act.activation(sq[c % 2], sT[:, :, chunk(c)], ACT.Square).then_inc(sq_ok, 1)

            def normed_hi(g, c):
                act.wait_ge(prod_ok, g + 1)
                act.activation(sn_hi[:, :, chunk(c)], u32[c % 2], ACT.Copy).then_inc(sn_hi_ok, 1)

            squares(0, 0, first=True)
            squares(1, 1, first=True)
            for c in range(NC - 1):
                normed_hi(c, c)
                if c + 2 < NC - 1:
                    squares(c + 2, c + 2)
            with act.Fori(0, ITERS) as it:
                def weights_hi(q):
                    m = q % MT
                    n = MROWS[m]
                    src = e[0:n, m % 2] if q < MT else E[0:n, m]
                    if q >= 2:
                        act.wait_ge(upd_mm, it * Q + q - 1)
                    act.activation(p_hi[0:n, q % 2], src, ACT.Copy, scale=inv[0:n, m, 2:3]).then_inc(p_hi_ok, 1)

                def slots_hi(c):
                    act.activation(sn_hi[:, :, chunk(c)], sT[:, :, chunk(c)], ACT.Copy).then_inc(s_hi_ok, 1)

                def take_updates(c):
                    b = 4 + DH * c if c < 2 else DH * (c - 2)
                    act.activation(U[c], psum[:, b:b + DH], ACT.Copy).then_inc(U_ok, 1)

                def updates_hi(c):
                    act.wait_ge(u_ok, it * NC + c + 1)
                    if c >= 2:
                        act.wait_ge(in_mm, it * GH + DH * (c - 1))
                    act.activation(u_hi[c % 2], U[c], ACT.Copy).then_inc(u_hi_ok, 1)

                act.wait_ge(s_ok, it * GH + 1)
                squares(it * NC + NC - 1, NC - 1)
                normed_hi(it * NC + NC - 1, NC - 1)
                for m in range(MT):
                    n = MROWS[m]
                    act.wait_ge(neg_ok, it * MT + m + 1)
                    if m == 0:
                        act.wait_ge(sn_lo_ok, it * NC + NC)
                    for half in range(2):
                        if half == 0 and m >= 2:
                            act.wait_ge(acc_ok, it * MT * NC + (m - 2) * NC + 2)
                            act.wait_ge(p_lo_ok, it * Q + m - 1)
                        out = e[0:n, m % 2] if half == 0 else E[0:n, m]
                        act.activation(out, psum[0:n, 2 * half:2 * half + 2].rearrange("p a n -> p (a n)"), ACT.Exp,
                                       bias=inv[0:n, m, 0:1], scale=rs16[0:n, m:m + 1],
                                       accum_out=mx[0:n, m % 2, NC + half:NC + half + 1]).then_inc(exp_ok, 1)
                    act.wait_ge(inv_ok, it * MT + m + 1)
                    weights_hi(m)
                for m in range(MT):
                    weights_hi(MT + m)
                    if m == 0:
                        act.wait_ge(upd_mm, it * Q + MT)
                        act.wait_ge(acc_ok, (it + 1) * MT * NC)
                        act.wait_ge(p_lo_ok, it * Q + MT)
                    if m < 2:
                        take_updates(m)
                    elif m < 2 + NC:
                        slots_hi(m - 2)
                act.wait_ge(upd_mm, (it + 1) * Q)
                act.wait_ge(p_lo_ok, (it + 1) * Q)
                take_updates(2)
                take_updates(3)
                updates_hi(0)
                for c in range(NC):
                    after = (it + 1) * NC + c - 1
                    if c + 1 < NC:
                        updates_hi(c + 1)
                    if c >= 1:
                        act.wait_ge(s_ok, it * GH + DH * c + 1)
                        squares(after, c - 1)
                    for h in range(DH):
                        i = c * DH + h
                        r, z, arg, new = (gates[i % 2][:, j] for j in range(4))
                        act.wait_ge(r_mm, it * GH + i + 1)
                        if i >= 2:
                            act.wait_ge(s_ok, it * GH + i)
                        act.activation(r, bank[1], ACT.Sigmoid, bias=bias[:, h:h + 1]).then_inc(r_ok, 1)
                        if c >= 1 and h == 1:
                            normed_hi(after, c - 1)
                        act.wait_ge(z_mm, it * GH + i + 1)
                        act.activation(z, bank[2], ACT.Sigmoid, bias=bias[:, DH + h:DH + h + 1]).then_inc(z_ok, 1)
                        act.wait_ge(arg_ok, it * GH + i + 1)
                        act.activation(new, arg, ACT.Tanh, bias=bias[:, 2 * DH + h:2 * DH + h + 1]).then_inc(n_ok, 1)

        @block.vector
        def _(v):
            v.memset(st[:], 0.0).then_inc(s_ok, 1)
            v.wait_ge(s_ok, 1)

            def factors(values, slot, counted, tiles):
                for j, t in enumerate(tiles):
                    last = v.tensor_scalar(diag[:, slot, j * P:(j + 1) * P], ident[:], values[:, t:t + 1], None, ALU.mult)
                last.then_inc(counted, 1)

            def rms(k, g, c, first=False):
                tiles = slice(c * TPC, (c + 1) * TPC)
                v.wait_ge(stat_mm, g + 1)
                k.step(v.tensor_scalar(st[:, 0, tiles], bank[4 + c % 2][:, 0:TPC], 1.0 / D, EPS_RMS, ALU.mult, ALU.add))
                rsqrt_steps(v, k, st[:, 1, tiles], st[:, 0, tiles], st[:, 2, tiles])
                if not (first and c < 2):
                    v.wait_ge(bc_mm, g - 1)
                factors(st[:, 1], c % 2, diag_ok, range(c * TPC, (c + 1) * TPC))

            def normed(g, c, first=False):
                v.wait_ge(bc_mm, g + 1)
                if not (first and c < 2):
                    v.wait_ge(sn_hi_ok, g - 1)
                    v.wait_ge(sn_lo_ok, g - 1)
                v.tensor_tensor(u32[c % 2], sT[:, :, chunk(c)], bc(bank[6 + c % 2], 1, DH), ALU.mult).then_inc(prod_ok, 1)

            def normed_lo(g, c):
                v.wait_ge(sn_hi_ok, g + 1)
                v.tensor_tensor(sn_lo[:, :, chunk(c)], u32[c % 2], sn_hi[:, :, chunk(c)].bitcast(F32),
                                ALU.subtract).then_inc(sn_lo_ok, 1)

            k = Chain(v, vchain)
            for c in range(NC):
                if c < NC - 1:
                    rms(k, c, c, first=True)
                if c >= 1:
                    normed(c - 1, c - 1, first=True)
                    normed_lo(c - 1, c - 1)
            assert k.n == FIRST_STEPS

            with v.Fori(0, ITERS) as it:
                k = Chain(v, vchain, it * V_STEPS + FIRST_STEPS)

                def add_weights(m, c):
                    n = MROWS[m]
                    src = e[0:n, m % 2, chunk(c)] if c < 2 else E[0:n, m, chunk(c - 2)]
                    if m == 0:
                        v.tensor_scalar(acc[0:n, chunk(c)], src, inv[0:n, m, 2:3], None, ALU.mult).then_inc(acc_ok, 1)
                    else:
                        v.wait_ge(acc_ok, it * MT * NC + (m - 1) * NC + c + 1)
                        v.scalar_tensor_tensor(out=acc[0:n, chunk(c)], in0=src, scalar=inv[0:n, m, 2:3],
                                               in1=acc[0:n, chunk(c)], op0=ALU.mult, op1=ALU.add).then_inc(acc_ok, 1)

                def weights_lo(q):
                    m = q % MT
                    n = MROWS[m]
                    src = e[0:n, m % 2] if q < MT else E[0:n, m]
                    v.wait_ge(p_hi_ok, it * Q + q + 1)
                    if q >= 2:
                        v.wait_ge(upd_mm, it * Q + q - 1)
                    v.scalar_tensor_tensor(out=p_lo[0:n, q % 2], in0=src, scalar=inv[0:n, m, 2:3],
                                           in1=p_hi[0:n, q % 2].bitcast(F32), op0=ALU.mult,
                                           op1=ALU.subtract).then_inc(p_lo_ok, 1)

                rms(k, it * NC + NC - 1, NC - 1)
                for m in range(MT):
                    n = MROWS[m]
                    for c in range(NC):
                        if m == 0 and c == 1:
                            normed(it * NC + NC - 1, NC - 1)
                        if m == 0 and c == 2:
                            normed_lo(it * NC + NC - 1, NC - 1)
                        v.wait_ge(score_mm, it * MT * NC + m * NC + c + 1)
                        mark = k.mark(v.tensor_reduce(mx[0:n, m % 2, c:c + 1], bank[c][0:n], AX_X, ALU.max))
                    v.wait_ge(vchain, mark)
                    k.step(v.tensor_reduce(inv[0:n, m, 0:1], mx[0:n, m % 2, 0:NC], AX_X, ALU.max))
                    v.tensor_scalar(inv[0:n, m, 0:1], inv[0:n, m, 0:1], rs16[0:n, m:m + 1], -1.0,
                                    ALU.mult, ALU.mult).then_inc(neg_ok, 1)
                    if m >= 1:
                        for c in range(NC - 1):
                            add_weights(m - 1, c)
                    v.wait_ge(exp_ok, it * Q + 2 * m + 2)
                    k.step(v.tensor_tensor(inv[0:n, m, 1:2], mx[0:n, m % 2, NC:NC + 1], mx[0:n, m % 2, NC + 1:NC + 2], ALU.add))
                    v.reciprocal(inv[0:n, m, 2:3], inv[0:n, m, 1:2]).then_inc(inv_ok, 1)
                    if m >= 1:
                        add_weights(m - 1, NC - 1)
                    weights_lo(m)
                for c in range(NC):
                    add_weights(MT - 1, c)

                def norm_updates(c):
                    v.wait_ge(U_ok, it * NC + c + 1)
                    v.wait_ge(rbc_mm, it * NC + c + 1)
                    v.tensor_tensor(U[c], U[c], bc(bank[4 + c], 1, DH), ALU.mult).then_inc(u_ok, 1)

                def slots_lo(c):
                    v.wait_ge(s_hi_ok, it * NC + c + 1)
                    v.tensor_tensor(sn_lo[:, :, chunk(c)], sT[:, :, chunk(c)], sn_hi[:, :, chunk(c)].bitcast(F32),
                                    ALU.subtract).then_inc(s_lo_ok, 1)

                for m in range(MT):
                    weights_lo(MT + m)
                    if 2 <= m < 2 + NC:
                        slots_lo(m - 2)
                    if m == 6:
                        v.wait_ge(row_mm, it + 1)
                        k.step(v.tensor_scalar(rw[:], bank[4][:, 0:NT], EPS_RMS, None, ALU.add))
                        k.step(v.reciprocal(rw[:], rw[:]))
                        factors(rw, 0, rdiag_ok, range(0, TPC))
                    if m in (7, 10, 11):
                        c = {7: 1, 10: 2, 11: 3}[m]
                        if c >= 2:
                            v.wait_ge(rbc_mm, it * NC + c - 1)
                        factors(rw, c % 2, rdiag_ok, range(c * TPC, (c + 1) * TPC))
                    if m in (11, 12):
                        norm_updates(m - 11)

                def updates_lo(c):
                    v.wait_ge(u_hi_ok, it * NC + c + 1)
                    v.tensor_tensor(u_lo[c % 2], U[c], u_hi[c % 2].bitcast(F32), ALU.subtract).then_inc(u_lo_ok, 1)

                updates_lo(0)
                norm_updates(2)
                norm_updates(3)
                for c in range(NC):
                    after = (it + 1) * NC + c - 1
                    if c + 1 < NC:
                        updates_lo(c + 1)
                    for h in range(DH):
                        i = c * DH + h
                        r, z, arg, new = (gates[i % 2][:, j] for j in range(4))
                        s = sT[:, h, chunk(c)]
                        v.wait_ge(hn_mm, it * GH + i + 1)
                        v.wait_ge(r_ok, it * GH + i + 1)
                        v.scalar_tensor_tensor(out=arg, in0=bank[0], scalar=bias[:, 3 * DH + h:3 * DH + h + 1], in1=r,
                                               op0=ALU.add, op1=ALU.mult).then_inc(hr_ok, 1)
                        if c >= 1 and h == 1:
                            normed_lo(after, c - 1)
                        if c >= 1 and h == 0:
                            rms(k, after, c - 1)
                        v.wait_ge(hr_ok, it * GH + i + 1)
                        v.wait_ge(in_mm, it * GH + i + 1)
                        v.tensor_tensor(arg, arg, bank[3], ALU.add).then_inc(arg_ok, 1)
                        v.wait_ge(n_ok, it * GH + i + 1)
                        k.step(v.tensor_tensor(s, s, new, ALU.subtract))
                        k.step(v.tensor_tensor(s, s, z, ALU.mult))
                        v.tensor_tensor(s, s, new, ALU.add).then_inc(s_ok, 1)
                        if c >= 1 and h == 0:
                            normed(after, c - 1)
                v_steps.append(k.n)

        @block.gpsimd
        def _(pool):
            def add_squares(g, c):
                pool.wait_ge(sq_ok, g + 1)
                pool.tensor_tensor(sq[c % 2][:, 0], sq[c % 2][:, 0], sq[c % 2][:, 1], ALU.add).then_inc(sum_ok, 1)

            for c in range(NC - 1):
                add_squares(c, c)
            with pool.Fori(0, ITERS) as it:
                add_squares(it * NC + NC - 1, NC - 1)
                for c in range(NC - 1):
                    add_squares((it + 1) * NC + c, c)

        @block.tensor
        def _(pe):
            def square_sums(g, c, first=False):
                pe.wait_ge(sum_ok, g + 1)
                if not (first and c < 2):
                    pe.wait_ge(diag_ok, g - 1)
                for j in range(TPC):
                    last = pe.matmul(bank[4 + c % 2][:, j:j + 1], sq[c % 2][:, 0, j * P:(j + 1) * P], ones[:, 0:1],
                                     start=True, stop=True)
                last.then_inc(stat_mm, 1)

            def broadcast(g, c, first=False):
                pe.wait_ge(diag_ok, g + 1)
                if not (first and c < 2):
                    pe.wait_ge(prod_ok, g - 1)
                pe.matmul(bank[6 + c % 2], ones[:], diag[:, c % 2], start=True, stop=True).then_inc(bc_mm, 1)

            for c in range(NC):
                if c < NC - 1:
                    square_sums(c, c, first=True)
                if c >= 1:
                    broadcast(c - 1, c - 1, first=True)
            with pe.Fori(0, ITERS) as it:
                def update(q):
                    m = q % MT
                    n = MROWS[m]
                    pe.wait_ge(p_lo_ok, it * Q + q + 1)
                    for c in range(2):
                        for h in range(DH):
                            b = (4 if q < MT else 0) + DH * c + h
                            last = three_pass(pe, bank[b], v_hi[0:n, m, hs(h)], v_lo[0:n, m, hs(h)],
                                              p_hi[0:n, q % 2, chunk(c)], p_lo[0:n, q % 2, chunk(c)], m == 0, m == MT - 1)
                    last.then_inc(upd_mm, 1)

                for m in range(MT):
                    n = MROWS[m]
                    ks = slice(m * P, m * P + n)
                    for c in range(NC):
                        if m == 0:
                            if c == 1:
                                square_sums(it * NC + NC - 1, NC - 1)
                            if c == 2:
                                broadcast(it * NC + NC - 1, NC - 1)
                            pe.wait_ge(sn_lo_ok, it * NC + c + 1)
                        elif c % 2 == 0:
                            pe.wait_ge(exp_ok, it * Q + 2 * (m - 1) + c // 2 + 1)
                        for h in range(DH):
                            last = three_pass(pe, bank[c][0:n], kq_hi[:, h, ks], kq_lo[:, h, ks],
                                              sn_hi[:, h, chunk(c)], sn_lo[:, h, chunk(c)], h == 0, h == DH - 1)
                        last.then_inc(score_mm, 1)
                    if m >= 1:
                        update(m - 1)
                update(MT - 1)

                def row_broadcast(c):
                    pe.wait_ge(rdiag_ok, it * NC + c + 1)
                    pe.matmul(bank[4 + c], ones[:], diag[:, c % 2], start=True, stop=True).then_inc(rbc_mm, 1)

                for m in range(MT):
                    if m == 0:
                        pe.wait_ge(exp_ok, (it + 1) * Q)
                    update(MT + m)
                    if m == 4:
                        pe.wait_ge(acc_ok, (it + 1) * MT * NC)
                        pe.wait_ge(U_ok, it * NC + 2)
                        for t in range(NT):
                            last = pe.matmul(bank[4][:, t:t + 1], acc[:, t * P:(t + 1) * P], ones[:, 0:1], start=True, stop=True)
                        last.then_inc(row_mm, 1)
                    if m in (8, 9, 11, 12):
                        row_broadcast((8, 9, 11, 12).index(m))

                def gate(b, e_from, h, c, parts, counted):
                    cols = slice(e_from * D + h * P, e_from * D + (h + 1) * P)
                    slots = [(wh_hi, wh_lo, sn_hi[:, k, chunk(c)], sn_lo[:, k, chunk(c)], k) for k in range(DH)]
                    updates = [(wi_hi, wi_lo, u_hi[c % 2][:, k], u_lo[c % 2][:, k], k) for k in range(DH)]
                    steps = slots * ("s" in parts) + updates * ("u" in parts)
                    for i, (w_hi, w_lo, x_hi, x_lo, k) in enumerate(steps):
                        if x_hi is updates[0][2]:
                            pe.wait_ge(u_lo_ok, it * NC + c + 1)
                        last = three_pass(pe, bank[b], w_hi[:, k, cols], w_lo[:, k, cols], x_hi, x_lo,
                                          i == 0, i == len(steps) - 1)
                    last.then_inc(counted, 1)

                for c in range(NC):
                    after = (it + 1) * NC + c - 1
                    pe.wait_ge(s_lo_ok, it * NC + c + 1)
                    for h in range(DH):
                        i = c * DH + h
                        if i == 0:
                            pe.wait_ge(U_ok, (it + 1) * NC)
                        else:
                            pe.wait_ge(hr_ok, it * GH + i)
                        gate(0, 2, h, c, "s", hn_mm)
                        if i > 0:
                            pe.wait_ge(r_ok, it * GH + i)
                        gate(1, 0, h, c, "su", r_mm)
                        if c >= 1 and h == 1:
                            broadcast(after, c - 1)
                        if i > 0:
                            pe.wait_ge(z_ok, it * GH + i)
                        gate(2, 1, h, c, "su", z_mm)
                        if c >= 1 and h == 0:
                            square_sums(after, c - 1)
                        if i > 0:
                            pe.wait_ge(arg_ok, it * GH + i)
                        gate(3, 2, h, c, "u", in_mm)
                pe.wait_ge(z_ok, (it + 1) * GH)
                pe.wait_ge(arg_ok, (it + 1) * GH)

    assert v_steps == [V_STEPS], v_steps


def prepare_context(nc, io, ctx, bank, dest):
    kq_hi, kq_lo, v_hi, v_lo = (dest[n] for n in ("kq_hi", "kq_lo", "v_hi", "v_lo"))
    wi_hi, wi_lo, wh_hi, wh_lo, rs16, bias = (dest[n] for n in ("wi_hi", "wi_lo", "wh_hi", "wh_lo", "rs16", "bias"))
    G = 3 * D

    def sb(name, shape, dt=F32):
        return ctx.enter_context(nc.sbuf_tensor("y_" + name, shape, dt))

    def sem(name):
        return ctx.enter_context(nc.semaphore("y_" + name))

    cx = sb("cx", [P, MT, D])
    cxT = sb("cxT", [P, DH, M])
    v32 = sb("v32", [P, MT, D])
    wq, wk, wv = (sb(n, [P, DH, D]) for n in ("wq", "wk", "wv"))
    wiT = sb("wiT", [P, DH, G])
    whT = sb("whT", [P, DH, G])
    wkq = sb("wkq", [P, DH, D])
    cols = sb("cols", [P, 2 * DH])
    bi = sb("bi", [P, 2 * 3 * DH])
    junk = sb("junk", [P, 2, D])
    ss, rs, tmp = sb("ss", [P, MT]), sb("rs", [P, MT]), sb("tmp", [P, MT])
    ld_w, ld_c, ld_cT, ld_g, zeroed = sem("ld_w"), sem("ld_c"), sem("ld_cT"), sem("ld_g"), sem("zeroed")
    squares, vchain, v32_ok, v_hi_ok = sem("squares"), sem("vchain"), sem("v32_ok"), sem("v_hi_ok")
    wkq_mm, wkq_ok, kq_mm, kq_hi_ok, kq_lo_ok = (sem(n) for n in ("wkq_mm", "wkq_ok", "kq_mm", "kq_hi_ok", "kq_lo_ok"))
    wi_mm, wi_hi_ok, wi_lo_ok, wh_hi_ok = sem("wi_mm"), sem("wi_hi_ok"), sem("wi_lo_ok"), sem("wh_hi_ok")
    FULL = MT - 1
    keys = [(h, c) for c in range(-(-M // CH)) for h in range(DH)]
    gru = [(h, n0, min(CH, G - n0)) for h in range(DH) for n0 in range(0, G, CH)]

    with nc.Block() as block:
        @block.sync
        def _(sp):
            for t, name in ((wq, "Wq"), (wk, "Wk"), (wv, "Wv")):
                sp.dma_start(t[:], io[name].rearrange("(c p) f -> p c f", p=P)).then_inc(ld_w, 16)
            sp.dma_start(cols[:], io["x_cols"]).then_inc(ld_w, 16)
            sp.dma_start(cxT[:], io["ctxT"].rearrange("(c p) t -> p c t", p=P)).then_inc(ld_cT, 16)
            sp.wait_ge(zeroed, 1)
            sp.dma_start(cx[:, 0:FULL], io["ctx"][0:FULL * P].rearrange("(t p) d -> p t d", p=P)).then_inc(ld_c, 16)
            sp.dma_start(cx[0:MROWS[-1], FULL], io["ctx"][FULL * P:]).then_inc(ld_c, 16)
            sp.dma_start(wiT[:], io["gru_wiT"].rearrange("(c p) f -> p c f", p=P)).then_inc(ld_g, 16)
            sp.dma_start(whT[:], io["gru_whT"].rearrange("(c p) f -> p c f", p=P)).then_inc(ld_g, 16)
            sp.dma_start(bi[:], io["gru_cols"]).then_inc(ld_g, 16)

        @block.scalar
        def _(act):
            act.wait_ge(ld_c, 32)
            for m in range(MT):
                if m >= 2:
                    act.wait_ge(squares, m - 1)
                act.activation(junk[:, m % 2], cx[:, m], ACT.Square, accum_out=ss[:, m:m + 1]).then_inc(squares, 1)
            for i, (h, c) in enumerate(keys):
                n = min(CH, M - c * CH)
                act.wait_ge(kq_mm, i + 1)
                act.activation(kq_hi[:, h, c * CH:c * CH + n], bank[2 + i % 2][:, 0:n], ACT.Copy,
                               scale=cols[:, DH + h:DH + h + 1]).then_inc(kq_hi_ok, 1)
            act.wait_ge(v32_ok, MT)
            act.activation(v_hi[:], v32[:], ACT.Copy).then_inc(v_hi_ok, 1)
            act.wait_ge(ld_g, 48)
            act.activation(wh_hi[:], whT[:], ACT.Copy).then_inc(wh_hi_ok, 1)
            for i, (h, n0, n) in enumerate(gru):
                act.wait_ge(wi_mm, i + 1)
                act.activation(wi_hi[:, h, n0:n0 + n], bank[4 + i % 2][:, 0:n], ACT.Copy,
                               scale=cols[:, h:h + 1]).then_inc(wi_hi_ok, 1)

        @block.vector
        def _(v):
            k = Chain(v, vchain)
            v.memset(cx[:, FULL], 0.0).then_inc(zeroed, 1)
            v.wait_ge(ld_w, 64)
            for h in range(DH):
                v.wait_ge(wkq_mm, h + 1)
                v.tensor_scalar(wkq[:, h], bank[h][:, 0:D], cols[:, h:h + 1], None, ALU.mult).then_inc(wkq_ok, 1)
            v.wait_ge(squares, MT)
            k.step(v.tensor_scalar(ss[:], ss[:], 1.0 / D, EPS_RMS, ALU.mult, ALU.add))
            rsqrt_steps(v, k, rs[:], ss[:], tmp[:])
            k.step(v.tensor_scalar(rs16[:], rs[:], float(D) ** -0.5, None, ALU.mult))
            for m in range(MT):
                v.tensor_scalar(v32[:, m], cx[:, m], rs[:, m:m + 1], None, ALU.mult).then_inc(v32_ok, 1)
            for i, (h, c) in enumerate(keys):
                n = min(CH, M - c * CH)
                v.wait_ge(kq_hi_ok, i + 1)
                v.scalar_tensor_tensor(out=kq_lo[:, h, c * CH:c * CH + n], in0=bank[2 + i % 2][:, 0:n],
                                       scalar=cols[:, DH + h:DH + h + 1],
                                       in1=kq_hi[:, h, c * CH:c * CH + n].bitcast(F32),
                                       op0=ALU.mult, op1=ALU.subtract).then_inc(kq_lo_ok, 1)
            v.wait_ge(v_hi_ok, 1)
            k.mark(v.tensor_tensor(v_lo[:], v32[:], v_hi[:].bitcast(F32), ALU.subtract))
            v.wait_ge(wh_hi_ok, 1)
            k.mark(v.tensor_tensor(wh_lo[:], whT[:], wh_hi[:].bitcast(F32), ALU.subtract))
            for i, (h, n0, n) in enumerate(gru):
                v.wait_ge(wi_hi_ok, i + 1)
                v.scalar_tensor_tensor(out=wi_lo[:, h, n0:n0 + n], in0=bank[4 + i % 2][:, 0:n], scalar=cols[:, h:h + 1],
                                       in1=wi_hi[:, h, n0:n0 + n].bitcast(F32), op0=ALU.mult,
                                       op1=ALU.subtract).then_inc(wi_lo_ok, 1)
            k.mark(v.tensor_tensor(bias[:, 0:2 * DH], bi[:, 0:2 * DH], bi[:, 3 * DH:5 * DH], ALU.add))
            k.mark(v.tensor_copy(bias[:, 2 * DH:3 * DH], bi[:, 2 * DH:3 * DH]))
            k.step(v.tensor_copy(bias[:, 3 * DH:], bi[:, 5 * DH:]))

        @block.tensor
        def _(pe):
            pe.wait_ge(ld_w, 64)
            for h in range(DH):
                for k in range(DH):
                    last = pe.matmul(bank[h][:, 0:D], wk[:, k, h * P:(h + 1) * P], wq[:, k], start=(k == 0), stop=(k == DH - 1))
                last.then_inc(wkq_mm, 1)
            pe.wait_ge(wkq_ok, DH)
            pe.wait_ge(ld_cT, 16)
            for i, (h, c) in enumerate(keys):
                n = min(CH, M - c * CH)
                if i >= 2:
                    pe.wait_ge(kq_lo_ok, i - 1)
                for k in range(DH):
                    last = pe.matmul(bank[2 + i % 2][:, 0:n], wkq[:, k, h * P:(h + 1) * P], cxT[:, k, c * CH:c * CH + n],
                                     start=(k == 0), stop=(k == DH - 1))
                last.then_inc(kq_mm, 1)
            pe.wait_ge(ld_g, 48)
            for i, (h, n0, n) in enumerate(gru):
                if i >= 2:
                    pe.wait_ge(wi_lo_ok, i - 1)
                for k in range(DH):
                    last = pe.matmul(bank[4 + i % 2][:, 0:n], wv[:, k, h * P:(h + 1) * P], wiT[:, k, n0:n0 + n],
                                     start=(k == 0), stop=(k == DH - 1))
                last.then_inc(wi_mm, 1)


SLOTS = 256
SH = SLOTS // P
TOP = 2
TILES = T * TOP // SLOTS + NE - 1
ROWS = TILES * SLOTS
SHIFT = SLOTS.bit_length() - 1


def layer_norm_tiles(v, k, tiles, z, stats, mv, var, rs, tmp, out, done):
    sl = slice(tiles[0], tiles[-1] + 1)
    for t in tiles:
        mark = k.mark(v.bn_stats(stats[:, t], z[:, t]))
    for t in tiles:
        v.wait_ge(k.sem, mark)
        mark2 = k.mark(v.bn_aggr(mv[:, t], stats[:, t]))
    v.wait_ge(k.sem, mark2)
    k.step(v.tensor_scalar(var[:, sl], mv[:, sl, 1], EPS_LN, None, ALU.add))
    rsqrt_steps(v, k, rs[:, sl], var[:, sl], tmp[:, 0:len(tiles)])
    for t in tiles:
        v.tensor_scalar(out[:, t], z[:, t], mv[:, t, 0:1], rs[:, t:t + 1], ALU.subtract, ALU.mult).then_inc(done, 1)


def route(nc, io, shared):
    ident, ones, sT = shared["ident"], shared["ones"], shared["sT"]
    emap, slot, gate = shared["emap"], shared["slot"], shared["gate"]
    with ExitStack() as ctx:
        def sb(name, shape, dt=F32):
            return ctx.enter_context(nc.sbuf_tensor("r_" + name, shape, dt))

        def sem(name):
            return ctx.enter_context(nc.semaphore("r_" + name))

        bank = [ctx.enter_context(nc.psum_tensor(f"r_bank{i}", [P, CH], F32)) for i in range(8)]
        x2 = sb("x2", [P, NT, D])
        x2T = sb("x2T", [P, 2, TPC, DH, P])
        stats, mv = sb("stats", [P, NT, 6]), sb("mv", [P, NT, 2])
        var, rs, tmp = sb("var", [P, NT]), sb("rs", [P, NT]), sb("tmp", [P, NT])
        rw = sb("rw", [P, DH, NE])
        rb = sb("rb", [P, 2, NE])
        tri = sb("tri", [P, P])
        lower = sb("lower", [P, NE, NE])
        tile_no = sb("tile_no", [P, TILES], I32)
        tile_f = sb("tile_f", [P, TILES])
        lg = sb("lg", [P, NT, NE])
        red = sb("red", [P, NT])
        pr = sb("pr", [P, NT, NE])
        pairs = sb("pairs", [P, NT, NE, NE])
        pairs2 = sb("pairs2", [P, NT, NE, NE])
        rank = sb("rank", [P, NT, NE])
        chosen = [sb(f"chosen{k}", [P, NT, NE]) for k in range(TOP)]
        sel = sb("sel", [P, NT, NE])
        place = sb("place", [P, NT, NE])
        cum = sb("cum", [P, NT + 1, NE])
        tot = sb("tot", [P, NT, NE])
        cnt = sb("cnt", [P, NE], I32)
        ntile, end = sb("ntile", [P, NE]), sb("end", [P, NE])
        emf = sb("emf", [P, TILES, NE])
        emr = sb("emr", [P, TILES])
        pf = sb("pf", [P, TOP, NT])

        ld_x, ld_r, consts, gchain, vchain = (sem(n) for n in ("ld_x", "ld_r", "consts", "gchain", "vchain"))
        turn_mm, z_ok, x2_ok, x2T_mm, x2T_ok, lg_mm, sub_ok, exp_ok = (
            sem(n) for n in ("turn_mm", "z_ok", "x2_ok", "x2T_mm", "x2T_ok", "lg_mm", "sub_ok", "exp_ok"))
        sel_ok, pos_mm, slot_ok, sent, kept = (sem(n) for n in ("sel_ok", "pos_mm", "slot_ok", "sent", "kept"))

        block = ctx.enter_context(nc.Block())

        @block.sync
        def _(sp):
            sp.dma_start(x2[:], io["x1"].rearrange("(t p) d -> p t d", p=P)).then_inc(ld_x, 16)
            sp.dma_start(rw[:], io["router_w"].rearrange("(c p) e -> p c e", p=P)).then_inc(ld_r, 16)
            sp.dma_start(rb[:, 0], io["router_b"].partition_broadcast(P)).then_inc(ld_r, 16)
            sp.dma_start(rb[:, 1], io["expert_bias"].partition_broadcast(P)).then_inc(ld_r, 16)
            shared["load_weights"](sp)
            sp.wait_ge(x2_ok, NT)
            sp.dma_start(io["x2"].rearrange("(t p) d -> p t d", p=P), x2[:]).then_inc(kept, 16)
            sp.wait_ge(kept, 16)

        @block.gpsimd
        def _(pool):
            g = Chain(pool, gchain)
            g.step(pool.memset(tri[:], 1.0))
            g.step(pool.affine_select(out=tri[:], in_=tri[:], compare_op=ALU.is_ge, fill=0.0,
                                      base=-1, pattern=[[1, P]], channel_multiplier=-1))
            g.step(pool.memset(lower[:], 1.0))
            g.step(pool.affine_select(out=lower[:], in_=lower[:], compare_op=ALU.is_ge, fill=0.0,
                                      base=-1, pattern=[[1, NE], [-1, NE]], channel_multiplier=0))
            pool.iota(tile_no[:], pattern=[[1, TILES]], base=0, channel_multiplier=0).then_inc(consts, 1)
            pool.wait_ge(slot_ok, 1)
            pool.wait_ge(x2_ok, NT)
            for t in range(NT):
                for k in range(TOP):
                    pool.indirect_dma_start(out=io["routed"], out_offset=bass.IndirectOffsetOnAxis(slot[:, k, t:t + 1], 0),
                                            in_=x2[:, t], in_offset=None).then_inc(sent, 16)
            pool.wait_ge(sent, 16 * NT * TOP)

        @block.scalar
        def _(act):
            for c in range(NC):
                for j in range(TPC):
                    t = c * TPC + j
                    act.wait_ge(x2T_mm, t + 1)
                    if c >= 2:
                        act.wait_ge(lg_mm, (c - 2) * TPC + j + 1)
                    act.activation(x2T[:, c % 2, j].rearrange("p h n -> p (h n)"), bank[2 + t % 2][:, 0:D], ACT.Copy).then_inc(x2T_ok, 1)
            act.wait_ge(sub_ok, 1)
            act.activation(pr[:], lg[:], ACT.Exp).then_inc(exp_ok, 1)

        @block.vector
        def _(v):
            k = Chain(v, vchain)
            v.wait_ge(ld_x, 16)
            for c in range(NC):
                tiles = list(range(c * TPC, (c + 1) * TPC))
                for t in tiles:
                    v.wait_ge(turn_mm, t + 1)
                    v.tensor_tensor(x2[:, t], bank[t % 2][:, 0:D], x2[:, t], ALU.add).then_inc(z_ok, 1)
                v.wait_ge(z_ok, tiles[-1] + 1)
                layer_norm_tiles(v, k, tiles, x2, stats, mv, var, rs, tmp, x2, x2_ok)
            v.wait_ge(lg_mm, NT)
            v.wait_ge(ld_r, 48)
            k.step(v.tensor_tensor(lg[:], bank[4][:, 0:NT * NE].rearrange("p (t e) -> p t e", e=NE), bc(rb[:, 0], 1, NT), ALU.add))
            k.step(v.tensor_tensor(lg[:], lg[:], bc(rb[:, 1], 1, NT), ALU.add))
            k.step(v.tensor_reduce(red[:], lg[:], AX_X, ALU.max))
            v.tensor_tensor(lg[:], lg[:], bc(red[:], 2, NE), ALU.subtract).then_inc(sub_ok, 1)
            v.wait_ge(exp_ok, 1)
            k.step(v.tensor_reduce(red[:], pr[:], AX_X, ALU.add))
            k.step(v.reciprocal(red[:], red[:]))
            k.step(v.tensor_tensor(pr[:], pr[:], bc(red[:], 2, NE), ALU.mult))
            v.wait_ge(consts, 1)
            k.step(v.tensor_tensor(pairs[:], bc(pr[:], 2, NE), bc(pr[:], 3, NE), ALU.is_equal))
            k.step(v.tensor_tensor(pairs[:], pairs[:], bc(lower[:], 1, NT), ALU.mult))
            k.step(v.tensor_tensor(pairs2[:], bc(pr[:], 2, NE), bc(pr[:], 3, NE), ALU.is_gt))
            k.step(v.tensor_tensor(pairs[:], pairs[:], pairs2[:], ALU.add))
            k.step(v.tensor_reduce(rank[:], pairs[:], AX_X, ALU.add))
            k.step(v.tensor_scalar(chosen[0][:], rank[:], 0.0, None, ALU.is_equal))
            k.step(v.tensor_scalar(chosen[1][:], rank[:], 1.0, None, ALU.is_equal))
            v.tensor_tensor(sel[:], chosen[0][:], chosen[1][:], ALU.add).then_inc(sel_ok, 1)
            for i in range(TOP):
                k.step(v.tensor_tensor(place[:], pr[:], chosen[i][:], ALU.mult))
                k.step(v.tensor_reduce(gate[:, i], place[:], AX_X, ALU.add))
            k.step(v.tensor_tensor(red[:], gate[:, 0], gate[:, 1], ALU.add))
            k.step(v.tensor_scalar(red[:], red[:], 1e-9, None, ALU.add))
            k.step(v.reciprocal(red[:], red[:]))
            for i in range(TOP):
                k.step(v.tensor_tensor(gate[:, i], gate[:, i], red[:], ALU.mult))
            v.wait_ge(pos_mm, 1)
            k.step(v.tensor_copy(tot[:], bank[6][:, 0:NT * NE].rearrange("p (t e) -> p t e", e=NE)))
            k.step(v.memset(cum[:, 0], 0.0))
            for t in range(NT):
                k.step(v.tensor_tensor(cum[:, t + 1], cum[:, t], tot[:, t], ALU.add))
            k.step(v.tensor_scalar(cnt[:], cum[:, NT], float(SLOTS - 1), None, ALU.add))
            k.step(v.tensor_scalar(cnt[:], cnt[:], SHIFT, None, ALU.arith_shift_right))
            k.step(v.tensor_copy(ntile[:], cnt[:]))
            k.step(v.tensor_copy(end[:, 0:1], ntile[:, 0:1]))
            for e in range(1, NE):
                k.step(v.tensor_tensor(end[:, e:e + 1], end[:, e - 1:e], ntile[:, e:e + 1], ALU.add))
            k.step(v.tensor_tensor(ntile[:], end[:], ntile[:], ALU.subtract))
            k.step(v.tensor_scalar(ntile[:], ntile[:], float(SLOTS), None, ALU.mult))
            k.step(v.tensor_tensor(place[:], bank[5][:, 0:NT * NE].rearrange("p (t e) -> p t e", e=NE), cum[:, 0:NT], ALU.add))
            k.step(v.tensor_tensor(place[:], place[:], bc(ntile[:], 1, NT), ALU.add))
            for i in range(TOP):
                k.step(v.tensor_tensor(rank[:], place[:], chosen[i][:], ALU.mult))
                k.step(v.tensor_reduce(pf[:, i], rank[:], AX_X, ALU.add))
            v.tensor_copy(slot[:], pf[:]).then_inc(slot_ok, 1)
            k.step(v.tensor_copy(tile_f[:], tile_no[:]))
            k.step(v.tensor_tensor(emf[:], bc(tile_f[:], 2, NE), bc(end[:], 1, TILES), ALU.is_ge))
            k.step(v.tensor_reduce(emr[:], emf[:], AX_X, ALU.add))
            k.step(v.tensor_scalar(emap[:], emr[:], float(NE - 1), None, ALU.min))

        @block.tensor
        def _(pe):
            def turn_x2(t):
                pe.wait_ge(x2_ok, t + 1)
                if t >= 2:
                    pe.wait_ge(x2T_ok, t - 1)
                for h in range(DH):
                    last = pe.transpose(bank[2 + t % 2][:, h * P:(h + 1) * P], x2[:, t, h * P:(h + 1) * P], ident[:])
                last.then_inc(x2T_mm, 1)

            def logits(t):
                pe.wait_ge(x2T_ok, t + 1)
                if t == 0:
                    pe.wait_ge(ld_r, 48)
                for h in range(DH):
                    last = pe.matmul(bank[4][:, t * NE:(t + 1) * NE], x2T[:, (t // TPC) % 2, t % TPC, h], rw[:, h],
                                     start=(h == 0), stop=(h == DH - 1))
                last.then_inc(lg_mm, 1)

            for t in range(NT):
                if t >= 2:
                    pe.wait_ge(z_ok, t - 1)
                for h in range(DH):
                    last = pe.transpose(bank[t % 2][:, h * P:(h + 1) * P], sT[:, h, t * P:(t + 1) * P], ident[:])
                last.then_inc(turn_mm, 1)
            for t in range(NT):
                turn_x2(t)
                if t >= 1:
                    logits(t - 1)
            logits(NT - 1)
            pe.wait_ge(consts, 1)
            pe.wait_ge(sel_ok, 1)
            pe.matmul(bank[5][:, 0:NT * NE], tri[:], sel[:].rearrange("p t e -> p (t e)"), start=True, stop=True)
            pe.matmul(bank[6][:, 0:NT * NE], ones[:], sel[:].rearrange("p t e -> p (t e)"), start=True,
                      stop=True).then_inc(pos_mm, 1)


def experts(nc, io, shared):
    ident, sT, emap = shared["ident"], shared["sT"], shared["emap"]
    w1, w2, b1, b2, ld_e = (shared[n] for n in ("w1", "w2", "b1", "b2", "ld_e"))
    FP = FT // 2
    with ExitStack() as ctx:
        def sb(name, shape, dt=F32):
            return ctx.enter_context(nc.sbuf_tensor("e_" + name, shape, dt))

        def sem(name):
            return ctx.enter_context(nc.semaphore("e_" + name))

        bank = [ctx.enter_context(nc.psum_tensor(f"e_bank{i}", [P, CH], F32)) for i in range(8)]
        w1_hi, w1_lo = sb("w1_hi", [P, DH, F], F32R), sb("w1_lo", [P, DH, F], F32R)
        w2_hi, w2_lo = sb("w2_hi", [P, FT, D], F32R), sb("w2_lo", [P, FT, D], F32R)
        xT_hi, xT_lo = sb("xT_hi", [P, 2, DH, SLOTS], F32R), sb("xT_lo", [P, 2, DH, SLOTS], F32R)
        g_hi, g_lo = sb("g_hi", [P, FT, SLOTS], F32R), sb("g_lo", [P, FT, SLOTS], F32R)
        room = sT[:].rearrange("p c (a n) -> p (c a) n", n=CH)
        xg = [room[:, i].rearrange("p (s d) -> p s d", s=SH) for i in range(2)]
        y = [room[:, 2 + i].rearrange("p (s d) -> p s d", s=SH) for i in range(2)]
        g32 = [room[:, 4 + i].rearrange("p (f n) -> p f n", f=2) for i in range(2)]

        ld_x, y_out = [sem("ld_x0"), sem("ld_x1")], [sem("y_out0"), sem("y_out1")]
        xT_mm, xT_hi_ok, xT_lo_ok, w1_hi_ok, w1_lo_ok, w2_hi_even, w2_hi_odd, w2_lo_ok = (
            sem(n) for n in ("xT_mm", "xT_hi_ok", "xT_lo_ok", "w1_hi_ok", "w1_lo_ok", "w2_hi_even", "w2_hi_odd", "w2_lo_ok"))
        up_mm, g32_ok, g_hi_ok, g_lo_ok, y_mm, y_ok = (
            sem(n) for n in ("up_mm", "g32_ok", "g_hi_ok", "g_lo_ok", "y_mm", "y_ok"))
        block = ctx.enter_context(nc.Block())

        @block.sync
        def _(sp):
            routed = io["routed"].rearrange("(i s p) d -> i p s d", s=SH, p=P)
            results = io["results"].rearrange("(i s p) d -> i p s d", s=SH, p=P)

            def load(i, slot):
                sp.dma_start(xg[slot], routed[bass.ds(i, 1)].rearrange("i p s d -> (i p) s d")).then_inc(ld_x[slot], 16)

            def store(i, slot):
                sp.wait_ge(y_ok, SH * (i + 1))
                sp.dma_start(results[bass.ds(i, 1)].rearrange("i p s d -> (i p) s d"), y[slot]).then_inc(y_out[slot], 16)

            load(0, 0)
            load(1, 1)
            with sp.Fori(0, TILES // 2 - 1) as it:
                for slot in range(2):
                    i = it * 2 + slot
                    sp.wait_ge(xT_mm, i + 1)
                    load(i + 2, slot)
                    store(i, slot)
            sp.wait_ge(xT_mm, TILES - 2)
            load(TILES - 1, 0)
            for i in range(TILES - 3, TILES):
                store(i, i % 2)
            sp.wait_ge(y_out[0], 16 * (TILES // 2 + 1))
            sp.wait_ge(y_out[1], 16 * (TILES // 2))

        @block.gpsimd
        def _(pool):
            pool.wait_ge(ld_e, 16 * (2 * NE + 2))

            def body(i, first=False):
                ex = pool.value_load(emap[0:1, bass.ds(i, 1)], min_val=0, max_val=NE - 1)
                if not first:
                    pool.wait_ge(y_mm, i * SH)
                for f in range(0, FP, 2):
                    pool.tensor_copy(w2_hi[:, 2 * f:2 * f + 2], w2[:, bass.ds(ex, 1), 2 * f:2 * f + 2].rearrange("p e c f -> p (e c) f")).then_inc(w2_hi_even, 1)

            body(0, first=True)
            with pool.Fori(1, TILES) as i:
                body(i)

        @block.scalar
        def _(act):
            act.wait_ge(ld_e, 16 * (2 * NE + 2))

            def turn(i, slot):
                act.wait_ge(xT_mm, i + 1)
                act.activation(xT_hi[:, slot].rearrange("p c n -> p (c n)"), bank[0][:], ACT.Copy).then_inc(xT_hi_ok, 1)

            def w1_high(i, ex, f):
                cols = slice(f * 2 * P, (f + 1) * 2 * P)
                act.activation(w1_hi[:, :, cols], w1[:, bass.ds(ex, 1), :, cols].rearrange("p e c f -> p (e c) f"), ACT.Copy).then_inc(w1_hi_ok, 1)

            def body(i, slot, n, first=False, last=False):
                ex = act.value_load(emap[0:1, bass.ds(i, 1)], min_val=0, max_val=NE - 1)
                if not last:
                    nx = act.value_load(emap[0:1, bass.ds(i + 1, 1)], min_val=0, max_val=NE - 1)
                for f in range(FP):
                    if f % 2 == 1:
                        if not first:
                            act.wait_ge(y_mm, i * SH)
                        act.activation(w2_hi[:, 2 * f:2 * f + 2], w2[:, bass.ds(ex, 1), 2 * f:2 * f + 2].rearrange("p e c f -> p (e c) f"), ACT.Copy).then_inc(w2_hi_odd, 1)
                    act.wait_ge(up_mm, i * FP + f + 1)
                    if not (first and f < 2):
                        act.wait_ge(g_lo_ok, i * FP + f - 1)
                    for a in range(2):
                        act.activation(g32[f % 2][:, a], bank[1 + f % 2][:, a * SLOTS:(a + 1) * SLOTS], ACT.Gelu,
                                       bias=b1[:, bass.ds(ex * FT + (2 * f + a), 1)]).then_inc(g32_ok, 1)
                    act.wait_ge(g32_ok, (i * FP + f + 1) * 2)
                    if not first:
                        act.wait_ge(y_mm, i * SH)
                    act.activation(g_hi[:, 2 * f:2 * f + 2], g32[f % 2], ACT.Copy).then_inc(g_hi_ok, 1)
                    if f == FP - 1 and not last:
                        turn(i + 1, 1 - slot)
                if not last:
                    for f in range(FP):
                        w1_high(i + 1, nx, f)

            ex0 = act.value_load(emap[0:1, 0:1], min_val=0, max_val=NE - 1)
            turn(0, 0)
            for f in range(FP):
                w1_high(0, ex0, f)
            body(0, 0, 0, first=True)
            body(1, 1, 0)
            with act.Fori(1, TILES // 2) as it:
                body(it * 2, 0, it)
                body(it * 2 + 1, 1, it)
            body(TILES - 1, 0, TILES // 2, last=True)

        @block.vector
        def _(v):
            v.wait_ge(ld_e, 16 * (2 * NE + 2))

            def turn(i, slot):
                v.wait_ge(xT_hi_ok, i + 1)
                v.tensor_tensor(xT_lo[:, slot].rearrange("p c n -> p (c n)"), bank[0][:],
                                xT_hi[:, slot].bitcast(F32).rearrange("p c n -> p (c n)"), ALU.subtract).then_inc(xT_lo_ok, 1)

            def split_w1(i, ex, f):
                cols = slice(f * 2 * P, (f + 1) * 2 * P)
                v.wait_ge(w1_hi_ok, i * FP + f + 1)
                v.tensor_tensor(w1_lo[:, :, cols], w1[:, bass.ds(ex, 1), :, cols].rearrange("p e c f -> p (e c) f"),
                                w1_hi[:, :, cols].bitcast(F32), ALU.subtract).then_inc(w1_lo_ok, 1)

            def split_w2(i, ex, f):
                v.wait_ge(w2_hi_odd if f % 2 else w2_hi_even, i * (FP // 2) + f // 2 + 1)
                v.tensor_tensor(w2_lo[:, 2 * f:2 * f + 2], w2[:, bass.ds(ex, 1), 2 * f:2 * f + 2].rearrange("p e c f -> p (e c) f"),
                                w2_hi[:, 2 * f:2 * f + 2].bitcast(F32), ALU.subtract).then_inc(w2_lo_ok, 1)

            def body(i, slot, n, warm_up=False, last=False):
                ex = v.value_load(emap[0:1, bass.ds(i, 1)], min_val=0, max_val=NE - 1)
                if not last:
                    nx = v.value_load(emap[0:1, bass.ds(i + 1, 1)], min_val=0, max_val=NE - 1)
                for f in range(FP):
                    split_w2(i, ex, f)
                    v.wait_ge(g_hi_ok, i * FP + f + 1)
                    v.tensor_tensor(g_lo[:, 2 * f:2 * f + 2], g32[f % 2], g_hi[:, 2 * f:2 * f + 2].bitcast(F32),
                                    ALU.subtract).then_inc(g_lo_ok, 1)
                    if f == FP - 1 and not last:
                        turn(i + 1, 1 - slot)
                for s in range(SH):
                    if not last:
                        split_w1(i + 1, nx, 2 * s)
                        split_w1(i + 1, nx, 2 * s + 1)
                    v.wait_ge(y_mm, i * SH + s + 1)
                    if s == 0 and not warm_up:
                        v.wait_ge(y_out[slot], 16 * n)
                    v.tensor_tensor(y[slot][:, s], bank[3 + s][:, 0:D], b2[:, bass.ds(ex * D, D)], ALU.add).then_inc(y_ok, 1)

            ex0 = v.value_load(emap[0:1, 0:1], min_val=0, max_val=NE - 1)
            turn(0, 0)
            for f in range(FP):
                split_w1(0, ex0, f)
            body(0, 0, 0, warm_up=True)
            body(1, 1, 0, warm_up=True)
            with v.Fori(1, TILES // 2) as it:
                body(it * 2, 0, it)
                body(it * 2 + 1, 1, it)
            body(TILES - 1, 0, TILES // 2, last=True)

        @block.tensor
        def _(pe):
            def turn(i, slot, n):
                pe.wait_ge(ld_x[slot], 16 * (n + 1))
                for h in range(DH):
                    for s in range(SH):
                        last = pe.transpose(bank[0][:, (h * SH + s) * P:(h * SH + s + 1) * P], xg[slot][:, s, h * P:(h + 1) * P], ident[:])
                last.then_inc(xT_mm, 1)

            def body(i, slot, n, first=False, last=False):
                pe.wait_ge(xT_lo_ok, i + 1)
                for f in range(FP):
                    pe.wait_ge(w1_lo_ok, i * FP + f + 1)
                    if not (first and f < 2):
                        pe.wait_ge(g32_ok, (i * FP + f - 1) * 2)
                    for a in range(2):
                        fs = slice((2 * f + a) * P, (2 * f + a + 1) * P)
                        for h in range(DH):
                            mm = three_pass(pe, bank[1 + f % 2][:, a * SLOTS:(a + 1) * SLOTS], w1_hi[:, h, fs], w1_lo[:, h, fs],
                                            xT_hi[:, slot, h], xT_lo[:, slot, h], h == 0, h == DH - 1)
                    mm.then_inc(up_mm, 1)
                    if f == 2 and not last:
                        turn(i + 1, 1 - slot, n + slot)
                for s in range(SH):
                    if not first:
                        pe.wait_ge(y_ok, (i - 1) * SH + s + 1)
                    for f in range(FT):
                        if s == 0 and f % 2 == 0:
                            pe.wait_ge(w2_lo_ok, i * FP + f // 2 + 1)
                            pe.wait_ge(g_lo_ok, i * FP + f // 2 + 1)
                        ss = slice(s * P, (s + 1) * P)
                        mm = three_pass(pe, bank[3 + s][:, 0:D], g_hi[:, f, ss], g_lo[:, f, ss], w2_hi[:, f], w2_lo[:, f],
                                        f == 0, f == FT - 1)
                    mm.then_inc(y_mm, 1)

            turn(0, 0, 0)
            body(0, 0, 0, first=True)
            body(1, 1, 0)
            with pe.Fori(1, TILES // 2) as it:
                body(it * 2, 0, it)
                body(it * 2 + 1, 1, it)
            body(TILES - 1, 0, TILES // 2, last=True)


def combine(nc, io, shared):
    slot, gate = shared["slot"], shared["gate"]
    with ExitStack() as ctx:
        def sb(name, shape, dt=F32):
            return ctx.enter_context(nc.sbuf_tensor("c_" + name, shape, dt))

        def sem(name):
            return ctx.enter_context(nc.semaphore("c_" + name))

        x2 = sb("x2", [P, NT, D])
        yk = sb("yk", [P, NT, TOP, D])
        stats, mv = sb("stats", [P, NT, 6]), sb("mv", [P, NT, 2])
        var, rs, tmp = sb("var", [P, NT]), sb("rs", [P, NT]), sb("tmp", [P, NT])
        ld_x, vchain, out_ok, stored = (sem(n) for n in ("ld_x", "vchain", "out_ok", "stored"))
        got = [sem(f"got{c}") for c in range(NC)]
        block = ctx.enter_context(nc.Block())

        @block.sync
        def _(sp):
            sp.dma_start(x2[:], io["x2"].rearrange("(t p) d -> p t d", p=P)).then_inc(ld_x, 16)
            out = io["out"].rearrange("(t p) d -> p t d", p=P)
            for c in range(NC):
                ts = slice(c * TPC, (c + 1) * TPC)
                sp.wait_ge(out_ok, (c + 1) * TPC)
                sp.dma_start(out[:, ts], x2[:, ts]).then_inc(stored, 16)
            sp.wait_ge(stored, 16 * NC)

        @block.gpsimd
        def _(pool):
            for t in range(NT):
                for k in range(TOP):
                    pool.indirect_dma_start(out=yk[:, t, k], out_offset=None, in_=io["results"],
                                            in_offset=bass.IndirectOffsetOnAxis(slot[:, k, t:t + 1], 0)).then_inc(got[t // TPC], 16)

        @block.vector
        def _(v):
            k = Chain(v, vchain)
            v.wait_ge(ld_x, 16)
            for c in range(NC):
                tiles = list(range(c * TPC, (c + 1) * TPC))
                v.wait_ge(got[c], 16 * TPC * TOP)
                for i in range(TOP):
                    for t in tiles:
                        mark = k.mark(v.scalar_tensor_tensor(out=x2[:, t], in0=yk[:, t, i], scalar=gate[:, i, t:t + 1],
                                                             in1=x2[:, t], op0=ALU.mult, op1=ALU.add))
                    v.wait_ge(vchain, mark)
                layer_norm_tiles(v, k, tiles, x2, stats, mv, var, rs, tmp, x2, out_ok)



def program(nc, io):
    with ExitStack() as ctx:
        def sb(name, shape, dt=F32):
            return ctx.enter_context(nc.sbuf_tensor(name, shape, dt))

        shared = {"ident": sb("ident", [P, P]), "ones": sb("ones", [P, P]), "sT": sb("sT", [P, DH, T])}
        decay_attention_and_mlp(nc, io, shared)
        cross_attention(nc, io, shared)
        shared |= {"emap": sb("emap", [P, TILES], I32), "slot": sb("slot", [P, TOP, NT], I32), "gate": sb("gate", [P, TOP, NT])}
        with ExitStack() as weights:
            def wsb(name, shape):
                return weights.enter_context(nc.sbuf_tensor(name, shape, F32))

            w1, w2 = wsb("w1", [P, NE, DH, F]), wsb("w2", [P, NE, FT, D])
            b1, b2 = wsb("b1", [P, NE * FT]), wsb("b2", [P, NE * D])
            ld_e = weights.enter_context(nc.semaphore("ld_e"))
            shared |= {"w1": w1, "w2": w2, "b1": b1, "b2": b2, "ld_e": ld_e}

            def load_weights(sp):
                sp.dma_start(b1[:], io["b1_cols"]).then_inc(ld_e, 16)
                sp.dma_start(b2[:], io["b2"].rearrange("e d -> (e d)").partition_broadcast(P)).then_inc(ld_e, 16)
                for e in range(NE):
                    sp.dma_start(w1[:, e], io["w1"][e].rearrange("(c p) f -> p c f", p=P)).then_inc(ld_e, 16)
                    sp.dma_start(w2[:, e], io["w2"][e].rearrange("(c p) f -> p c f", p=P)).then_inc(ld_e, 16)

            shared["load_weights"] = load_weights
            route(nc, io, shared)
            experts(nc, io, shared)
        combine(nc, io, shared)


def kernel(**inputs):
    import numpy as np
    import concourse.bacc as bacc
    from concourse.bass_utils import run_bass_kernel_spmd

    a = {name: np.asarray(value) for name, value in inputs.items()}

    def turned(x):
        return np.ascontiguousarray(x.T)

    def columns(*names):
        return np.ascontiguousarray(np.concatenate([a[n].reshape(-1, P).T for n in names], axis=1))

    x, context = a["x"][0], a["ctx_1024"][0]
    send = {
        "x": x, "xT": turned(x), "u": a["L0_attn_u"], "v": a["L0_attn_v"],
        "decay": a["L0_attn_decay_logit"], "alpha": a["L0_attn_alpha_logit"],
        "gate": a["L0_attn_k_base_gate_logit"].reshape(1), "taps": a["L0_attn_k_base_kernel"],
        "projT": turned(a["L0_attn_proj_w"]), "proj_b": a["L0_attn_proj_b"], "norm1_w": a["L0_attn_norm1_w"],
        "mlp_w1": a["L0_attn_mlp_w1"], "mlp_w2": a["L0_attn_mlp_w2"], "mlp_b2": a["L0_attn_mlp_b2"],
        "a_cols": columns("L0_attn_norm1_w", "L0_attn_norm2_w", "L0_attn_mlp_b1"),
        "ctx": context, "ctxT": turned(context),
        "Wq": a["L0_xattn_Wq"], "Wk": a["L0_xattn_Wk"], "Wv": a["L0_xattn_Wv"],
        "gru_wiT": turned(a["L0_xattn_gru_wi"]), "gru_whT": turned(a["L0_xattn_gru_wh"]),
        "x_cols": columns("L0_xattn_input_norm_w", "L0_xattn_slot_norm_w"),
        "gru_cols": columns("L0_xattn_gru_bi", "L0_xattn_gru_bh"),
        "router_w": a["L0_ffn_router_w"], "router_b": a["L0_ffn_router_b"], "expert_bias": a["L0_ffn_expert_bias"],
        "w1": a["L0_ffn_w1"], "w2": a["L0_ffn_w2"], "b1_cols": columns("L0_ffn_b1"), "b2": a["L0_ffn_b2"],
    }
    nc = bacc.Bacc("TRN2", target_bir_lowering=False, num_devices=1, dynamic_dma_scratch_size=4096)
    io = {k: nc.dram_tensor(f"in_{k}", v.shape, F32, kind="ExternalInput").ap() for k, v in send.items()}
    for name, shape in (("x1", (T, D)), ("x2", (T, D)), ("routed", (ROWS, D)), ("results", (ROWS, D))):
        io[name] = nc.dram_tensor(f"scratch_{name}", shape, F32).ap()
    io["out"] = nc.dram_tensor("out", (T, D), F32, kind="ExternalOutput").ap()
    program(nc, io)
    r = run_bass_kernel_spmd(nc, [{f"in_{k}": v for k, v in send.items()}], core_ids=[0])
    return r.results[0]["out"].reshape(1, T, D)
```

```python
from contextlib import ExitStack

import concourse.bass as bass
from concourse import mybir

F32 = mybir.dt.float32
F32R = mybir.dt.float32r
I32 = mybir.dt.int32
ALU = mybir.AluOpType
ACT = mybir.ActivationFunctionType
AX_X = mybir.AxisListType.X

P = 128
T = 2048
D = 256
DH = D // P
NT = T // P
CH = 512
NC = T // CH
TPC = CH // P
R = 16
SUB = 32
NSUB = P // SUB
KTAP = 4
F = 4 * D
FT = F // P
M = 1601
MT = -(-M // P)
MROWS = [min(P, M - m * P) for m in range(MT)]
ITERS = 3
NE = 8
EPS_LN = 1e-5
EPS_RMS = 1e-6
RSQRT_MAGIC = float(0x5F3759DF)
NEWTON = 3
RSQRT_STEPS = 2 + 3 * NEWTON


def bc(ap, axis, n):
    return ap.unsqueeze(axis).broadcast_to([*ap.shape[:axis], n, *ap.shape[axis:]])


class Chain:

    def __init__(self, eng, sem, base=0):
        self.eng, self.sem, self.n, self.base = eng, sem, 0, base

    def step(self, ins):
        self.n += 1
        ins.then_inc(self.sem, 1)
        self.eng.wait_ge(self.sem, self.base + self.n)

    def mark(self, ins):
        self.n += 1
        ins.then_inc(self.sem, 1)
        return self.base + self.n


def rsqrt_steps(v, chain, y, x, tmp):
    chain.step(v.tensor_scalar(tmp.bitcast(I32), x.bitcast(I32), 1, None, ALU.logical_shift_right))
    chain.step(v.tensor_scalar(y.bitcast(I32), tmp.bitcast(I32), -1.0, RSQRT_MAGIC, ALU.mult, ALU.add))
    for _ in range(NEWTON):
        chain.step(v.scalar_tensor_tensor(out=tmp, in0=y, scalar=-0.5, in1=y, op0=ALU.mult, op1=ALU.mult))
        chain.step(v.tensor_tensor(tmp, tmp, x, ALU.mult))
        chain.step(v.scalar_tensor_tensor(out=y, in0=tmp, scalar=1.5, in1=y, op0=ALU.add, op1=ALU.mult))


def three_pass(pe, out, w_hi, w_lo, x_hi, x_lo, start, stop):
    pe.matmul(out, w_hi, x_lo, start=start, stop=False)
    pe.matmul(out, w_lo, x_hi, start=False, stop=False)
    return pe.matmul(out, w_hi, x_hi, start=False, stop=stop)


def decay_attention_and_mlp(nc, io, shared):
    ident, ones, sT = shared["ident"], shared["ones"], shared["sT"]
    with ExitStack() as ctx:
        def sb(name, shape, dt=F32):
            return ctx.enter_context(nc.sbuf_tensor(name, shape, dt))

        def sem(name):
            return ctx.enter_context(nc.semaphore(name))

        bank = [ctx.enter_context(nc.psum_tensor(f"a_bank{i}", [P, CH], F32)) for i in range(8)]

        x = sb("a_x", [P, NT, D])
        hn = sb("a_hn", [P, NT, D])
        h2 = sb("a_h2", [P, NT, D])
        n2 = sb("a_n2", [P, 2, TPC, D])
        xT = oT = sT
        hT_hi = sb("a_hT_hi", [P, DH, 3 * CH], F32R)
        hT_lo = sb("a_hT_lo", [P, DH, 3 * CH], F32R)
        g32 = sb("a_g32", [P, 2, CH])
        g_hi = sb("a_g_hi", [P, FT, CH], F32R)
        g_lo = sb("a_g_lo", [P, FT, CH], F32R)
        w1_32 = sb("a_w1_32", [P, DH * F])
        w2_32 = n2[:].rearrange("p a t d -> p (a t d)")
        w1_hi = sb("a_w1_hi", [P, DH, F], F32R)
        w1_lo = sb("a_w1_lo", [P, DH, F], F32R)
        w2_hi = sb("a_w2_hi", [P, FT, D], F32R)
        w2_lo = sb("a_w2_lo", [P, FT, D], F32R)
        projT = sb("a_projT", [P, DH, D])
        uv = sb("a_uv", [P, DH, 2 * R])
        rows = sb("a_rows", [P, 3, D])
        cols = sb("a_cols", [P, 2 * DH + FT])
        sg = sb("a_sg", [P, 2 * R + 2])
        traw = sb("a_traw", [P, KTAP])
        lg = sb("a_lg", [P, R + 1])
        gk = sb("a_gk", [P, KTAP])
        expo = sb("a_expo", [P, 2, NSUB + 1], I32)
        expf = sb("a_expf", [P, 2, NSUB + 1])
        kw = sb("a_kw", [P, NSUB + 1, R])
        qw = sb("a_qw", [P, NSUB + 1, R])
        coef = sb("a_coef", [P, 1])
        taps = sb("a_taps", [P, KTAP, P + KTAP - 1])
        band = sb("a_band", [P, P + KTAP - 1])
        later = sb("a_later", [P, P])
        qk = sb("a_qk", [P, NT, 2, R])
        qkn = sb("a_qkn", [P, NT * 2])
        qkr = sb("a_qkr", [P, NT * 2])
        kcat = sb("a_kcat", [P, NT, 6, R])
        qcat = sb("a_qcat", [P, NT, 6, R])
        qkT = sb("a_qkT", [96, 3, 2 * P])
        AT = sb("a_AT", [P, 2, P])
        S = sb("a_S", [P, 4, D])
        ss = sb("a_ss", [P, NT])
        rs = sb("a_rs", [P, NT])
        tmp = sb("a_tmp", [P, 2 * NT])
        junk = sb("a_junk", [P, 2, D])
        qk_sq = junk[:].rearrange("p a (t b r) -> p (a t) b r", b=2, r=R)
        stats = sb("a_stats", [P, NT, 6])
        mv = sb("a_mv", [P, NT, 2])

        ld_x, ld_xT, ld_w, ld_mlp = sem("a_ld_x"), sem("a_ld_xT"), sem("a_ld_w"), sem("a_ld_mlp")
        consts, masked, hi_w = sem("a_consts"), sem("a_masked"), sem("a_hi_w")
        vchain, achain, gchain = sem("a_vchain"), sem("a_achain"), sem("a_gchain")
        squares, zeroed, gammas, expos, coef_ok = (sem(f"a_{n}") for n in ("squares", "zeroed", "gammas", "expos", "coef_ok"))
        hn_ok, uv_ok, qk_mm, cats = sem("a_hn_ok"), sem("a_uv_ok"), sem("a_qk_mm"), sem("a_cats")
        turned, turned_sb = sem("a_turned"), sem("a_turned_sb")
        A_mm, A_sb, o_mm, o_sb, S_mm, S_sb = (sem(f"a_{n}") for n in ("A_mm", "A_sb", "o_mm", "o_sb", "S_mm", "S_sb"))
        xb_ok, h2_mm, h2_sb, sq2, n2_ok = (sem(f"a_{n}") for n in ("xb_ok", "h2_mm", "h2_sb", "sq2", "n2_ok"))
        hT_mm, hT_hi_ok, hT_lo_ok, w_lo_ok = sem("a_hT_mm"), sem("a_hT_hi_ok"), sem("a_hT_lo_ok"), sem("a_w_lo_ok")
        up_mm, gelu_ok, g_ok, y_mm, z_ok, res_ok = (sem(f"a_{n}") for n in ("up_mm", "gelu_ok", "g_ok", "y_mm", "z_ok", "res_ok"))
        x1_ok, x1_mm, x1_sb, x1_out = (sem(f"a_{n}") for n in ("x1_ok", "x1_mm", "x1_sb", "x1_out"))


        def tile(t):
            return slice(t * P, (t + 1) * P)

        def chunk(c):
            return slice(c * CH, (c + 1) * CH)

        block = ctx.enter_context(nc.Block())

        @block.sync
        def _(sp):
            sp.dma_start(x[:], io["x"].rearrange("(t p) d -> p t d", p=P)).then_inc(ld_x, 16)
            sp.dma_start(w1_32[:].rearrange("p (c f) -> p c f", c=DH),
                         io["mlp_w1"].rearrange("(c p) f -> p c f", p=P)).then_inc(ld_mlp, 16)
            sp.dma_start(w2_32.rearrange("p (c f) -> p c f", c=FT),
                         io["mlp_w2"].rearrange("(c p) f -> p c f", p=P)).then_inc(ld_mlp, 16)
            sp.wait_ge(x1_ok, NC)
            sp.dma_start(io["x1"].rearrange("(t p) d -> p t d", p=P), h2[:]).then_inc(x1_out, 16)
            sp.wait_ge(x1_out, 16)

        @block.gpsimd
        def _(pool):
            g = Chain(pool, gchain)
            g.step(pool.memset(ident[:], 0.0))
            g.step(pool.memset(later[:], 1.0))
            g.step(pool.memset(taps[:], 0.0))
            g.step(pool.affine_select(out=ident[:], in_=ident[:], compare_op=ALU.not_equal, fill=1.0,
                                      base=0, pattern=[[-1, P]], channel_multiplier=1))
            g.step(pool.affine_select(out=later[:], in_=later[:], compare_op=ALU.is_ge, fill=0.0,
                                      base=0, pattern=[[1, P]], channel_multiplier=-1))
            for t in range(KTAP):
                g.step(pool.affine_select(out=taps[:, t, 0:P], in_=taps[:, t, 0:P], compare_op=ALU.not_equal,
                                          fill=1.0, base=-t, pattern=[[1, P]], channel_multiplier=-1))
                g.step(pool.affine_select(out=taps[:, t, P:], in_=taps[:, t, P:], compare_op=ALU.not_equal,
                                          fill=1.0, base=KTAP - 1 - t, pattern=[[-1, KTAP - 1]],
                                          channel_multiplier=1))
            g.step(pool.iota(expo[:, 0, :], pattern=[[SUB, NSUB + 1]], base=0, channel_multiplier=-1))
            g.step(pool.iota(expo[:, 1, 0:NSUB], pattern=[[-SUB, NSUB]], base=0, channel_multiplier=1))
            g.step(pool.iota(expo[:, 1, NSUB:], pattern=[[0, 1]], base=0, channel_multiplier=1))
            g.step(pool.memset(coef[:], 1.0))
            g.step(pool.affine_select(out=coef[:], in_=coef[:], compare_op=ALU.is_ge, fill=0.0,
                                      base=64 + R - 1, pattern=[[0, 1]], channel_multiplier=-1))
            g.step(pool.memset(kcat[:], 0.0))
            g.step(pool.memset(qcat[:], 0.0))
            g.step(pool.affine_select(out=kcat[:, :, 5, 0:KTAP - 1], in_=kcat[:, :, 5, 0:KTAP - 1],
                                      compare_op=ALU.not_equal, fill=1.0, base=-(P - KTAP + 1),
                                      pattern=[[0, NT], [-1, KTAP - 1]], channel_multiplier=1))
            g.step(pool.memset(ones[:], 1.0))
            pool.memset(S[:], 0.0).then_inc(consts, 1)
            pool.wait_ge(gammas, 4)
            g.step(pool.affine_select(out=kw[:, 0:NSUB, :], in_=kw[:, 0:NSUB, :], compare_op=ALU.is_ge, fill=0.0,
                                      base=SUB - 1, pattern=[[SUB, NSUB], [0, R]], channel_multiplier=-1))
            g.step(pool.affine_select(out=qw[:, 0:NSUB, :], in_=qw[:, 0:NSUB, :], compare_op=ALU.is_ge, fill=0.0,
                                      base=SUB - 1, pattern=[[SUB, NSUB], [0, R]], channel_multiplier=-1))
            pool.affine_select(out=qw[:, 0:NSUB, :], in_=qw[:, 0:NSUB, :], compare_op=ALU.is_ge, fill=0.0,
                               base=0, pattern=[[-SUB, NSUB], [0, R]], channel_multiplier=1).then_inc(masked, 1)
            pool.wait_ge(ld_w, 16 * 9)
            pool.wait_ge(ld_x, 16)
            for t in range(NT):
                pool.tensor_tensor(h2[:, t], x[:, t], rows[:, 1], ALU.add).then_inc(xb_ok, 1)
            for t in range(NT):
                pool.wait_ge(h2_sb, t + 1)
                g.step(pool.tensor_tensor(hn[:, t], h2[:, t], x[:, t], ALU.add))
                pool.tensor_tensor(hn[:, t], hn[:, t], rows[:, 2], ALU.add).then_inc(res_ok, 1)

        @block.scalar
        def _(act):
            act.dma_start(xT[:], io["xT"].rearrange("(c p) t -> p c t", p=P)).then_inc(ld_xT, 16)
            act.dma_start(cols[:], io["a_cols"]).then_inc(ld_xT, 16)
            act.dma_start(uv[:, :, 0:R], io["u"].rearrange("(c p) r -> p c r", p=P)).then_inc(ld_xT, 16)
            act.dma_start(uv[:, :, R:], io["v"].rearrange("(c p) r -> p c r", p=P)).then_inc(ld_xT, 16)
            for i, name in enumerate(("norm1_w", "proj_b", "mlp_b2")):
                act.dma_start(rows[:, i], io[name].partition_broadcast(P)).then_inc(ld_w, 16)
            act.wait_ge(zeroed, 1)
            act.dma_start(sg[:, 0:R], io["decay"].partition_broadcast(P)).then_inc(ld_w, 16)
            act.dma_start(sg[:, R:2 * R], io["alpha"].partition_broadcast(P)).then_inc(ld_w, 16)
            act.dma_start(sg[64:64 + R, 2 * R:2 * R + 1], io["decay"].unsqueeze(1)).then_inc(ld_w, 16)
            act.dma_start(sg[:, 2 * R + 1:], io["gate"].partition_broadcast(P)).then_inc(ld_w, 16)
            act.dma_start(traw[:], io["taps"].partition_broadcast(P)).then_inc(ld_w, 16)
            act.dma_start(projT[:], io["projT"].rearrange("(c p) f -> p c f", p=P)).then_inc(ld_w, 16)
            act.wait_ge(ld_x, 16)
            for t in range(NT):
                if t >= 2:
                    act.wait_ge(squares, t - 1)
                act.activation(junk[:, t % 2], x[:, t], ACT.Square, accum_out=ss[:, t:t + 1]).then_inc(squares, 1)
            act.wait_ge(ld_w, 16 * 9)
            act.activation(sg[:], sg[:], ACT.Exp, scale=-1.0).then_inc(gammas, 1)
            act.wait_ge(expos, 1)
            act.activation(lg[:], lg[:], ACT.Ln).then_inc(gammas, 1)
            act.wait_ge(coef_ok, 1)
            act.activation(kw[:], kw[:], ACT.Exp).then_inc(gammas, 1)
            act.activation(qw[:], qw[:], ACT.Exp).then_inc(gammas, 1)
            act.activation(lg[:, R:], lg[:, R:], ACT.Exp, scale=float(P)).then_inc(gammas, 1)
            act.wait_ge(ld_mlp, 32)
            act.activation(w1_hi[:].rearrange("p c f -> p (c f)"), w1_32[:], ACT.Copy).then_inc(hi_w, 1)
            act.activation(w2_hi[:].rearrange("p c f -> p (c f)"), w2_32, ACT.Copy).then_inc(hi_w, 1)
            for t in range(NT + 2):
                if t < NT:
                    act.wait_ge(turned, t + 1)
                    if t >= 3:
                        act.wait_ge(o_mm, t - 2)
                    act.activation(qkT[:, t % 3], bank[t % 2][0:96, 0:2 * P], ACT.Copy).then_inc(turned_sb, 1)
                if t >= 2:
                    act.wait_ge(o_mm, t - 1)
                    act.activation(oT[:, :, tile(t - 2)], bank[4 + t % 2][:, 0:2 * P].rearrange("p (c t) -> p c t", c=DH),
                                   ACT.Copy).then_inc(o_sb, 1)
            for t in range(NT):
                act.wait_ge(h2_sb, t + 1)
                act.wait_ge(squares, NT + t - 1)
                act.activation(junk[:, t % 2], h2[:, t], ACT.Square, accum_out=ss[:, t:t + 1]).then_inc(squares, 1)

            def high_part(c):
                for h in range(DH):
                    act.wait_ge(hT_mm, DH * c + h + 1)
                    act.activation(hT_hi[:, h, chunk(c % 3)], bank[2 + (c % 2) * 2 + h][:], ACT.Copy,
                                   scale=cols[:, 2 + h:3 + h]).then_inc(hT_hi_ok, 1)

            high_part(0)
            high_part(1)
            for c in range(NC):
                for f in range(FT):
                    n = c * FT + f
                    act.wait_ge(up_mm, n + 1)
                    if n >= 2:
                        act.wait_ge(g_ok, n - 1)
                    act.activation(g32[:, f % 2], bank[6 + f % 2][:], ACT.Gelu_apprx_tanh,
                                   bias=cols[:, 4 + f:5 + f]).then_inc(gelu_ok, 1)
                    if f == 3 and c + 2 < NC:
                        high_part(c + 2)
            for c in range(NC):
                for h in range(DH):
                    act.wait_ge(x1_mm, DH * c + h + 1)
                    act.activation(sT[:, h, chunk(c)], bank[2 + (c % 2) * 2 + h][:], ACT.Copy).then_inc(x1_sb, 1)

        def low_part(v, c):
            for h in range(DH):
                v.wait_ge(hT_hi_ok, DH * c + h + 1)
                v.scalar_tensor_tensor(out=hT_lo[:, h, chunk(c % 3)], in0=bank[2 + (c % 2) * 2 + h][:],
                                       scalar=cols[:, 2 + h:3 + h], in1=hT_hi[:, h, chunk(c % 3)].bitcast(F32),
                                       op0=ALU.mult, op1=ALU.subtract).then_inc(hT_lo_ok, 1)

        @block.vector
        def _(v):
            k = Chain(v, vchain)
            v.memset(sg[:], 0.0).then_inc(zeroed, 1)
            v.wait_ge(ld_xT, 64)
            for h in range(DH):
                v.tensor_scalar(uv[:, h], uv[:, h], cols[:, h:h + 1], None, ALU.mult).then_inc(uv_ok, 1)
            v.wait_ge(squares, NT)
            k.step(v.tensor_scalar(ss[:], ss[:], 1.0 / D, EPS_RMS, ALU.mult, ALU.add))
            rsqrt_steps(v, k, rs[:], ss[:], tmp[:, 0:NT])
            v.wait_ge(ld_w, 16 * 9)
            for t in range(NT):
                v.scalar_tensor_tensor(out=hn[:, t], in0=x[:, t], scalar=rs[:, t:t + 1], in1=rows[:, 0],
                                       op0=ALU.mult, op1=ALU.mult).then_inc(hn_ok, 1)
            v.wait_ge(gammas, 1)
            k.step(v.tensor_scalar(sg[:], sg[:], 1.0, None, ALU.add))
            k.step(v.reciprocal(sg[:], sg[:]))
            k.step(v.tensor_scalar(lg[:, 0:R], sg[:, 0:R], 0.15, 1.0, ALU.max, ALU.min))
            v.tensor_scalar(lg[:, R:], sg[:, 2 * R:2 * R + 1], 0.15, 1.0, ALU.max, ALU.min).then_inc(expos, 1)
            v.wait_ge(consts, 1)
            k.step(v.tensor_copy(expf[:], expo[:]))
            k.step(v.tensor_scalar(expf[:], expf[:], 1.0 - SUB, None, ALU.max))
            v.wait_ge(gammas, 2)
            k.step(v.tensor_tensor(kw[:], bc(expf[:, 0], 2, R), bc(lg[:, 0:R], 1, NSUB + 1), ALU.mult))
            v.tensor_tensor(qw[:], bc(expf[:, 1], 2, R), bc(lg[:, 0:R], 1, NSUB + 1), ALU.mult).then_inc(coef_ok, 1)
            k.step(v.tensor_scalar(gk[:], traw[:], sg[:, 2 * R + 1:], None, ALU.mult))
            k.step(v.tensor_scalar(band[:], taps[:, 0], gk[:, 0:1], None, ALU.mult))
            for t in range(1, KTAP):
                k.step(v.scalar_tensor_tensor(out=band[:], in0=taps[:, t], scalar=gk[:, t:t + 1], in1=band[:],
                                              op0=ALU.mult, op1=ALU.add))
            k.step(v.tensor_copy(qcat[:, :, 5, 0:KTAP - 1], bc(band[:, P:], 1, NT)))
            v.wait_ge(gammas, 5)
            k.step(v.tensor_tensor(coef[:], coef[:], lg[:, R:], ALU.mult))
            v.wait_ge(masked, 1)
            k.step(v.tensor_tensor(qw[:], qw[:], bc(sg[:, R:2 * R], 1, NSUB + 1), ALU.mult))
            v.wait_ge(qk_mm, 1)
            k.step(v.tensor_tensor(qk[:].rearrange("p t a r -> p t (a r)"),
                                   bank[7][:].rearrange("p (t n) -> p t n", t=NT), bc(rs[:], 2, 2 * R), ALU.mult))
            k.step(v.tensor_tensor(qk_sq, qk[:], qk[:], ALU.mult))
            k.step(v.tensor_reduce(qkn[:], qk_sq.rearrange("p t a r -> p (t a) r"), AX_X, ALU.add))
            k.step(v.tensor_scalar(qkn[:], qkn[:], 1e-16, None, ALU.max))
            rsqrt_steps(v, k, qkr[:], qkn[:], tmp[:])
            k.step(v.tensor_tensor(qk[:].rearrange("p t a r -> p (t a) r"), qk[:].rearrange("p t a r -> p (t a) r"),
                                   bc(qkr[:], 2, R), ALU.mult))
            k.step(v.tensor_tensor(kcat[:, :, 0:NSUB + 1, :], bc(qk[:, :, 1], 2, NSUB + 1), bc(kw[:], 1, NT), ALU.mult))
            v.tensor_tensor(qcat[:, :, 0:NSUB + 1, :], bc(qk[:, :, 0], 2, NSUB + 1), bc(qw[:], 1, NT),
                            ALU.mult).then_inc(cats, 1)
            for t in range(NT + 1):
                if t < NT:
                    v.wait_ge(S_mm, t + 1)
                    if t >= 3:
                        v.wait_ge(o_mm, t - 2)
                    if t >= 1:
                        v.wait_ge(S_sb, t)
                    v.scalar_tensor_tensor(out=S[64:64 + R + KTAP - 1, (t + 1) % 4], in0=S[64:64 + R + KTAP - 1, t % 4],
                                           scalar=coef[64:64 + R + KTAP - 1, 0:1],
                                           in1=bank[6 + t % 2][64:64 + R + KTAP - 1, 0:D],
                                           op0=ALU.mult, op1=ALU.add).then_inc(S_sb, 1)
                if t >= 1:
                    v.wait_ge(A_mm, t)
                    if t >= 3:
                        v.wait_ge(o_mm, t - 2)
                    k.step(v.tensor_tensor(AT[:, (t - 1) % 2], bank[2 + (t - 1) % 2][:, 0:P], later[:], ALU.mult))
                    v.tensor_tensor(AT[:, (t - 1) % 2], AT[:, (t - 1) % 2], band[:, 0:P], ALU.add).then_inc(A_sb, 1)
            v.wait_ge(hi_w, 2)
            v.tensor_tensor(w1_lo[:].rearrange("p c f -> p (c f)"), w1_32[:],
                            w1_hi[:].bitcast(F32).rearrange("p c f -> p (c f)"), ALU.subtract).then_inc(w_lo_ok, 1)
            v.tensor_tensor(w2_lo[:].rearrange("p c f -> p (c f)"), w2_32,
                            w2_hi[:].bitcast(F32).rearrange("p c f -> p (c f)"), ALU.subtract).then_inc(w_lo_ok, 1)
            for c in range(NC):
                for t in range(c * TPC, (c + 1) * TPC):
                    v.wait_ge(h2_mm, t + 1)
                    v.wait_ge(xb_ok, t + 1)
                    v.tensor_tensor(h2[:, t], bank[t % 2][:, 0:D], h2[:, t], ALU.add).then_inc(h2_sb, 1)
            for c in range(NC):
                sl = slice(c * TPC, (c + 1) * TPC)
                v.wait_ge(squares, NT + (c + 1) * TPC)
                k.step(v.tensor_scalar(ss[:, sl], ss[:, sl], 1.0 / D, EPS_RMS, ALU.mult, ALU.add))
                rsqrt_steps(v, k, rs[:, sl], ss[:, sl], tmp[:, 0:TPC])
                if c >= 2:
                    v.wait_ge(hT_mm, DH * (c - 1))
                for j in range(TPC):
                    t = c * TPC + j
                    v.tensor_scalar(n2[:, c % 2, j], h2[:, t], rs[:, t:t + 1], None, ALU.mult).then_inc(n2_ok, 1)
                if 1 <= c <= 2:
                    low_part(v, c - 1)
            for c in range(NC):
                for f in range(FT):
                    n = c * FT + f
                    v.wait_ge(gelu_ok, n + 1)
                    if c >= 1:
                        v.wait_ge(y_mm, TPC * c)
                    k.step(v.tensor_copy(g_hi[:, f], g32[:, f % 2]))
                    v.tensor_tensor(g_lo[:, f], g32[:, f % 2], g_hi[:, f].bitcast(F32), ALU.subtract).then_inc(g_ok, 1)
                    if f == 4 and c + 2 < NC:
                        low_part(v, c + 2)
                for t in range(c * TPC, (c + 1) * TPC):
                    v.wait_ge(y_mm, t + 1)
                    v.wait_ge(res_ok, t + 1)
                    v.tensor_tensor(hn[:, t], bank[t % 2][:, 0:D], hn[:, t], ALU.add).then_inc(z_ok, 1)
                    v.wait_ge(z_ok, t + 1)
                    k.step(v.bn_stats(stats[:, t], hn[:, t]))
                    k.step(v.bn_aggr(mv[:, t], stats[:, t]))
                sl = slice(c * TPC, (c + 1) * TPC)
                k.step(v.tensor_scalar(ss[:, sl], mv[:, sl, 1], EPS_LN, None, ALU.add))
                rsqrt_steps(v, k, rs[:, sl], ss[:, sl], tmp[:, 0:TPC])
                for t in range(c * TPC, (c + 1) * TPC):
                    last = v.tensor_scalar(h2[:, t], hn[:, t], mv[:, t, 0:1], rs[:, t:t + 1], ALU.subtract, ALU.mult)
                last.then_inc(x1_ok, 1)

        @block.tensor
        def _(pe):
            pe.wait_ge(ld_xT, 64)
            pe.wait_ge(uv_ok, 2)
            for t in range(NT):
                for h in range(DH):
                    last = pe.matmul(bank[7][:, t * 2 * R:(t + 1) * 2 * R], xT[:, h, tile(t)], uv[:, h],
                                     start=(h == 0), stop=(h == DH - 1))
            last.then_inc(qk_mm, 1)
            pe.wait_ge(consts, 1)
            pe.wait_ge(cats, 1)
            for t in range(NT + 2):
                if t < NT:
                    if t >= 2:
                        pe.wait_ge(turned_sb, t - 1)
                    pe.transpose(bank[t % 2][0:96, 0:P], qcat[:, t].rearrange("p s r -> p (s r)"), ident[:])
                    pe.transpose(bank[t % 2][0:96, P:2 * P], kcat[:, t].rearrange("p s r -> p (s r)"),
                                 ident[:]).then_inc(turned, 1)
                    pe.wait_ge(hn_ok, t + 1)
                    if t >= 2:
                        pe.wait_ge(S_sb, t - 1)
                    pe.matmul(bank[6 + t % 2][64:64 + R + KTAP - 1, 0:D],
                              kcat[:, t].rearrange("p s r -> p (s r)")[:, 64:64 + R + KTAP - 1], hn[:, t],
                              start=True, stop=True).then_inc(S_mm, 1)
                if 1 <= t <= NT:
                    pe.wait_ge(turned_sb, t)
                    if t >= 3:
                        pe.wait_ge(A_sb, t - 2)
                    u = (t - 1) % 3
                    pe.matmul(bank[2 + (t - 1) % 2][:, 0:P], qkT[0:64, u, P:2 * P], qkT[0:64, u, 0:P],
                              start=True, stop=True).then_inc(A_mm, 1)
                if t >= 2:
                    u = t - 2
                    pe.wait_ge(A_sb, u + 1)
                    if u >= 1:
                        pe.wait_ge(S_sb, u)
                    if u >= 2:
                        pe.wait_ge(o_sb, u - 1)
                    for h in range(DH):
                        out = bank[4 + u % 2][:, h * P:(h + 1) * P]
                        pe.matmul(out, hn[:, u, h * P:(h + 1) * P], AT[:, u % 2], start=True, stop=False)
                        last = pe.matmul(out, S[64:64 + R + KTAP - 1, u % 4, h * P:(h + 1) * P],
                                         qkT[64:64 + R + KTAP - 1, u % 3, 0:P], start=False, stop=True)
                    last.then_inc(o_mm, 1)
            for t in range(NT):
                pe.wait_ge(o_sb, t + 1)
                if t >= 2:
                    pe.wait_ge(h2_sb, t - 1)
                for h in range(DH):
                    last = pe.matmul(bank[t % 2][:, 0:D], oT[:, h, tile(t)], projT[:, h], start=(h == 0), stop=(h == DH - 1))
                last.then_inc(h2_mm, 1)

            def turn_n2(c):
                if c >= 2:
                    pe.wait_ge(hT_lo_ok, DH * (c - 1))
                pe.wait_ge(n2_ok, (c + 1) * TPC)
                for h in range(DH):
                    for j in range(TPC):
                        last = pe.transpose(bank[2 + (c % 2) * 2 + h][:, j * P:(j + 1) * P],
                                            n2[:, c % 2, j, h * P:(h + 1) * P], ident[:])
                    last.then_inc(hT_mm, 1)

            def turn_x1(c):
                if c >= 2:
                    pe.wait_ge(x1_sb, DH * (c - 1))
                pe.wait_ge(x1_ok, c + 1)
                for h in range(DH):
                    for j in range(TPC):
                        last = pe.transpose(bank[2 + (c % 2) * 2 + h][:, j * P:(j + 1) * P],
                                            h2[:, c * TPC + j, h * P:(h + 1) * P], ident[:])
                    last.then_inc(x1_mm, 1)

            turn_n2(0)
            turn_n2(1)
            pe.wait_ge(w_lo_ok, 2)
            for c in range(NC):
                pe.wait_ge(hT_lo_ok, DH * (c + 1))
                for f in range(FT):
                    n = c * FT + f
                    if n >= 2:
                        pe.wait_ge(gelu_ok, n - 1)
                    fs = slice(f * P, (f + 1) * P)
                    for h in range(DH):
                        last = three_pass(pe, bank[6 + f % 2][:], w1_hi[:, h, fs], w1_lo[:, h, fs],
                                          hT_hi[:, h, chunk(c % 3)], hT_lo[:, h, chunk(c % 3)], h == 0, h == DH - 1)
                    last.then_inc(up_mm, 1)
                    if f == 1 and c + 2 < NC:
                        turn_n2(c + 2)
                for j in range(TPC):
                    t = c * TPC + j
                    if t >= 2:
                        pe.wait_ge(z_ok, t - 1)
                    for f in range(FT):
                        pe.wait_ge(g_ok, c * FT + f + 1)
                        last = three_pass(pe, bank[t % 2][:, 0:D], g_hi[:, f, j * P:(j + 1) * P], g_lo[:, f, j * P:(j + 1) * P],
                                          w2_hi[:, f], w2_lo[:, f], f == 0, f == FT - 1)
                    last.then_inc(y_mm, 1)
            for c in range(NC):
                turn_x1(c)


def cross_attention(nc, io, shared):
    ident, ones, sT = shared["ident"], shared["ones"], shared["sT"]
    HALF = T // 2
    G = 3 * D
    FIRST_STEPS = (NC - 1) * (1 + RSQRT_STEPS)
    V_STEPS, v_steps = NC * (1 + RSQRT_STEPS) + MT * (NC + 2) + 2 + NC * DH * 2, []
    with ExitStack() as ctx:
        def sb(name, shape, dt=F32, stack=ctx):
            return stack.enter_context(nc.sbuf_tensor(name, shape, dt))

        def sem(name, stack=ctx):
            return stack.enter_context(nc.semaphore("x_" + name))

        psum = ctx.enter_context(nc.psum_tensor("x_psum", [P, 8, CH], F32))
        bank = [psum[:, i] for i in range(8)]

        kq_hi = sb("x_kq_hi", [P, DH, M], F32R)
        kq_lo = sb("x_kq_lo", [P, DH, M], F32R)
        v_hi = sb("x_v_hi", [P, MT, D], F32R)
        v_lo = sb("x_v_lo", [P, MT, D], F32R)
        wi_hi = sb("x_wi_hi", [P, DH, G], F32R)
        wi_lo = sb("x_wi_lo", [P, DH, G], F32R)
        wh_hi = sb("x_wh_hi", [P, DH, G], F32R)
        wh_lo = sb("x_wh_lo", [P, DH, G], F32R)
        rs16 = sb("x_rs16", [P, MT])
        bias = sb("x_bias", [P, 4 * DH])

        def hs(h):
            return slice(h * P, (h + 1) * P)

        def chunk(c):
            return slice(c * CH, (c + 1) * CH)

        with ExitStack() as pre:
            prepare_context(nc, io, pre, bank, dict(kq_hi=kq_hi, kq_lo=kq_lo, v_hi=v_hi, v_lo=v_lo, wi_hi=wi_hi,
                                                    wi_lo=wi_lo, wh_hi=wh_hi, wh_lo=wh_lo, rs16=rs16, bias=bias))

        sn_hi = sb("x_sn_hi", [P, DH, T], F32R)
        sn_lo = sb("x_sn_lo", [P, DH, T], F32R)
        E = sb("x_E", [P, MT, HALF])
        e = sb("x_e", [P, 2, HALF])
        p_hi = sb("x_p_hi", [P, 2, HALF], F32R)
        p_lo = sb("x_p_lo", [P, 2, HALF], F32R)
        acc = sb("x_acc", [P, T])
        diag = sb("x_diag", [P, 2, CH])
        st = sb("x_st", [P, 3, NT])
        rw = sb("x_rw", [P, NT])
        mx = sb("x_mx", [P, 2, NC + 2])
        inv = sb("x_inv", [P, MT, 3])
        room = E[:].rearrange("p m (a n) -> p (m a) n", n=CH)
        gates = [room[:, 4 + 4 * i:8 + 4 * i] for i in range(2)]
        sq = [room[:, 12 + DH * i:12 + DH * (i + 1)] for i in range(2)]
        u32 = [room[:, 16 + DH * i:16 + DH * (i + 1)] for i in range(2)]
        U = [e[:, c].rearrange("p (h n) -> p h n", h=DH) for c in range(2)] + [room[:, DH * c:DH * (c + 1)] for c in range(2)]
        u_hi = [p_hi[:, i].rearrange("p (h n) -> p h n", h=DH) for i in range(2)]
        u_lo = [p_lo[:, i].rearrange("p (h n) -> p h n", h=DH) for i in range(2)]

        (sq_ok, sum_ok, stat_mm, diag_ok, bc_mm, prod_ok, sn_hi_ok, sn_lo_ok) = (
            sem(n) for n in ("sq_ok", "sum_ok", "stat_mm", "diag_ok", "bc_mm", "prod_ok", "sn_hi_ok", "sn_lo_ok"))
        (score_mm, neg_ok, exp_ok, inv_ok, p_hi_ok, p_lo_ok, acc_ok, upd_mm) = (
            sem(n) for n in ("score_mm", "neg_ok", "exp_ok", "inv_ok", "p_hi_ok", "p_lo_ok", "acc_ok", "upd_mm"))
        (U_ok, s_hi_ok, s_lo_ok, row_mm, rdiag_ok, rbc_mm, u_ok, u_hi_ok, u_lo_ok) = (
            sem(n) for n in ("U_ok", "s_hi_ok", "s_lo_ok", "row_mm", "rdiag_ok", "rbc_mm", "u_ok", "u_hi_ok", "u_lo_ok"))
        (r_mm, z_mm, hn_mm, in_mm, r_ok, z_ok, hr_ok, arg_ok, n_ok, s_ok, vchain) = (
            sem(n) for n in ("r_mm", "z_mm", "hn_mm", "in_mm", "r_ok", "z_ok", "hr_ok", "arg_ok", "n_ok", "s_ok", "vchain"))

        GH = NC * DH
        Q = 2 * MT
        block = ctx.enter_context(nc.Block())

        @block.scalar
        def _(act):
            def squares(g, c, first=False):
                if not (first and c < 2):
                    act.wait_ge(stat_mm, g - 1)
                act.activation(sq[c % 2], sT[:, :, chunk(c)], ACT.Square).then_inc(sq_ok, 1)

            def normed_hi(g, c):
                act.wait_ge(prod_ok, g + 1)
                act.activation(sn_hi[:, :, chunk(c)], u32[c % 2], ACT.Copy).then_inc(sn_hi_ok, 1)

            squares(0, 0, first=True)
            squares(1, 1, first=True)
            for c in range(NC - 1):
                normed_hi(c, c)
                if c + 2 < NC - 1:
                    squares(c + 2, c + 2)
            with act.Fori(0, ITERS) as it:
                def weights_hi(q):
                    m = q % MT
                    n = MROWS[m]
                    src = e[0:n, m % 2] if q < MT else E[0:n, m]
                    if q >= 2:
                        act.wait_ge(upd_mm, it * Q + q - 1)
                    act.activation(p_hi[0:n, q % 2], src, ACT.Copy, scale=inv[0:n, m, 2:3]).then_inc(p_hi_ok, 1)

                def slots_hi(c):
                    act.activation(sn_hi[:, :, chunk(c)], sT[:, :, chunk(c)], ACT.Copy).then_inc(s_hi_ok, 1)

                def take_updates(c):
                    b = 4 + DH * c if c < 2 else DH * (c - 2)
                    act.activation(U[c], psum[:, b:b + DH], ACT.Copy).then_inc(U_ok, 1)

                def updates_hi(c):
                    act.wait_ge(u_ok, it * NC + c + 1)
                    if c >= 2:
                        act.wait_ge(in_mm, it * GH + DH * (c - 1))
                    act.activation(u_hi[c % 2], U[c], ACT.Copy).then_inc(u_hi_ok, 1)

                act.wait_ge(s_ok, it * GH + 1)
                squares(it * NC + NC - 1, NC - 1)
                normed_hi(it * NC + NC - 1, NC - 1)
                for m in range(MT):
                    n = MROWS[m]
                    act.wait_ge(neg_ok, it * MT + m + 1)
                    if m == 0:
                        act.wait_ge(sn_lo_ok, it * NC + NC)
                    for half in range(2):
                        if half == 0 and m >= 2:
                            act.wait_ge(acc_ok, it * MT * NC + (m - 2) * NC + 2)
                            act.wait_ge(p_lo_ok, it * Q + m - 1)
                        out = e[0:n, m % 2] if half == 0 else E[0:n, m]
                        act.activation(out, psum[0:n, 2 * half:2 * half + 2].rearrange("p a n -> p (a n)"), ACT.Exp,
                                       bias=inv[0:n, m, 0:1], scale=rs16[0:n, m:m + 1],
                                       accum_out=mx[0:n, m % 2, NC + half:NC + half + 1]).then_inc(exp_ok, 1)
                    act.wait_ge(inv_ok, it * MT + m + 1)
                    weights_hi(m)
                for m in range(MT):
                    weights_hi(MT + m)
                    if m == 0:
                        act.wait_ge(upd_mm, it * Q + MT)
                        act.wait_ge(acc_ok, (it + 1) * MT * NC)
                        act.wait_ge(p_lo_ok, it * Q + MT)
                    if m < 2:
                        take_updates(m)
                    elif m < 2 + NC:
                        slots_hi(m - 2)
                act.wait_ge(upd_mm, (it + 1) * Q)
                act.wait_ge(p_lo_ok, (it + 1) * Q)
                take_updates(2)
                take_updates(3)
                updates_hi(0)
                for c in range(NC):
                    after = (it + 1) * NC + c - 1
                    if c + 1 < NC:
                        updates_hi(c + 1)
                    if c >= 1:
                        act.wait_ge(s_ok, it * GH + DH * c + 1)
                        squares(after, c - 1)
                    for h in range(DH):
                        i = c * DH + h
                        r, z, arg, new = (gates[i % 2][:, j] for j in range(4))
                        act.wait_ge(r_mm, it * GH + i + 1)
                        if i >= 2:
                            act.wait_ge(s_ok, it * GH + i)
                        act.activation(r, bank[1], ACT.Sigmoid, bias=bias[:, h:h + 1]).then_inc(r_ok, 1)
                        if c >= 1 and h == 1:
                            normed_hi(after, c - 1)
                        act.wait_ge(z_mm, it * GH + i + 1)
                        act.activation(z, bank[2], ACT.Sigmoid, bias=bias[:, DH + h:DH + h + 1]).then_inc(z_ok, 1)
                        act.wait_ge(arg_ok, it * GH + i + 1)
                        act.activation(new, arg, ACT.Tanh, bias=bias[:, 2 * DH + h:2 * DH + h + 1]).then_inc(n_ok, 1)

        @block.vector
        def _(v):
            v.memset(st[:], 0.0).then_inc(s_ok, 1)
            v.wait_ge(s_ok, 1)

            def factors(values, slot, counted, tiles):
                for j, t in enumerate(tiles):
                    last = v.tensor_scalar(diag[:, slot, j * P:(j + 1) * P], ident[:], values[:, t:t + 1], None, ALU.mult)
                last.then_inc(counted, 1)

            def rms(k, g, c, first=False):
                tiles = slice(c * TPC, (c + 1) * TPC)
                v.wait_ge(stat_mm, g + 1)
                k.step(v.tensor_scalar(st[:, 0, tiles], bank[4 + c % 2][:, 0:TPC], 1.0 / D, EPS_RMS, ALU.mult, ALU.add))
                rsqrt_steps(v, k, st[:, 1, tiles], st[:, 0, tiles], st[:, 2, tiles])
                if not (first and c < 2):
                    v.wait_ge(bc_mm, g - 1)
                factors(st[:, 1], c % 2, diag_ok, range(c * TPC, (c + 1) * TPC))

            def normed(g, c, first=False):
                v.wait_ge(bc_mm, g + 1)
                if not (first and c < 2):
                    v.wait_ge(sn_hi_ok, g - 1)
                    v.wait_ge(sn_lo_ok, g - 1)
                v.tensor_tensor(u32[c % 2], sT[:, :, chunk(c)], bc(bank[6 + c % 2], 1, DH), ALU.mult).then_inc(prod_ok, 1)

            def normed_lo(g, c):
                v.wait_ge(sn_hi_ok, g + 1)
                v.tensor_tensor(sn_lo[:, :, chunk(c)], u32[c % 2], sn_hi[:, :, chunk(c)].bitcast(F32),
                                ALU.subtract).then_inc(sn_lo_ok, 1)

            k = Chain(v, vchain)
            for c in range(NC):
                if c < NC - 1:
                    rms(k, c, c, first=True)
                if c >= 1:
                    normed(c - 1, c - 1, first=True)
                    normed_lo(c - 1, c - 1)
            assert k.n == FIRST_STEPS

            with v.Fori(0, ITERS) as it:
                k = Chain(v, vchain, it * V_STEPS + FIRST_STEPS)

                def add_weights(m, c):
                    n = MROWS[m]
                    src = e[0:n, m % 2, chunk(c)] if c < 2 else E[0:n, m, chunk(c - 2)]
                    if m == 0:
                        v.tensor_scalar(acc[0:n, chunk(c)], src, inv[0:n, m, 2:3], None, ALU.mult).then_inc(acc_ok, 1)
                    else:
                        v.wait_ge(acc_ok, it * MT * NC + (m - 1) * NC + c + 1)
                        v.scalar_tensor_tensor(out=acc[0:n, chunk(c)], in0=src, scalar=inv[0:n, m, 2:3],
                                               in1=acc[0:n, chunk(c)], op0=ALU.mult, op1=ALU.add).then_inc(acc_ok, 1)

                def weights_lo(q):
                    m = q % MT
                    n = MROWS[m]
                    src = e[0:n, m % 2] if q < MT else E[0:n, m]
                    v.wait_ge(p_hi_ok, it * Q + q + 1)
                    if q >= 2:
                        v.wait_ge(upd_mm, it * Q + q - 1)
                    v.scalar_tensor_tensor(out=p_lo[0:n, q % 2], in0=src, scalar=inv[0:n, m, 2:3],
                                           in1=p_hi[0:n, q % 2].bitcast(F32), op0=ALU.mult,
                                           op1=ALU.subtract).then_inc(p_lo_ok, 1)

                rms(k, it * NC + NC - 1, NC - 1)
                for m in range(MT):
                    n = MROWS[m]
                    for c in range(NC):
                        if m == 0 and c == 1:
                            normed(it * NC + NC - 1, NC - 1)
                        if m == 0 and c == 2:
                            normed_lo(it * NC + NC - 1, NC - 1)
                        v.wait_ge(score_mm, it * MT * NC + m * NC + c + 1)
                        mark = k.mark(v.tensor_reduce(mx[0:n, m % 2, c:c + 1], bank[c][0:n], AX_X, ALU.max))
                    v.wait_ge(vchain, mark)
                    k.step(v.tensor_reduce(inv[0:n, m, 0:1], mx[0:n, m % 2, 0:NC], AX_X, ALU.max))
                    v.tensor_scalar(inv[0:n, m, 0:1], inv[0:n, m, 0:1], rs16[0:n, m:m + 1], -1.0,
                                    ALU.mult, ALU.mult).then_inc(neg_ok, 1)
                    if m >= 1:
                        for c in range(NC - 1):
                            add_weights(m - 1, c)
                    v.wait_ge(exp_ok, it * Q + 2 * m + 2)
                    k.step(v.tensor_tensor(inv[0:n, m, 1:2], mx[0:n, m % 2, NC:NC + 1], mx[0:n, m % 2, NC + 1:NC + 2], ALU.add))
                    v.reciprocal(inv[0:n, m, 2:3], inv[0:n, m, 1:2]).then_inc(inv_ok, 1)
                    if m >= 1:
                        add_weights(m - 1, NC - 1)
                    weights_lo(m)
                for c in range(NC):
                    add_weights(MT - 1, c)

                def norm_updates(c):
                    v.wait_ge(U_ok, it * NC + c + 1)
                    v.wait_ge(rbc_mm, it * NC + c + 1)
                    v.tensor_tensor(U[c], U[c], bc(bank[4 + c], 1, DH), ALU.mult).then_inc(u_ok, 1)

                def slots_lo(c):
                    v.wait_ge(s_hi_ok, it * NC + c + 1)
                    v.tensor_tensor(sn_lo[:, :, chunk(c)], sT[:, :, chunk(c)], sn_hi[:, :, chunk(c)].bitcast(F32),
                                    ALU.subtract).then_inc(s_lo_ok, 1)

                for m in range(MT):
                    weights_lo(MT + m)
                    if 2 <= m < 2 + NC:
                        slots_lo(m - 2)
                    if m == 6:
                        v.wait_ge(row_mm, it + 1)
                        k.step(v.tensor_scalar(rw[:], bank[4][:, 0:NT], EPS_RMS, None, ALU.add))
                        k.step(v.reciprocal(rw[:], rw[:]))
                        factors(rw, 0, rdiag_ok, range(0, TPC))
                    if m in (7, 10, 11):
                        c = {7: 1, 10: 2, 11: 3}[m]
                        if c >= 2:
                            v.wait_ge(rbc_mm, it * NC + c - 1)
                        factors(rw, c % 2, rdiag_ok, range(c * TPC, (c + 1) * TPC))
                    if m in (11, 12):
                        norm_updates(m - 11)

                def updates_lo(c):
                    v.wait_ge(u_hi_ok, it * NC + c + 1)
                    v.tensor_tensor(u_lo[c % 2], U[c], u_hi[c % 2].bitcast(F32), ALU.subtract).then_inc(u_lo_ok, 1)

                updates_lo(0)
                norm_updates(2)
                norm_updates(3)
                for c in range(NC):
                    after = (it + 1) * NC + c - 1
                    if c + 1 < NC:
                        updates_lo(c + 1)
                    for h in range(DH):
                        i = c * DH + h
                        r, z, arg, new = (gates[i % 2][:, j] for j in range(4))
                        s = sT[:, h, chunk(c)]
                        v.wait_ge(hn_mm, it * GH + i + 1)
                        v.wait_ge(r_ok, it * GH + i + 1)
                        v.scalar_tensor_tensor(out=arg, in0=bank[0], scalar=bias[:, 3 * DH + h:3 * DH + h + 1], in1=r,
                                               op0=ALU.add, op1=ALU.mult).then_inc(hr_ok, 1)
                        if c >= 1 and h == 1:
                            normed_lo(after, c - 1)
                        if c >= 1 and h == 0:
                            rms(k, after, c - 1)
                        v.wait_ge(hr_ok, it * GH + i + 1)
                        v.wait_ge(in_mm, it * GH + i + 1)
                        v.tensor_tensor(arg, arg, bank[3], ALU.add).then_inc(arg_ok, 1)
                        v.wait_ge(n_ok, it * GH + i + 1)
                        k.step(v.tensor_tensor(s, s, new, ALU.subtract))
                        k.step(v.tensor_tensor(s, s, z, ALU.mult))
                        v.tensor_tensor(s, s, new, ALU.add).then_inc(s_ok, 1)
                        if c >= 1 and h == 0:
                            normed(after, c - 1)
                v_steps.append(k.n)

        @block.gpsimd
        def _(pool):
            def add_squares(g, c):
                pool.wait_ge(sq_ok, g + 1)
                pool.tensor_tensor(sq[c % 2][:, 0], sq[c % 2][:, 0], sq[c % 2][:, 1], ALU.add).then_inc(sum_ok, 1)

            for c in range(NC - 1):
                add_squares(c, c)
            with pool.Fori(0, ITERS) as it:
                add_squares(it * NC + NC - 1, NC - 1)
                for c in range(NC - 1):
                    add_squares((it + 1) * NC + c, c)

        @block.tensor
        def _(pe):
            def square_sums(g, c, first=False):
                pe.wait_ge(sum_ok, g + 1)
                if not (first and c < 2):
                    pe.wait_ge(diag_ok, g - 1)
                for j in range(TPC):
                    last = pe.matmul(bank[4 + c % 2][:, j:j + 1], sq[c % 2][:, 0, j * P:(j + 1) * P], ones[:, 0:1],
                                     start=True, stop=True)
                last.then_inc(stat_mm, 1)

            def broadcast(g, c, first=False):
                pe.wait_ge(diag_ok, g + 1)
                if not (first and c < 2):
                    pe.wait_ge(prod_ok, g - 1)
                pe.matmul(bank[6 + c % 2], ones[:], diag[:, c % 2], start=True, stop=True).then_inc(bc_mm, 1)

            for c in range(NC):
                if c < NC - 1:
                    square_sums(c, c, first=True)
                if c >= 1:
                    broadcast(c - 1, c - 1, first=True)
            with pe.Fori(0, ITERS) as it:
                def update(q):
                    m = q % MT
                    n = MROWS[m]
                    pe.wait_ge(p_lo_ok, it * Q + q + 1)
                    for c in range(2):
                        for h in range(DH):
                            b = (4 if q < MT else 0) + DH * c + h
                            last = three_pass(pe, bank[b], v_hi[0:n, m, hs(h)], v_lo[0:n, m, hs(h)],
                                              p_hi[0:n, q % 2, chunk(c)], p_lo[0:n, q % 2, chunk(c)], m == 0, m == MT - 1)
                    last.then_inc(upd_mm, 1)

                for m in range(MT):
                    n = MROWS[m]
                    ks = slice(m * P, m * P + n)
                    for c in range(NC):
                        if m == 0:
                            if c == 1:
                                square_sums(it * NC + NC - 1, NC - 1)
                            if c == 2:
                                broadcast(it * NC + NC - 1, NC - 1)
                            pe.wait_ge(sn_lo_ok, it * NC + c + 1)
                        elif c % 2 == 0:
                            pe.wait_ge(exp_ok, it * Q + 2 * (m - 1) + c // 2 + 1)
                        for h in range(DH):
                            last = three_pass(pe, bank[c][0:n], kq_hi[:, h, ks], kq_lo[:, h, ks],
                                              sn_hi[:, h, chunk(c)], sn_lo[:, h, chunk(c)], h == 0, h == DH - 1)
                        last.then_inc(score_mm, 1)
                    if m >= 1:
                        update(m - 1)
                update(MT - 1)

                def row_broadcast(c):
                    pe.wait_ge(rdiag_ok, it * NC + c + 1)
                    pe.matmul(bank[4 + c], ones[:], diag[:, c % 2], start=True, stop=True).then_inc(rbc_mm, 1)

                for m in range(MT):
                    if m == 0:
                        pe.wait_ge(exp_ok, (it + 1) * Q)
                    update(MT + m)
                    if m == 4:
                        pe.wait_ge(acc_ok, (it + 1) * MT * NC)
                        pe.wait_ge(U_ok, it * NC + 2)
                        for t in range(NT):
                            last = pe.matmul(bank[4][:, t:t + 1], acc[:, t * P:(t + 1) * P], ones[:, 0:1], start=True, stop=True)
                        last.then_inc(row_mm, 1)
                    if m in (8, 9, 11, 12):
                        row_broadcast((8, 9, 11, 12).index(m))

                def gate(b, e_from, h, c, parts, counted):
                    cols = slice(e_from * D + h * P, e_from * D + (h + 1) * P)
                    slots = [(wh_hi, wh_lo, sn_hi[:, k, chunk(c)], sn_lo[:, k, chunk(c)], k) for k in range(DH)]
                    updates = [(wi_hi, wi_lo, u_hi[c % 2][:, k], u_lo[c % 2][:, k], k) for k in range(DH)]
                    steps = slots * ("s" in parts) + updates * ("u" in parts)
                    for i, (w_hi, w_lo, x_hi, x_lo, k) in enumerate(steps):
                        if x_hi is updates[0][2]:
                            pe.wait_ge(u_lo_ok, it * NC + c + 1)
                        last = three_pass(pe, bank[b], w_hi[:, k, cols], w_lo[:, k, cols], x_hi, x_lo,
                                          i == 0, i == len(steps) - 1)
                    last.then_inc(counted, 1)

                for c in range(NC):
                    after = (it + 1) * NC + c - 1
                    pe.wait_ge(s_lo_ok, it * NC + c + 1)
                    for h in range(DH):
                        i = c * DH + h
                        if i == 0:
                            pe.wait_ge(U_ok, (it + 1) * NC)
                        else:
                            pe.wait_ge(hr_ok, it * GH + i)
                        gate(0, 2, h, c, "s", hn_mm)
                        if i > 0:
                            pe.wait_ge(r_ok, it * GH + i)
                        gate(1, 0, h, c, "su", r_mm)
                        if c >= 1 and h == 1:
                            broadcast(after, c - 1)
                        if i > 0:
                            pe.wait_ge(z_ok, it * GH + i)
                        gate(2, 1, h, c, "su", z_mm)
                        if c >= 1 and h == 0:
                            square_sums(after, c - 1)
                        if i > 0:
                            pe.wait_ge(arg_ok, it * GH + i)
                        gate(3, 2, h, c, "u", in_mm)
                pe.wait_ge(z_ok, (it + 1) * GH)
                pe.wait_ge(arg_ok, (it + 1) * GH)

    assert v_steps == [V_STEPS], v_steps


def prepare_context(nc, io, ctx, bank, dest):
    kq_hi, kq_lo, v_hi, v_lo = (dest[n] for n in ("kq_hi", "kq_lo", "v_hi", "v_lo"))
    wi_hi, wi_lo, wh_hi, wh_lo, rs16, bias = (dest[n] for n in ("wi_hi", "wi_lo", "wh_hi", "wh_lo", "rs16", "bias"))
    G = 3 * D

    def sb(name, shape, dt=F32):
        return ctx.enter_context(nc.sbuf_tensor("y_" + name, shape, dt))

    def sem(name):
        return ctx.enter_context(nc.semaphore("y_" + name))

    cx = sb("cx", [P, MT, D])
    cxT = sb("cxT", [P, DH, M])
    v32 = sb("v32", [P, MT, D])
    wq, wk, wv = (sb(n, [P, DH, D]) for n in ("wq", "wk", "wv"))
    wiT = sb("wiT", [P, DH, G])
    whT = sb("whT", [P, DH, G])
    wkq = sb("wkq", [P, DH, D])
    cols = sb("cols", [P, 2 * DH])
    bi = sb("bi", [P, 2 * 3 * DH])
    junk = sb("junk", [P, 2, D])
    ss, rs, tmp = sb("ss", [P, MT]), sb("rs", [P, MT]), sb("tmp", [P, MT])
    ld_w, ld_c, ld_cT, ld_g, zeroed = sem("ld_w"), sem("ld_c"), sem("ld_cT"), sem("ld_g"), sem("zeroed")
    squares, vchain, v32_ok, v_hi_ok = sem("squares"), sem("vchain"), sem("v32_ok"), sem("v_hi_ok")
    wkq_mm, wkq_ok, kq_mm, kq_hi_ok, kq_lo_ok = (sem(n) for n in ("wkq_mm", "wkq_ok", "kq_mm", "kq_hi_ok", "kq_lo_ok"))
    wi_mm, wi_hi_ok, wi_lo_ok, wh_hi_ok = sem("wi_mm"), sem("wi_hi_ok"), sem("wi_lo_ok"), sem("wh_hi_ok")
    FULL = MT - 1
    keys = [(h, c) for c in range(-(-M // CH)) for h in range(DH)]
    gru = [(h, n0, min(CH, G - n0)) for h in range(DH) for n0 in range(0, G, CH)]

    with nc.Block() as block:
        @block.sync
        def _(sp):
            for t, name in ((wq, "Wq"), (wk, "Wk"), (wv, "Wv")):
                sp.dma_start(t[:], io[name].rearrange("(c p) f -> p c f", p=P)).then_inc(ld_w, 16)
            sp.dma_start(cols[:], io["x_cols"]).then_inc(ld_w, 16)
            sp.dma_start(cxT[:], io["ctxT"].rearrange("(c p) t -> p c t", p=P)).then_inc(ld_cT, 16)
            sp.wait_ge(zeroed, 1)
            sp.dma_start(cx[:, 0:FULL], io["ctx"][0:FULL * P].rearrange("(t p) d -> p t d", p=P)).then_inc(ld_c, 16)
            sp.dma_start(cx[0:MROWS[-1], FULL], io["ctx"][FULL * P:]).then_inc(ld_c, 16)
            sp.dma_start(wiT[:], io["gru_wiT"].rearrange("(c p) f -> p c f", p=P)).then_inc(ld_g, 16)
            sp.dma_start(whT[:], io["gru_whT"].rearrange("(c p) f -> p c f", p=P)).then_inc(ld_g, 16)
            sp.dma_start(bi[:], io["gru_cols"]).then_inc(ld_g, 16)

        @block.scalar
        def _(act):
            act.wait_ge(ld_c, 32)
            for m in range(MT):
                if m >= 2:
                    act.wait_ge(squares, m - 1)
                act.activation(junk[:, m % 2], cx[:, m], ACT.Square, accum_out=ss[:, m:m + 1]).then_inc(squares, 1)
            for i, (h, c) in enumerate(keys):
                n = min(CH, M - c * CH)
                act.wait_ge(kq_mm, i + 1)
                act.activation(kq_hi[:, h, c * CH:c * CH + n], bank[2 + i % 2][:, 0:n], ACT.Copy,
                               scale=cols[:, DH + h:DH + h + 1]).then_inc(kq_hi_ok, 1)
            act.wait_ge(v32_ok, MT)
            act.activation(v_hi[:], v32[:], ACT.Copy).then_inc(v_hi_ok, 1)
            act.wait_ge(ld_g, 48)
            act.activation(wh_hi[:], whT[:], ACT.Copy).then_inc(wh_hi_ok, 1)
            for i, (h, n0, n) in enumerate(gru):
                act.wait_ge(wi_mm, i + 1)
                act.activation(wi_hi[:, h, n0:n0 + n], bank[4 + i % 2][:, 0:n], ACT.Copy,
                               scale=cols[:, h:h + 1]).then_inc(wi_hi_ok, 1)

        @block.vector
        def _(v):
            k = Chain(v, vchain)
            v.memset(cx[:, FULL], 0.0).then_inc(zeroed, 1)
            v.wait_ge(ld_w, 64)
            for h in range(DH):
                v.wait_ge(wkq_mm, h + 1)
                v.tensor_scalar(wkq[:, h], bank[h][:, 0:D], cols[:, h:h + 1], None, ALU.mult).then_inc(wkq_ok, 1)
            v.wait_ge(squares, MT)
            k.step(v.tensor_scalar(ss[:], ss[:], 1.0 / D, EPS_RMS, ALU.mult, ALU.add))
            rsqrt_steps(v, k, rs[:], ss[:], tmp[:])
            k.step(v.tensor_scalar(rs16[:], rs[:], float(D) ** -0.5, None, ALU.mult))
            for m in range(MT):
                v.tensor_scalar(v32[:, m], cx[:, m], rs[:, m:m + 1], None, ALU.mult).then_inc(v32_ok, 1)
            for i, (h, c) in enumerate(keys):
                n = min(CH, M - c * CH)
                v.wait_ge(kq_hi_ok, i + 1)
                v.scalar_tensor_tensor(out=kq_lo[:, h, c * CH:c * CH + n], in0=bank[2 + i % 2][:, 0:n],
                                       scalar=cols[:, DH + h:DH + h + 1],
                                       in1=kq_hi[:, h, c * CH:c * CH + n].bitcast(F32),
                                       op0=ALU.mult, op1=ALU.subtract).then_inc(kq_lo_ok, 1)
            v.wait_ge(v_hi_ok, 1)
            k.mark(v.tensor_tensor(v_lo[:], v32[:], v_hi[:].bitcast(F32), ALU.subtract))
            v.wait_ge(wh_hi_ok, 1)
            k.mark(v.tensor_tensor(wh_lo[:], whT[:], wh_hi[:].bitcast(F32), ALU.subtract))
            for i, (h, n0, n) in enumerate(gru):
                v.wait_ge(wi_hi_ok, i + 1)
                v.scalar_tensor_tensor(out=wi_lo[:, h, n0:n0 + n], in0=bank[4 + i % 2][:, 0:n], scalar=cols[:, h:h + 1],
                                       in1=wi_hi[:, h, n0:n0 + n].bitcast(F32), op0=ALU.mult,
                                       op1=ALU.subtract).then_inc(wi_lo_ok, 1)
            k.mark(v.tensor_tensor(bias[:, 0:2 * DH], bi[:, 0:2 * DH], bi[:, 3 * DH:5 * DH], ALU.add))
            k.mark(v.tensor_copy(bias[:, 2 * DH:3 * DH], bi[:, 2 * DH:3 * DH]))
            k.step(v.tensor_copy(bias[:, 3 * DH:], bi[:, 5 * DH:]))

        @block.tensor
        def _(pe):
            pe.wait_ge(ld_w, 64)
            for h in range(DH):
                for k in range(DH):
                    last = pe.matmul(bank[h][:, 0:D], wk[:, k, h * P:(h + 1) * P], wq[:, k], start=(k == 0), stop=(k == DH - 1))
                last.then_inc(wkq_mm, 1)
            pe.wait_ge(wkq_ok, DH)
            pe.wait_ge(ld_cT, 16)
            for i, (h, c) in enumerate(keys):
                n = min(CH, M - c * CH)
                if i >= 2:
                    pe.wait_ge(kq_lo_ok, i - 1)
                for k in range(DH):
                    last = pe.matmul(bank[2 + i % 2][:, 0:n], wkq[:, k, h * P:(h + 1) * P], cxT[:, k, c * CH:c * CH + n],
                                     start=(k == 0), stop=(k == DH - 1))
                last.then_inc(kq_mm, 1)
            pe.wait_ge(ld_g, 48)
            for i, (h, n0, n) in enumerate(gru):
                if i >= 2:
                    pe.wait_ge(wi_lo_ok, i - 1)
                for k in range(DH):
                    last = pe.matmul(bank[4 + i % 2][:, 0:n], wv[:, k, h * P:(h + 1) * P], wiT[:, k, n0:n0 + n],
                                     start=(k == 0), stop=(k == DH - 1))
                last.then_inc(wi_mm, 1)


SLOTS = 256
SH = SLOTS // P
TOP = 2
TILES = T * TOP // SLOTS + NE - 1
ROWS = TILES * SLOTS
PLACES = ROWS // P
assert PLACES <= P
SHIFT = SLOTS.bit_length() - 1


def layer_norm_factors(v, k, tiles, z, stats, mv, rs, tmp, nb, counted):
    sl = slice(tiles[0], tiles[-1] + 1)
    for t in tiles:
        mark = k.mark(v.bn_stats(stats[:, t], z[:, t]))
    v.wait_ge(k.sem, mark)
    for t in tiles:
        mark = k.mark(v.bn_aggr(mv[:, t], stats[:, t]))
    v.wait_ge(k.sem, mark)
    k.step(v.tensor_scalar(nb[:, sl], mv[:, sl, 1], EPS_LN, None, ALU.add))
    rsqrt_steps(v, k, rs[:, sl], nb[:, sl], tmp[:, sl])
    v.scalar_tensor_tensor(out=nb[:, sl], in0=mv[:, sl, 0], scalar=-1.0, in1=rs[:, sl], op0=ALU.mult,
                           op1=ALU.mult).then_inc(counted, 1)


def route(nc, io, shared):
    ident, ones, sT = shared["ident"], shared["ones"], shared["sT"]
    emap, token_of, row_of, gate = shared["emap"], shared["token_of"], shared["row_of"], shared["gate"]
    KT = TOP * NT
    HALF = KT // 2
    with ExitStack() as ctx:
        def sb(name, shape, dt=F32):
            return ctx.enter_context(nc.sbuf_tensor("r_" + name, shape, dt))

        def sem(name):
            return ctx.enter_context(nc.semaphore("r_" + name))

        bank = [ctx.enter_context(nc.psum_tensor(f"r_bank{i}", [P, CH], F32)) for i in range(8)]
        TURN_BANKS = (0, 1, 6, 7)
        x2 = sb("x2", [P, NT, D])
        x2T = sb("x2T", [P, 2, DH, P])
        stats, mv = sb("stats", [P, NT, 6]), sb("mv", [P, NT, 2])
        nb, rs, tmp = sb("nb", [P, NT]), sb("rs", [P, NT]), sb("tmp", [P, NT])
        rw = sb("rw", [P, DH, NE])
        rb = sb("rb", [P, 2, NE])
        tri = sb("tri", [P, P])
        earlier_i = sb("earlier_i", [P, NE], I32)
        tile_no = sb("tile_no", [P, TILES], I32)
        lane_i = sb("lane_i", [P, P], I32)
        row_i = sb("row_i", [P, TOP, NT], I32)
        spare_i = sb("spare_i", [P, PLACES], I32)
        earlier, tile_f, lane, row, spare = (sb(n, t.shape) for n, t in (
            ("earlier", earlier_i), ("tile_f", tile_no), ("lane", lane_i), ("row", row_i), ("spare", spare_i)))
        lg = sb("lg", [P, NT, NE])
        red = sb("red", [P, NT])
        pr = sb("pr", [P, NT, NE])
        left = sb("left", [P, NT, NE])
        equal = sb("equal", [P, NT, NE])
        chosen = [sb(f"chosen{k}", [P, NT, NE]) for k in range(TOP)]
        sel = sb("sel", [P, NT, NE])
        place = sb("place", [P, NT, NE])
        cum = sb("cum", [P, 2, NT + NT // 2, NE])
        end = sb("end", [P, 2, NE + NE // 2])
        cnt = sb("cnt", [P, NE], I32)
        ntile, start = sb("ntile", [P, NE]), sb("start", [P, NE])
        emf = sb("emf", [P, TILES, NE])
        emr = sb("emr", [P, TILES])
        pf = sb("pf", [P, TOP, NT])
        pi, hi_i, lo_i = (sb(n, [P, KT], I32) for n in ("pi", "hi_i", "lo_i"))
        hi_f, lo_f = sb("hi_f", [P, KT]), sb("lo_f", [P, KT])
        lane_is = sb("lane_is", [P, 4, KT // 4, P])
        column_is = sb("column_is", [P, KT, PLACES])
        found, empty = sb("found", [P, PLACES]), sb("empty", [P, PLACES])
        found_i = sb("found_i", [P, PLACES], I32)

        ld_x = [sem(f"ld_x{c}") for c in range(NC)]
        ld_r, consts, gchain, vchain = (sem(n) for n in ("ld_r", "consts", "gchain", "vchain"))
        turn_mm, z_ok, norm_ok, x2_ok, x2T_mm, x2T_ok, lg_mm, sub_ok, exp_ok = (
            sem(n) for n in ("turn_mm", "z_ok", "norm_ok", "x2_ok", "x2T_mm", "x2T_ok", "lg_mm", "sub_ok", "exp_ok"))
        sel_ok, pos_mm, column_ok, lane_ok, found_mm, kept = (
            sem(n) for n in ("sel_ok", "pos_mm", "column_ok", "lane_ok", "found_mm", "kept"))

        block = ctx.enter_context(nc.Block())

        @block.sync
        def _(sp):
            x1 = io["x1"].rearrange("(t p) d -> p t d", p=P)
            for c in range(NC):
                ts = slice(c * TPC, (c + 1) * TPC)
                sp.dma_start(x2[:, ts], x1[:, ts]).then_inc(ld_x[c], 16)
            sp.dma_start(rw[:], io["router_w"].rearrange("(c p) e -> p c e", p=P)).then_inc(ld_r, 16)
            sp.dma_start(rb[:, 0], io["router_b"].partition_broadcast(P)).then_inc(ld_r, 16)
            sp.dma_start(rb[:, 1], io["expert_bias"].partition_broadcast(P)).then_inc(ld_r, 16)
            shared["load_weights"](sp)
            sp.wait_ge(x2_ok, NT)
            sp.dma_start(io["x2"].rearrange("(t p) d -> p t d", p=P), x2[:]).then_inc(kept, 16)
            sp.wait_ge(kept, 16)

        @block.gpsimd
        def _(pool):
            g = Chain(pool, gchain)
            g.step(pool.memset(tri[:], 1.0))
            g.step(pool.affine_select(out=tri[:], in_=tri[:], compare_op=ALU.is_ge, fill=0.0,
                                      base=-1, pattern=[[1, P]], channel_multiplier=-1))
            pool.iota(tile_no[:], pattern=[[1, TILES]], base=0, channel_multiplier=0).then_inc(consts, 1)
            pool.iota(earlier_i[:], pattern=[[-1, NE]], base=NE, channel_multiplier=0).then_inc(consts, 1)
            pool.iota(lane_i[:], pattern=[[1, P]], base=0, channel_multiplier=0).then_inc(consts, 1)
            pool.iota(row_i[:], pattern=[[T, TOP], [P, NT]], base=1, channel_multiplier=1).then_inc(consts, 1)
            pool.iota(spare_i[:], pattern=[[P, PLACES]], base=TOP * T + 1, channel_multiplier=1).then_inc(consts, 1)
            pool.memset(cum[:], 0.0).then_inc(consts, 1)
            pool.memset(end[:], 0.0).then_inc(consts, 1)
            pool.wait_ge(consts, 7)
            for to, i in ((tile_f, tile_no), (earlier, earlier_i), (lane, lane_i), (row, row_i), (spare, spare_i)):
                pool.tensor_copy(to[:], i[:]).then_inc(consts, 1)

        @block.scalar
        def _(act):
            def apply(c):
                act.wait_ge(norm_ok, c + 1)
                for t in range(c * TPC, (c + 1) * TPC):
                    act.activation(x2[:, t], x2[:, t], ACT.Identity, bias=nb[:, t:t + 1], scale=rs[:, t:t + 1]).then_inc(x2_ok, 1)

            def take_turned(c):
                for t in range(c * TPC, (c + 1) * TPC):
                    act.wait_ge(x2T_mm, t + 1)
                    if t >= 2:
                        act.wait_ge(lg_mm, t - 1)
                    act.activation(x2T[:, t % 2].rearrange("p h n -> p (h n)"), bank[2 + t % 2][:, 0:D], ACT.Copy).then_inc(x2T_ok, 1)

            for c in range(NC):
                apply(c)
                take_turned(c)
            act.wait_ge(sub_ok, 1)
            act.activation(pr[:], lg[:], ACT.Exp).then_inc(exp_ok, 1)

        @block.vector
        def _(v):
            k = Chain(v, vchain)
            for c in range(NC):
                tiles = list(range(c * TPC, (c + 1) * TPC))
                v.wait_ge(ld_x[c], 16)
                for t in tiles:
                    v.wait_ge(turn_mm, t + 1)
                    v.tensor_tensor(x2[:, t], bank[TURN_BANKS[t % 4]][:, 0:D], x2[:, t], ALU.add).then_inc(z_ok, 1)
                v.wait_ge(z_ok, tiles[-1] + 1)
                layer_norm_factors(v, k, tiles, x2, stats, mv, rs, tmp, nb, norm_ok)
            v.wait_ge(lg_mm, NT)
            v.wait_ge(ld_r, 48)
            k.step(v.tensor_tensor(lg[:], bank[4][:, 0:NT * NE].rearrange("p (t e) -> p t e", e=NE), bc(rb[:, 0], 1, NT), ALU.add))
            k.step(v.tensor_tensor(lg[:], lg[:], bc(rb[:, 1], 1, NT), ALU.add))
            k.step(v.tensor_reduce(red[:], lg[:], AX_X, ALU.max))
            v.tensor_tensor(lg[:], lg[:], bc(red[:], 2, NE), ALU.subtract).then_inc(sub_ok, 1)
            v.wait_ge(exp_ok, 1)
            k.step(v.tensor_reduce(red[:], pr[:], AX_X, ALU.add))
            k.step(v.reciprocal(red[:], red[:]))
            k.step(v.tensor_tensor(pr[:], pr[:], bc(red[:], 2, NE), ALU.mult))
            v.wait_ge(consts, 12)
            for i in range(TOP):
                options = pr if i == 0 else left
                k.step(v.tensor_reduce(gate[:, i], options[:], AX_X, ALU.max))
                k.step(v.tensor_tensor(equal[:], options[:], bc(gate[:, i], 2, NE), ALU.is_equal))
                k.step(v.tensor_tensor(equal[:], equal[:], bc(earlier[:], 1, NT), ALU.mult))
                k.step(v.tensor_reduce(red[:], equal[:], AX_X, ALU.max))
                k.step(v.tensor_tensor(chosen[i][:], equal[:], bc(red[:], 2, NE), ALU.is_equal))
                if i == 0:
                    k.step(v.scalar_tensor_tensor(out=left[:], in0=chosen[0][:], scalar=-2.0, in1=pr[:], op0=ALU.mult, op1=ALU.add))
            v.tensor_tensor(sel[:], chosen[0][:], chosen[1][:], ALU.add).then_inc(sel_ok, 1)
            k.step(v.tensor_tensor(red[:], gate[:, 0], gate[:, 1], ALU.add))
            k.step(v.tensor_scalar(red[:], red[:], 1e-9, None, ALU.add))
            k.step(v.reciprocal(red[:], red[:]))
            for i in range(TOP):
                k.step(v.tensor_tensor(gate[:, i], gate[:, i], red[:], ALU.mult))
            v.wait_ge(pos_mm, 1)
            Z = NT // 2
            k.step(v.tensor_copy(cum[:, 0, Z:], bank[6][:, 0:NT * NE].rearrange("p (t e) -> p t e", e=NE)))
            at = 0
            for step in (1, 2, 4, 8):
                k.step(v.tensor_tensor(cum[:, 1 - at, Z:], cum[:, at, Z:], cum[:, at, Z - step:Z + NT - step], ALU.add))
                at = 1 - at
            k.step(v.tensor_scalar(cnt[:], cum[:, at, Z + NT - 1], float(SLOTS - 1), None, ALU.add))
            k.step(v.tensor_scalar(cnt[:], cnt[:], SHIFT, None, ALU.arith_shift_right))
            k.step(v.tensor_copy(ntile[:], cnt[:]))
            Y = NE // 2
            k.step(v.tensor_copy(end[:, 0, Y:], ntile[:]))
            to = 0
            for step in (1, 2, 4):
                k.step(v.tensor_tensor(end[:, 1 - to, Y:], end[:, to, Y:], end[:, to, Y - step:Y + NE - step], ALU.add))
                to = 1 - to
            k.step(v.tensor_tensor(start[:], end[:, to, Y:], ntile[:], ALU.subtract))
            k.step(v.tensor_scalar(start[:], start[:], float(SLOTS), None, ALU.mult))
            k.step(v.tensor_tensor(place[:], bank[5][:, 0:NT * NE].rearrange("p (t e) -> p t e", e=NE),
                                   cum[:, at, Z - 1:Z + NT - 1], ALU.add))
            k.step(v.tensor_tensor(place[:], place[:], bc(start[:], 1, NT), ALU.add))
            for i in range(TOP):
                k.step(v.tensor_tensor(equal[:], place[:], chosen[i][:], ALU.mult))
                k.step(v.tensor_reduce(pf[:, i], equal[:], AX_X, ALU.add))
            k.step(v.tensor_copy(pi[:], pf[:].rearrange("p k t -> p (k t)")))
            k.step(v.tensor_scalar(hi_i[:], pi[:], P.bit_length() - 1, None, ALU.arith_shift_right))
            k.step(v.tensor_scalar(lo_i[:], pi[:], P - 1, None, ALU.bitwise_and))
            k.step(v.tensor_copy(hi_f[:], hi_i[:]))
            k.step(v.tensor_copy(lo_f[:], lo_i[:]))
            row_kt = row[:].rearrange("p k t -> p (k t)")
            for g in range(4):
                ks = slice(g * KT // 4, (g + 1) * KT // 4)
                k.step(v.tensor_tensor(column_is[:, ks], bc(lane[:, 0:PLACES], 1, KT // 4), bc(hi_f[:, ks], 2, PLACES), ALU.is_equal))
                k.step(v.tensor_tensor(column_is[:, ks], column_is[:, ks], bc(row_kt[:, ks], 2, PLACES), ALU.mult))
                v.tensor_tensor(lane_is[:, g], bc(lane[:], 1, KT // 4), bc(lo_f[:, ks], 2, P), ALU.is_equal).then_inc(lane_ok, 1)
            k.step(v.tensor_tensor(emf[:], bc(tile_f[:], 2, NE), bc(end[:, to, Y:], 1, TILES), ALU.is_ge))
            k.step(v.tensor_reduce(emr[:], emf[:], AX_X, ALU.add))
            k.step(v.tensor_scalar(emap[:], emr[:], float(NE - 1), None, ALU.min))
            v.wait_ge(found_mm, 1)
            k.step(v.tensor_scalar(found[:], bank[7][:, 0:PLACES], -1.0, None, ALU.add))
            k.step(v.tensor_scalar(empty[:], bank[7][:, 0:PLACES], 0.0, None, ALU.is_equal))
            k.step(v.tensor_tensor(empty[:], empty[:], spare[:], ALU.mult))
            k.step(v.tensor_copy(found_i[:], found[:]))
            k.step(v.tensor_scalar(token_of[:], found_i[:], T - 1, None, ALU.bitwise_and))
            k.step(v.tensor_tensor(row_of[:], found[:], empty[:], ALU.add))

        @block.tensor
        def _(pe):
            def turn(t):
                if t >= 4:
                    pe.wait_ge(z_ok, t - 3)
                for h in range(DH):
                    last = pe.transpose(bank[TURN_BANKS[t % 4]][:, h * P:(h + 1) * P], sT[:, h, t * P:(t + 1) * P], ident[:])
                last.then_inc(turn_mm, 1)

            def turn_x2(t):
                pe.wait_ge(x2_ok, t + 1)
                if t >= 2:
                    pe.wait_ge(x2T_ok, t - 1)
                for h in range(DH):
                    last = pe.transpose(bank[2 + t % 2][:, h * P:(h + 1) * P], x2[:, t, h * P:(h + 1) * P], ident[:])
                last.then_inc(x2T_mm, 1)

            def logits(t):
                pe.wait_ge(x2T_ok, t + 1)
                if t == 0:
                    pe.wait_ge(ld_r, 48)
                for h in range(DH):
                    last = pe.matmul(bank[4][:, t * NE:(t + 1) * NE], x2T[:, t % 2, h], rw[:, h],
                                     start=(h == 0), stop=(h == DH - 1))
                last.then_inc(lg_mm, 1)

            for t in range(TPC):
                turn(t)
            for t in range(NT):
                if t + TPC < NT:
                    turn(t + TPC)
                turn_x2(t)
                if t >= 1:
                    logits(t - 1)
            logits(NT - 1)
            pe.wait_ge(consts, 12)
            pe.wait_ge(sel_ok, 1)
            pe.matmul(bank[5][:, 0:NT * NE], tri[:], sel[:].rearrange("p t e -> p (t e)"), start=True, stop=True)
            pe.matmul(bank[6][:, 0:NT * NE], ones[:], sel[:].rearrange("p t e -> p (t e)"), start=True,
                      stop=True).then_inc(pos_mm, 1)
            for i in range(KT):
                pe.wait_ge(lane_ok, i // (KT // 4) + 1)
                last = pe.matmul(bank[7][:, 0:PLACES], lane_is[:, i // (KT // 4), i % (KT // 4)], column_is[:, i],
                                 start=(i == 0), stop=(i == KT - 1))
            last.then_inc(found_mm, 1)


def experts(nc, io, shared):
    ident, sT, emap = shared["ident"], shared["sT"], shared["emap"]
    token_of, row_of = shared["token_of"], shared["row_of"]
    w1, w2, b1, b2, ld_e = (shared[n] for n in ("w1", "w2", "b1", "b2", "ld_e"))
    FP = FT // 2
    with ExitStack() as ctx:
        def sb(name, shape, dt=F32):
            return ctx.enter_context(nc.sbuf_tensor("e_" + name, shape, dt))

        def sem(name):
            return ctx.enter_context(nc.semaphore("e_" + name))

        bank = [ctx.enter_context(nc.psum_tensor(f"e_bank{i}", [P, CH], F32)) for i in range(8)]
        w1_hi, w1_lo = sb("w1_hi", [P, DH, F], F32R), sb("w1_lo", [P, DH, F], F32R)
        w2_hi, w2_lo = sb("w2_hi", [P, FT, D], F32R), sb("w2_lo", [P, FT, D], F32R)
        xT_hi, xT_lo = sb("xT_hi", [P, 2, DH, SLOTS], F32R), sb("xT_lo", [P, 2, DH, SLOTS], F32R)
        g_hi, g_lo = sb("g_hi", [P, FT, SLOTS], F32R), sb("g_lo", [P, FT, SLOTS], F32R)
        room = sT[:].rearrange("p c (a n) -> p (c a) n", n=CH)
        xg = [room[:, i].rearrange("p (s d) -> p s d", s=SH) for i in range(2)]
        y = [room[:, 2 + i].rearrange("p (s d) -> p s d", s=SH) for i in range(2)]
        g32 = [room[:, 4 + i].rearrange("p (f n) -> p f n", f=2) for i in range(2)]

        tokens, rows = sb("tokens", [P, 2 * SH], I32), sb("rows", [P, 2 * SH], I32)
        tokens_ok, rows_ok = sem("tokens_ok"), sem("rows_ok")
        passed = sem("passed")

        ld_x, y_out = [sem("ld_x0"), sem("ld_x1")], [sem("y_out0"), sem("y_out1")]
        xT_mm, xT_hi_ok, xT_lo_ok, w1_hi_ok, w1_lo_ok, w2_hi_even, w2_hi_odd, w2_lo_ok = (
            sem(n) for n in ("xT_mm", "xT_hi_ok", "xT_lo_ok", "w1_hi_ok", "w1_lo_ok", "w2_hi_even", "w2_hi_odd", "w2_lo_ok"))
        up_mm, g32_ok, g_hi_ok, g_lo_ok, y_mm, y_ok = (
            sem(n) for n in ("up_mm", "g32_ok", "g_hi_ok", "g_lo_ok", "y_mm", "y_ok"))
        block = ctx.enter_context(nc.Block())

        @block.gpsimd
        def _(pool):
            def take(i, slot, first=False):
                if not first:
                    pool.wait_ge(xT_mm, i - 1)
                pool.tensor_copy(tokens[:, slot * SH:(slot + 1) * SH], token_of[:, bass.ds(i * SH, SH)]).then_inc(tokens_ok, 1)
                pool.wait_ge(tokens_ok, i + 1)
                pool.sem_inc(passed, 1)
                for s in range(SH):
                    pool.indirect_dma_start(out=xg[slot][:, s], out_offset=None, in_=io["x2"],
                                            in_offset=bass.IndirectOffsetOnAxis(tokens[:, slot * SH + s:slot * SH + s + 1], 0)).then_inc(ld_x[slot], 16)

            def give(i, slot):
                pool.wait_ge(y_ok, SH * i + 1)
                pool.tensor_copy(rows[:, slot * SH:(slot + 1) * SH], row_of[:, bass.ds(i * SH, SH)]).then_inc(rows_ok, 1)
                pool.wait_ge(rows_ok, i + 1)
                for s in range(SH):
                    pool.wait_ge(y_ok, SH * i + s + 1)
                    pool.sem_inc(passed, 1)
                    pool.indirect_dma_start(out=io["results"], out_offset=bass.IndirectOffsetOnAxis(rows[:, slot * SH + s:slot * SH + s + 1], 0),
                                            in_=y[slot][:, s], in_offset=None).then_inc(y_out[slot], 16)

            def weights(i, first=False):
                ex = pool.value_load(emap[0:1, bass.ds(i, 1)], min_val=0, max_val=NE - 1)
                if not first:
                    pool.wait_ge(y_mm, i * SH)
                for f in range(0, FP, 2):
                    pool.tensor_copy(w2_hi[:, 2 * f:2 * f + 2], w2[:, bass.ds(ex, 1), 2 * f:2 * f + 2].rearrange("p e c f -> p (e c) f")).then_inc(w2_hi_even, 1)

            take(0, 0, first=True)
            take(1, 1, first=True)
            pool.wait_ge(ld_e, 16 * (2 * NE + 2))
            weights(0, first=True)
            take(2, 0)
            weights(1)
            take(3, 1)
            give(0, 0)
            with pool.Fori(1, TILES // 2 - 1) as it:
                for slot in range(2):
                    i = it * 2 + slot
                    weights(i)
                    take(i + 2, slot)
                    give(i - 1, 1 - slot)
            weights(TILES - 3)
            take(TILES - 1, 0)
            give(TILES - 4, 1)
            for i in range(TILES - 2, TILES):
                weights(i)
                give(i - 1, (i - 1) % 2)
            give(TILES - 1, 0)
            pool.wait_ge(y_out[0], 16 * SH * (TILES // 2 + 1))
            pool.wait_ge(y_out[1], 16 * SH * (TILES // 2))

        @block.scalar
        def _(act):
            act.wait_ge(ld_e, 16 * (2 * NE + 2))

            def turn(i, slot):
                act.wait_ge(xT_mm, i + 1)
                act.activation(xT_hi[:, slot].rearrange("p c n -> p (c n)"), bank[0][:], ACT.Copy).then_inc(xT_hi_ok, 1)

            def w1_high(i, ex, f):
                cols = slice(f * 2 * P, (f + 1) * 2 * P)
                act.activation(w1_hi[:, :, cols], w1[:, bass.ds(ex, 1), :, cols].rearrange("p e c f -> p (e c) f"), ACT.Copy).then_inc(w1_hi_ok, 1)

            def body(i, slot, n, first=False, last=False):
                ex = act.value_load(emap[0:1, bass.ds(i, 1)], min_val=0, max_val=NE - 1)
                if not last:
                    nx = act.value_load(emap[0:1, bass.ds(i + 1, 1)], min_val=0, max_val=NE - 1)
                for f in range(FP):
                    if f % 2 == 1:
                        if not first:
                            act.wait_ge(y_mm, i * SH)
                        act.activation(w2_hi[:, 2 * f:2 * f + 2], w2[:, bass.ds(ex, 1), 2 * f:2 * f + 2].rearrange("p e c f -> p (e c) f"), ACT.Copy).then_inc(w2_hi_odd, 1)
                    act.wait_ge(up_mm, i * FP + f + 1)
                    if not (first and f < 2):
                        act.wait_ge(g_lo_ok, i * FP + f - 1)
                    for a in range(2):
                        act.activation(g32[f % 2][:, a], bank[1 + f % 2][:, a * SLOTS:(a + 1) * SLOTS], ACT.Gelu,
                                       bias=b1[:, bass.ds(ex * FT + (2 * f + a), 1)]).then_inc(g32_ok, 1)
                    act.wait_ge(g32_ok, (i * FP + f + 1) * 2)
                    if not first:
                        act.wait_ge(y_mm, i * SH)
                    act.activation(g_hi[:, 2 * f:2 * f + 2], g32[f % 2], ACT.Copy).then_inc(g_hi_ok, 1)
                    if f == FP - 1 and not last:
                        turn(i + 1, 1 - slot)
                if not last:
                    for f in range(FP):
                        w1_high(i + 1, nx, f)

            ex0 = act.value_load(emap[0:1, 0:1], min_val=0, max_val=NE - 1)
            turn(0, 0)
            for f in range(FP):
                w1_high(0, ex0, f)
            body(0, 0, 0, first=True)
            body(1, 1, 0)
            with act.Fori(1, TILES // 2) as it:
                body(it * 2, 0, it)
                body(it * 2 + 1, 1, it)
            body(TILES - 1, 0, TILES // 2, last=True)

        @block.vector
        def _(v):
            v.wait_ge(ld_e, 16 * (2 * NE + 2))

            def turn(i, slot):
                v.wait_ge(xT_hi_ok, i + 1)
                v.tensor_tensor(xT_lo[:, slot].rearrange("p c n -> p (c n)"), bank[0][:],
                                xT_hi[:, slot].bitcast(F32).rearrange("p c n -> p (c n)"), ALU.subtract).then_inc(xT_lo_ok, 1)

            def split_w1(i, ex, f):
                cols = slice(f * 2 * P, (f + 1) * 2 * P)
                v.wait_ge(w1_hi_ok, i * FP + f + 1)
                v.tensor_tensor(w1_lo[:, :, cols], w1[:, bass.ds(ex, 1), :, cols].rearrange("p e c f -> p (e c) f"),
                                w1_hi[:, :, cols].bitcast(F32), ALU.subtract).then_inc(w1_lo_ok, 1)

            def split_w2(i, ex, f):
                v.wait_ge(w2_hi_odd if f % 2 else w2_hi_even, i * (FP // 2) + f // 2 + 1)
                v.tensor_tensor(w2_lo[:, 2 * f:2 * f + 2], w2[:, bass.ds(ex, 1), 2 * f:2 * f + 2].rearrange("p e c f -> p (e c) f"),
                                w2_hi[:, 2 * f:2 * f + 2].bitcast(F32), ALU.subtract).then_inc(w2_lo_ok, 1)

            def body(i, slot, n, warm_up=False, last=False):
                ex = v.value_load(emap[0:1, bass.ds(i, 1)], min_val=0, max_val=NE - 1)
                if not last:
                    nx = v.value_load(emap[0:1, bass.ds(i + 1, 1)], min_val=0, max_val=NE - 1)
                for f in range(FP):
                    split_w2(i, ex, f)
                    v.wait_ge(g_hi_ok, i * FP + f + 1)
                    v.tensor_tensor(g_lo[:, 2 * f:2 * f + 2], g32[f % 2], g_hi[:, 2 * f:2 * f + 2].bitcast(F32),
                                    ALU.subtract).then_inc(g_lo_ok, 1)
                    if f == FP - 1 and not last:
                        turn(i + 1, 1 - slot)
                for s in range(SH):
                    if not last:
                        split_w1(i + 1, nx, 2 * s)
                        split_w1(i + 1, nx, 2 * s + 1)
                    v.wait_ge(y_mm, i * SH + s + 1)
                    if s == 0 and not warm_up:
                        v.wait_ge(y_out[slot], 16 * SH * n)
                    v.tensor_tensor(y[slot][:, s], bank[3 + s][:, 0:D], b2[:, bass.ds(ex * D, D)], ALU.add).then_inc(y_ok, 1)

            ex0 = v.value_load(emap[0:1, 0:1], min_val=0, max_val=NE - 1)
            turn(0, 0)
            for f in range(FP):
                split_w1(0, ex0, f)
            body(0, 0, 0, warm_up=True)
            body(1, 1, 0, warm_up=True)
            with v.Fori(1, TILES // 2) as it:
                body(it * 2, 0, it)
                body(it * 2 + 1, 1, it)
            body(TILES - 1, 0, TILES // 2, last=True)

        @block.tensor
        def _(pe):
            def turn(i, slot, n):
                pe.wait_ge(ld_x[slot], 16 * SH * (n + 1))
                for h in range(DH):
                    for s in range(SH):
                        last = pe.transpose(bank[0][:, (h * SH + s) * P:(h * SH + s + 1) * P], xg[slot][:, s, h * P:(h + 1) * P], ident[:])
                last.then_inc(xT_mm, 1)

            def body(i, slot, n, first=False, last=False):
                pe.wait_ge(xT_lo_ok, i + 1)
                for f in range(FP):
                    pe.wait_ge(w1_lo_ok, i * FP + f + 1)
                    if not (first and f < 2):
                        pe.wait_ge(g32_ok, (i * FP + f - 1) * 2)
                    for a in range(2):
                        fs = slice((2 * f + a) * P, (2 * f + a + 1) * P)
                        for h in range(DH):
                            mm = three_pass(pe, bank[1 + f % 2][:, a * SLOTS:(a + 1) * SLOTS], w1_hi[:, h, fs], w1_lo[:, h, fs],
                                            xT_hi[:, slot, h], xT_lo[:, slot, h], h == 0, h == DH - 1)
                    mm.then_inc(up_mm, 1)
                    if f == 2 and not last:
                        turn(i + 1, 1 - slot, n + slot)
                for s in range(SH):
                    if not first:
                        pe.wait_ge(y_ok, (i - 1) * SH + s + 1)
                    for f in range(FT):
                        if s == 0 and f % 2 == 0:
                            pe.wait_ge(w2_lo_ok, i * FP + f // 2 + 1)
                            pe.wait_ge(g_lo_ok, i * FP + f // 2 + 1)
                        ss = slice(s * P, (s + 1) * P)
                        mm = three_pass(pe, bank[3 + s][:, 0:D], g_hi[:, f, ss], g_lo[:, f, ss], w2_hi[:, f], w2_lo[:, f],
                                        f == 0, f == FT - 1)
                    mm.then_inc(y_mm, 1)

            turn(0, 0, 0)
            body(0, 0, 0, first=True)
            body(1, 1, 0)
            with pe.Fori(1, TILES // 2) as it:
                body(it * 2, 0, it)
                body(it * 2 + 1, 1, it)
            body(TILES - 1, 0, TILES // 2, last=True)


def combine(nc, io, shared):
    gate = shared["gate"]
    with ExitStack() as ctx:
        def sb(name, shape, dt=F32):
            return ctx.enter_context(nc.sbuf_tensor("c_" + name, shape, dt))

        def sem(name):
            return ctx.enter_context(nc.semaphore("c_" + name))

        x2 = sb("x2", [P, NT, D])
        yk = sb("yk", [P, TOP, NT, D])
        stats, mv = sb("stats", [P, NT, 6]), sb("mv", [P, NT, 2])
        nb, rs, tmp = sb("nb", [P, NT]), sb("rs", [P, NT]), sb("tmp", [P, NT])
        vchain, norm_ok, out_ok, stored = (sem(n) for n in ("vchain", "norm_ok", "out_ok", "stored"))
        loaded = [sem(f"loaded{c}") for c in range(NC)]
        block = ctx.enter_context(nc.Block())

        def chunk(c):
            return slice(c * TPC, (c + 1) * TPC)

        @block.sync
        def _(sp):
            for c in range(NC):
                sp.dma_start(x2[:, chunk(c)], io["x2"].rearrange("(t p) d -> p t d", p=P)[:, chunk(c)]).then_inc(loaded[c], 16)
                for k in range(TOP):
                    results = io["results"][k * T:(k + 1) * T].rearrange("(t p) d -> p t d", p=P)
                    sp.dma_start(yk[:, k, chunk(c)], results[:, chunk(c)]).then_inc(loaded[c], 16)
            out = io["out"].rearrange("(t p) d -> p t d", p=P)
            for c in range(NC):
                sp.wait_ge(out_ok, (c + 1) * TPC)
                sp.dma_start(out[:, chunk(c)], x2[:, chunk(c)]).then_inc(stored, 16)
            sp.wait_ge(stored, 16 * NC)

        @block.scalar
        def _(act):
            for c in range(NC):
                act.wait_ge(norm_ok, c + 1)
                for t in range(c * TPC, (c + 1) * TPC):
                    act.activation(x2[:, t], x2[:, t], ACT.Identity, bias=nb[:, t:t + 1], scale=rs[:, t:t + 1]).then_inc(out_ok, 1)

        @block.vector
        def _(v):
            k = Chain(v, vchain)
            for c in range(NC):
                tiles = list(range(c * TPC, (c + 1) * TPC))
                v.wait_ge(loaded[c], 16 * (1 + TOP))
                for i in range(TOP):
                    for t in tiles:
                        mark = k.mark(v.scalar_tensor_tensor(out=x2[:, t], in0=yk[:, i, t], scalar=gate[:, i, t:t + 1],
                                                             in1=x2[:, t], op0=ALU.mult, op1=ALU.add))
                    v.wait_ge(vchain, mark)
                layer_norm_factors(v, k, tiles, x2, stats, mv, rs, tmp, nb, norm_ok)



def program(nc, io):
    with ExitStack() as ctx:
        def sb(name, shape, dt=F32):
            return ctx.enter_context(nc.sbuf_tensor(name, shape, dt))

        shared = {"ident": sb("ident", [P, P]), "ones": sb("ones", [P, P]), "sT": sb("sT", [P, DH, T])}
        decay_attention_and_mlp(nc, io, shared)
        cross_attention(nc, io, shared)
        shared |= {"emap": sb("emap", [P, TILES], I32), "token_of": sb("token_of", [P, PLACES], I32),
                   "row_of": sb("row_of", [P, PLACES], I32), "gate": sb("gate", [P, TOP, NT])}
        with ExitStack() as weights:
            def wsb(name, shape):
                return weights.enter_context(nc.sbuf_tensor(name, shape, F32))

            w1, w2 = wsb("w1", [P, NE, DH, F]), wsb("w2", [P, NE, FT, D])
            b1, b2 = wsb("b1", [P, NE * FT]), wsb("b2", [P, NE * D])
            ld_e = weights.enter_context(nc.semaphore("ld_e"))
            shared |= {"w1": w1, "w2": w2, "b1": b1, "b2": b2, "ld_e": ld_e}

            def load_weights(sp):
                sp.dma_start(b1[:], io["b1_cols"]).then_inc(ld_e, 16)
                sp.dma_start(b2[:], io["b2"].rearrange("e d -> (e d)").partition_broadcast(P)).then_inc(ld_e, 16)
                for e in range(NE):
                    sp.dma_start(w1[:, e], io["w1"][e].rearrange("(c p) f -> p c f", p=P)).then_inc(ld_e, 16)
                    sp.dma_start(w2[:, e], io["w2"][e].rearrange("(c p) f -> p c f", p=P)).then_inc(ld_e, 16)

            shared["load_weights"] = load_weights
            route(nc, io, shared)
            experts(nc, io, shared)
        combine(nc, io, shared)


def kernel(**inputs):
    import numpy as np
    import concourse.bacc as bacc
    from concourse.bass_utils import run_bass_kernel_spmd

    a = {name: np.asarray(value) for name, value in inputs.items()}

    def turned(x):
        return np.ascontiguousarray(x.T)

    def columns(*names):
        return np.ascontiguousarray(np.concatenate([a[n].reshape(-1, P).T for n in names], axis=1))

    x, context = a["x"][0], a["ctx_1024"][0]
    send = {
        "x": x, "xT": turned(x), "u": a["L0_attn_u"], "v": a["L0_attn_v"],
        "decay": a["L0_attn_decay_logit"], "alpha": a["L0_attn_alpha_logit"],
        "gate": a["L0_attn_k_base_gate_logit"].reshape(1), "taps": a["L0_attn_k_base_kernel"],
        "projT": turned(a["L0_attn_proj_w"]), "proj_b": a["L0_attn_proj_b"], "norm1_w": a["L0_attn_norm1_w"],
        "mlp_w1": a["L0_attn_mlp_w1"], "mlp_w2": a["L0_attn_mlp_w2"], "mlp_b2": a["L0_attn_mlp_b2"],
        "a_cols": columns("L0_attn_norm1_w", "L0_attn_norm2_w", "L0_attn_mlp_b1"),
        "ctx": context, "ctxT": turned(context),
        "Wq": a["L0_xattn_Wq"], "Wk": a["L0_xattn_Wk"], "Wv": a["L0_xattn_Wv"],
        "gru_wiT": turned(a["L0_xattn_gru_wi"]), "gru_whT": turned(a["L0_xattn_gru_wh"]),
        "x_cols": columns("L0_xattn_input_norm_w", "L0_xattn_slot_norm_w"),
        "gru_cols": columns("L0_xattn_gru_bi", "L0_xattn_gru_bh"),
        "router_w": a["L0_ffn_router_w"], "router_b": a["L0_ffn_router_b"], "expert_bias": a["L0_ffn_expert_bias"],
        "w1": a["L0_ffn_w1"], "w2": a["L0_ffn_w2"], "b1_cols": columns("L0_ffn_b1"), "b2": a["L0_ffn_b2"],
    }
    nc = bacc.Bacc("TRN2", target_bir_lowering=False, num_devices=1, dynamic_dma_scratch_size=4096)
    io = {k: nc.dram_tensor(f"in_{k}", v.shape, F32, kind="ExternalInput").ap() for k, v in send.items()}
    for name, shape in (("x1", (T, D)), ("x2", (T, D)), ("results", (TOP * T + ROWS, D))):
        io[name] = nc.dram_tensor(f"scratch_{name}", shape, F32).ap()
    io["out"] = nc.dram_tensor("out", (T, D), F32, kind="ExternalOutput").ap()
    program(nc, io)
    r = run_bass_kernel_spmd(nc, [{f"in_{k}": v for k, v in send.items()}], core_ids=[0])
    return r.results[0]["out"].reshape(1, T, D)
```

```python
from contextlib import ExitStack

import concourse.bass as bass
from concourse import mybir

F32 = mybir.dt.float32
F32R = mybir.dt.float32r
I32 = mybir.dt.int32
ALU = mybir.AluOpType
ACT = mybir.ActivationFunctionType
AX_X = mybir.AxisListType.X

P = 128
T = 2048
D = 256
DH = D // P
NT = T // P
CH = 512
NC = T // CH
TPC = CH // P
R = 16
SUB = 32
NSUB = P // SUB
KTAP = 4
F = 4 * D
FT = F // P
M = 1601
MT = -(-M // P)
MROWS = [min(P, M - m * P) for m in range(MT)]
ITERS = 3
NE = 8
EPS_LN = 1e-5
EPS_RMS = 1e-6
RSQRT_MAGIC = float(0x5F3759DF)
NEWTON = 3
RSQRT_STEPS = 2 + 3 * NEWTON


def bc(ap, axis, n):
    return ap.unsqueeze(axis).broadcast_to([*ap.shape[:axis], n, *ap.shape[axis:]])


class Chain:

    def __init__(self, eng, sem, base=0):
        self.eng, self.sem, self.n, self.base = eng, sem, 0, base

    def step(self, ins):
        self.n += 1
        ins.then_inc(self.sem, 1)
        self.eng.wait_ge(self.sem, self.base + self.n)

    def mark(self, ins):
        self.n += 1
        ins.then_inc(self.sem, 1)
        return self.base + self.n


def rsqrt_steps(v, chain, y, x, tmp):
    chain.step(v.tensor_scalar(tmp.bitcast(I32), x.bitcast(I32), 1, None, ALU.logical_shift_right))
    chain.step(v.tensor_scalar(y.bitcast(I32), tmp.bitcast(I32), -1.0, RSQRT_MAGIC, ALU.mult, ALU.add))
    for _ in range(NEWTON):
        chain.step(v.scalar_tensor_tensor(out=tmp, in0=y, scalar=-0.5, in1=y, op0=ALU.mult, op1=ALU.mult))
        chain.step(v.tensor_tensor(tmp, tmp, x, ALU.mult))
        chain.step(v.scalar_tensor_tensor(out=y, in0=tmp, scalar=1.5, in1=y, op0=ALU.add, op1=ALU.mult))


def three_pass(pe, out, w_hi, w_lo, x_hi, x_lo, start, stop):
    pe.matmul(out, w_hi, x_lo, start=start, stop=False)
    pe.matmul(out, w_lo, x_hi, start=False, stop=False)
    return pe.matmul(out, w_hi, x_hi, start=False, stop=stop)


def decay_attention_and_mlp(nc, io, shared):
    ident, ones, sT = shared["ident"], shared["ones"], shared["sT"]
    with ExitStack() as ctx:
        def sb(name, shape, dt=F32):
            return ctx.enter_context(nc.sbuf_tensor(name, shape, dt))

        def sem(name):
            return ctx.enter_context(nc.semaphore(name))

        bank = [ctx.enter_context(nc.psum_tensor(f"a_bank{i}", [P, CH], F32)) for i in range(8)]

        x = sb("a_x", [P, NT, D])
        hn = sb("a_hn", [P, NT, D])
        h2 = sb("a_h2", [P, NT, D])
        n2 = sb("a_n2", [P, 2, TPC, D])
        xT = oT = sT
        hT_hi = sb("a_hT_hi", [P, DH, 3 * CH], F32R)
        hT_lo = sb("a_hT_lo", [P, DH, 3 * CH], F32R)
        g32 = sb("a_g32", [P, 2, CH])
        g_hi = sb("a_g_hi", [P, FT, CH], F32R)
        g_lo = sb("a_g_lo", [P, FT, CH], F32R)
        w1_32 = sb("a_w1_32", [P, DH * F])
        w2_32 = n2[:].rearrange("p a t d -> p (a t d)")
        w1_hi = sb("a_w1_hi", [P, DH, F], F32R)
        w1_lo = sb("a_w1_lo", [P, DH, F], F32R)
        w2_hi = sb("a_w2_hi", [P, FT, D], F32R)
        w2_lo = sb("a_w2_lo", [P, FT, D], F32R)
        projT = sb("a_projT", [P, DH, D])
        uv = sb("a_uv", [P, DH, 2 * R])
        rows = sb("a_rows", [P, 3, D])
        cols = sb("a_cols", [P, 2 * DH + FT])
        sg = sb("a_sg", [P, 2 * R + 2])
        traw = sb("a_traw", [P, KTAP])
        lg = sb("a_lg", [P, R + 1])
        gk = sb("a_gk", [P, KTAP])
        expo = sb("a_expo", [P, 2, NSUB + 1], I32)
        expf = sb("a_expf", [P, 2, NSUB + 1])
        kw = sb("a_kw", [P, NSUB + 1, R])
        qw = sb("a_qw", [P, NSUB + 1, R])
        coef = sb("a_coef", [P, 1])
        taps = sb("a_taps", [P, KTAP, P + KTAP - 1])
        band = sb("a_band", [P, P + KTAP - 1])
        later = sb("a_later", [P, P])
        qk = sb("a_qk", [P, NT, 2, R])
        qkn = sb("a_qkn", [P, NT * 2])
        qkr = sb("a_qkr", [P, NT * 2])
        kcat = sb("a_kcat", [P, NT, 6, R])
        qcat = sb("a_qcat", [P, NT, 6, R])
        qkT = sb("a_qkT", [96, 3, 2 * P])
        AT = sb("a_AT", [P, 2, P])
        S = sb("a_S", [P, 4, D])
        ss = sb("a_ss", [P, NT])
        rs = sb("a_rs", [P, NT])
        tmp = sb("a_tmp", [P, 2 * NT])
        junk = sb("a_junk", [P, 2, D])
        qk_sq = junk[:].rearrange("p a (t b r) -> p (a t) b r", b=2, r=R)
        stats = sb("a_stats", [P, NT, 6])
        mv = sb("a_mv", [P, NT, 2])

        ld_x, ld_xT, ld_w, ld_mlp = sem("a_ld_x"), sem("a_ld_xT"), sem("a_ld_w"), sem("a_ld_mlp")
        ld_t, ld_uv, rs_ok = sem("a_ld_t"), sem("a_ld_uv"), sem("a_rs_ok")
        consts, masked, hi_w = sem("a_consts"), sem("a_masked"), sem("a_hi_w")
        vchain, gchain = sem("a_vchain"), sem("a_gchain")
        squares, zeroed, gammas, expos, coef_ok = (sem(f"a_{n}") for n in ("squares", "zeroed", "gammas", "expos", "coef_ok"))
        hn_ok, uv_ok, qk_mm, cats = sem("a_hn_ok"), sem("a_uv_ok"), sem("a_qk_mm"), sem("a_cats")
        turned, turned_sb = sem("a_turned"), sem("a_turned_sb")
        A_mm, A_sb, o_mm, o_sb, S_mm, S_sb = (sem(f"a_{n}") for n in ("A_mm", "A_sb", "o_mm", "o_sb", "S_mm", "S_sb"))
        xb_ok, h2_mm, h2_sb, n2_ok = (sem(f"a_{n}") for n in ("xb_ok", "h2_mm", "h2_sb", "n2_ok"))
        hT_mm, hT_hi_ok, hT_lo_ok, w_lo_ok = sem("a_hT_mm"), sem("a_hT_hi_ok"), sem("a_hT_lo_ok"), sem("a_w_lo_ok")
        up_mm, gelu_ok, g_ok, y_mm, z_ok, res_ok = (sem(f"a_{n}") for n in ("up_mm", "gelu_ok", "g_ok", "y_mm", "z_ok", "res_ok"))
        x1_ok, x1_mm, x1_sb, x1_out = (sem(f"a_{n}") for n in ("x1_ok", "x1_mm", "x1_sb", "x1_out"))


        def tile(t):
            return slice(t * P, (t + 1) * P)

        def chunk(c):
            return slice(c * CH, (c + 1) * CH)

        PROJ_BANKS = (0, 1, 6, 7)
        block = ctx.enter_context(nc.Block())

        @block.sync
        def _(sp):
            sp.dma_start(x[:], io["x"].rearrange("(t p) d -> p t d", p=P)).then_inc(ld_x, 16)
            sp.wait_ge(ld_xT, 16)
            sp.dma_start(w1_32[:].rearrange("p (c f) -> p c f", c=DH),
                         io["mlp_w1"].rearrange("(c p) f -> p c f", p=P)).then_inc(ld_mlp, 16)
            sp.dma_start(w2_32.rearrange("p (c f) -> p c f", c=FT),
                         io["mlp_w2"].rearrange("(c p) f -> p c f", p=P)).then_inc(ld_mlp, 16)
            for c in range(NC):
                ts = slice(c * TPC, (c + 1) * TPC)
                sp.wait_ge(x1_ok, c + 1)
                sp.dma_start(io["x1"].rearrange("(t p) d -> p t d", p=P)[:, ts], h2[:, ts]).then_inc(x1_out, 16)
            sp.wait_ge(x1_out, 16 * NC)

        @block.gpsimd
        def _(pool):
            g = Chain(pool, gchain)
            g.step(pool.memset(ident[:], 0.0))
            g.step(pool.memset(later[:], 1.0))
            g.step(pool.memset(taps[:], 0.0))
            g.step(pool.affine_select(out=ident[:], in_=ident[:], compare_op=ALU.not_equal, fill=1.0,
                                      base=0, pattern=[[-1, P]], channel_multiplier=1))
            g.step(pool.affine_select(out=later[:], in_=later[:], compare_op=ALU.is_ge, fill=0.0,
                                      base=0, pattern=[[1, P]], channel_multiplier=-1))
            for t in range(KTAP):
                g.step(pool.affine_select(out=taps[:, t, 0:P], in_=taps[:, t, 0:P], compare_op=ALU.not_equal,
                                          fill=1.0, base=-t, pattern=[[1, P]], channel_multiplier=-1))
                g.step(pool.affine_select(out=taps[:, t, P:], in_=taps[:, t, P:], compare_op=ALU.not_equal,
                                          fill=1.0, base=KTAP - 1 - t, pattern=[[-1, KTAP - 1]],
                                          channel_multiplier=1))
            g.step(pool.iota(expo[:, 0, :], pattern=[[SUB, NSUB + 1]], base=0, channel_multiplier=-1))
            g.step(pool.iota(expo[:, 1, 0:NSUB], pattern=[[-SUB, NSUB]], base=0, channel_multiplier=1))
            g.step(pool.iota(expo[:, 1, NSUB:], pattern=[[0, 1]], base=0, channel_multiplier=1))
            g.step(pool.memset(coef[:], 1.0))
            g.step(pool.affine_select(out=coef[:], in_=coef[:], compare_op=ALU.is_ge, fill=0.0,
                                      base=64 + R - 1, pattern=[[0, 1]], channel_multiplier=-1))
            g.step(pool.memset(kcat[:], 0.0))
            g.step(pool.memset(qcat[:], 0.0))
            g.step(pool.affine_select(out=kcat[:, :, 5, 0:KTAP - 1], in_=kcat[:, :, 5, 0:KTAP - 1],
                                      compare_op=ALU.not_equal, fill=1.0, base=-(P - KTAP + 1),
                                      pattern=[[0, NT], [-1, KTAP - 1]], channel_multiplier=1))
            g.step(pool.memset(ones[:], 1.0))
            pool.memset(S[:], 0.0).then_inc(consts, 1)
            pool.wait_ge(gammas, 4)
            g.step(pool.affine_select(out=kw[:, 0:NSUB, :], in_=kw[:, 0:NSUB, :], compare_op=ALU.is_ge, fill=0.0,
                                      base=SUB - 1, pattern=[[SUB, NSUB], [0, R]], channel_multiplier=-1))
            g.step(pool.affine_select(out=qw[:, 0:NSUB, :], in_=qw[:, 0:NSUB, :], compare_op=ALU.is_ge, fill=0.0,
                                      base=SUB - 1, pattern=[[SUB, NSUB], [0, R]], channel_multiplier=-1))
            pool.affine_select(out=qw[:, 0:NSUB, :], in_=qw[:, 0:NSUB, :], compare_op=ALU.is_ge, fill=0.0,
                               base=0, pattern=[[-SUB, NSUB], [0, R]], channel_multiplier=1).then_inc(masked, 1)
            pool.wait_ge(ld_w, 16 * 4)
            pool.wait_ge(ld_x, 16)
            pool.wait_ge(rs_ok, 1)
            for t in range(NT):
                g.step(pool.tensor_scalar(h2[:, t], x[:, t], rs[:, t:t + 1], None, ALU.mult))
                pool.tensor_tensor(hn[:, t], h2[:, t], rows[:, 0], ALU.mult).then_inc(hn_ok, 1)
            pool.wait_ge(hn_ok, NT)
            for t in range(NT):
                pool.tensor_tensor(h2[:, t], x[:, t], rows[:, 1], ALU.add).then_inc(xb_ok, 1)
            for t in range(NT):
                pool.wait_ge(h2_sb, t + 1)
                g.step(pool.tensor_tensor(hn[:, t], h2[:, t], x[:, t], ALU.add))
                pool.tensor_tensor(hn[:, t], hn[:, t], rows[:, 2], ALU.add).then_inc(res_ok, 1)

        @block.scalar
        def _(act):
            act.wait_ge(zeroed, 1)
            act.dma_start(sg[:, 0:R], io["decay"].partition_broadcast(P)).then_inc(ld_t, 16)
            act.dma_start(sg[:, R:2 * R], io["alpha"].partition_broadcast(P)).then_inc(ld_t, 16)
            act.dma_start(sg[64:64 + R, 2 * R:2 * R + 1], io["decay"].unsqueeze(1)).then_inc(ld_t, 16)
            act.dma_start(sg[:, 2 * R + 1:], io["gate"].partition_broadcast(P)).then_inc(ld_t, 16)
            act.dma_start(traw[:], io["taps"].partition_broadcast(P)).then_inc(ld_t, 16)
            act.dma_start(cols[:], io["a_cols"]).then_inc(ld_uv, 16)
            act.dma_start(uv[:, :, 0:R], io["u"].rearrange("(c p) r -> p c r", p=P)).then_inc(ld_uv, 16)
            act.dma_start(uv[:, :, R:], io["v"].rearrange("(c p) r -> p c r", p=P)).then_inc(ld_uv, 16)
            act.dma_start(xT[:], io["xT"].rearrange("(c p) t -> p c t", p=P)).then_inc(ld_xT, 16)
            for i, name in enumerate(("norm1_w", "proj_b", "mlp_b2")):
                act.dma_start(rows[:, i], io[name].partition_broadcast(P)).then_inc(ld_w, 16)
            act.dma_start(projT[:], io["projT"].rearrange("(c p) f -> p c f", p=P)).then_inc(ld_w, 16)
            act.wait_ge(ld_t, 16 * 5)
            act.activation(sg[:], sg[:], ACT.Exp, scale=-1.0).then_inc(gammas, 1)
            act.wait_ge(expos, 1)
            act.activation(lg[:], lg[:], ACT.Ln).then_inc(gammas, 1)
            act.wait_ge(coef_ok, 1)
            act.activation(kw[:], kw[:], ACT.Exp).then_inc(gammas, 1)
            act.activation(qw[:], qw[:], ACT.Exp).then_inc(gammas, 1)
            act.activation(lg[:, R:], lg[:, R:], ACT.Exp, scale=float(P)).then_inc(gammas, 1)
            act.wait_ge(ld_x, 16)
            for t in range(NT):
                if t >= 2:
                    act.wait_ge(squares, t - 1)
                act.activation(junk[:, t % 2], x[:, t], ACT.Square, accum_out=ss[:, t:t + 1]).then_inc(squares, 1)
            act.wait_ge(ld_mlp, 32)
            act.activation(w1_hi[:].rearrange("p c f -> p (c f)"), w1_32[:], ACT.Copy).then_inc(hi_w, 1)
            act.activation(w2_hi[:].rearrange("p c f -> p (c f)"), w2_32, ACT.Copy).then_inc(hi_w, 1)
            for t in range(NT + 2):
                if t < NT:
                    act.wait_ge(turned, t + 1)
                    if t >= 3:
                        act.wait_ge(o_mm, t - 2)
                    act.activation(qkT[:, t % 3], bank[t % 2][0:96, 0:2 * P], ACT.Copy).then_inc(turned_sb, 1)
                if t >= 2:
                    act.wait_ge(o_mm, t - 1)
                    act.activation(oT[:, :, tile(t - 2)], bank[4 + t % 2][:, 0:2 * P].rearrange("p (c t) -> p c t", c=DH),
                                   ACT.Copy).then_inc(o_sb, 1)
            def h2_squares(c):
                for t in range(c * TPC, (c + 1) * TPC):
                    act.wait_ge(h2_sb, t + 1)
                    act.wait_ge(squares, NT + t - 1)
                    act.activation(junk[:, t % 2], h2[:, t], ACT.Square, accum_out=ss[:, t:t + 1]).then_inc(squares, 1)

            def high_part(c):
                for h in range(DH):
                    act.wait_ge(hT_mm, DH * c + h + 1)
                    act.activation(hT_hi[:, h, chunk(c % 3)], bank[2 + (c % 2) * 2 + h][:], ACT.Copy,
                                   scale=cols[:, 2 + h:3 + h]).then_inc(hT_hi_ok, 1)

            def take_x1(c):
                for h in range(DH):
                    act.wait_ge(x1_mm, DH * c + h + 1)
                    act.activation(sT[:, h, chunk(c)], bank[2 + (c % 2) * 2 + h][:], ACT.Copy).then_inc(x1_sb, 1)

            for c in range(NC):
                h2_squares(c)
                if c >= 2:
                    high_part(c - 2)
            for c in range(NC):
                for f in range(FT):
                    n = c * FT + f
                    act.wait_ge(up_mm, n + 1)
                    if n >= 2:
                        act.wait_ge(g_ok, n - 1)
                    act.activation(g32[:, f % 2], bank[6 + f % 2][:], ACT.Gelu_apprx_tanh,
                                   bias=cols[:, 4 + f:5 + f]).then_inc(gelu_ok, 1)
                    if f == 5 and c + 2 < NC:
                        high_part(c + 2)
                    if f == 7 and c >= 2:
                        take_x1(c - 2)
            take_x1(NC - 2)
            take_x1(NC - 1)

        def low_part(v, c):
            for h in range(DH):
                v.wait_ge(hT_hi_ok, DH * c + h + 1)
                v.scalar_tensor_tensor(out=hT_lo[:, h, chunk(c % 3)], in0=bank[2 + (c % 2) * 2 + h][:],
                                       scalar=cols[:, 2 + h:3 + h], in1=hT_hi[:, h, chunk(c % 3)].bitcast(F32),
                                       op0=ALU.mult, op1=ALU.subtract).then_inc(hT_lo_ok, 1)

        @block.vector
        def _(v):
            k = Chain(v, vchain)
            v.memset(sg[:], 0.0).then_inc(zeroed, 1)
            v.wait_ge(gammas, 1)
            k.step(v.tensor_scalar(sg[:], sg[:], 1.0, None, ALU.add))
            k.step(v.reciprocal(sg[:], sg[:]))
            k.step(v.tensor_scalar(lg[:, 0:R], sg[:, 0:R], 0.15, 1.0, ALU.max, ALU.min))
            v.tensor_scalar(lg[:, R:], sg[:, 2 * R:2 * R + 1], 0.15, 1.0, ALU.max, ALU.min).then_inc(expos, 1)
            v.wait_ge(consts, 1)
            k.step(v.tensor_copy(expf[:], expo[:]))
            k.step(v.tensor_scalar(expf[:], expf[:], 1.0 - SUB, None, ALU.max))
            v.wait_ge(gammas, 2)
            k.step(v.tensor_tensor(kw[:], bc(expf[:, 0], 2, R), bc(lg[:, 0:R], 1, NSUB + 1), ALU.mult))
            v.tensor_tensor(qw[:], bc(expf[:, 1], 2, R), bc(lg[:, 0:R], 1, NSUB + 1), ALU.mult).then_inc(coef_ok, 1)
            k.step(v.tensor_scalar(gk[:], traw[:], sg[:, 2 * R + 1:], None, ALU.mult))
            k.step(v.tensor_scalar(band[:], taps[:, 0], gk[:, 0:1], None, ALU.mult))
            for t in range(1, KTAP):
                k.step(v.scalar_tensor_tensor(out=band[:], in0=taps[:, t], scalar=gk[:, t:t + 1], in1=band[:],
                                              op0=ALU.mult, op1=ALU.add))
            k.step(v.tensor_copy(qcat[:, :, 5, 0:KTAP - 1], bc(band[:, P:], 1, NT)))
            v.wait_ge(gammas, 5)
            k.step(v.tensor_tensor(coef[:], coef[:], lg[:, R:], ALU.mult))
            v.wait_ge(ld_uv, 48)
            for h in range(DH):
                v.tensor_scalar(uv[:, h], uv[:, h], cols[:, h:h + 1], None, ALU.mult).then_inc(uv_ok, 1)
            v.wait_ge(squares, NT)
            k.step(v.tensor_scalar(ss[:], ss[:], 1.0 / D, EPS_RMS, ALU.mult, ALU.add))
            rsqrt_steps(v, k, rs[:], ss[:], tmp[:, 0:NT])
            v.sem_inc(rs_ok, 1)
            v.wait_ge(masked, 1)
            k.step(v.tensor_tensor(qw[:], qw[:], bc(sg[:, R:2 * R], 1, NSUB + 1), ALU.mult))
            for g in range(2):
                ts, n = slice(g * NT // 2, (g + 1) * NT // 2), NT // 2
                ps = slice(g * NT, (g + 1) * NT)
                pairs = qk[:, ts].rearrange("p t a r -> p (t a) r")
                sq = qk_sq[:, ts].rearrange("p t a r -> p (t a) r")
                v.wait_ge(qk_mm, g + 1)
                k.step(v.tensor_tensor(pairs.rearrange("p (t a) r -> p t (a r)", a=2),
                                       bank[7 - g][:, 0:n * 2 * R].rearrange("p (t n) -> p t n", t=n),
                                       bc(rs[:, ts], 2, 2 * R), ALU.mult))
                k.step(v.tensor_tensor(sq, pairs, pairs, ALU.mult))
                k.step(v.tensor_reduce(qkn[:, ps], sq, AX_X, ALU.add))
                k.step(v.tensor_scalar(qkn[:, ps], qkn[:, ps], 1e-16, None, ALU.max))
                rsqrt_steps(v, k, qkr[:, ps], qkn[:, ps], tmp[:, ps])
                k.step(v.tensor_tensor(pairs, pairs, bc(qkr[:, ps], 2, R), ALU.mult))
                k.step(v.tensor_tensor(kcat[:, ts, 0:NSUB + 1, :], bc(qk[:, ts, 1], 2, NSUB + 1), bc(kw[:], 1, n), ALU.mult))
                v.tensor_tensor(qcat[:, ts, 0:NSUB + 1, :], bc(qk[:, ts, 0], 2, NSUB + 1), bc(qw[:], 1, n),
                                ALU.mult).then_inc(cats, 1)
            for t in range(NT + 1):
                if t < NT:
                    v.wait_ge(S_mm, t + 1)
                    if t >= 3:
                        v.wait_ge(o_mm, t - 2)
                    if t >= 1:
                        v.wait_ge(S_sb, t)
                    v.scalar_tensor_tensor(out=S[64:64 + R + KTAP - 1, (t + 1) % 4], in0=S[64:64 + R + KTAP - 1, t % 4],
                                           scalar=coef[64:64 + R + KTAP - 1, 0:1],
                                           in1=bank[6 + t % 2][64:64 + R + KTAP - 1, 0:D],
                                           op0=ALU.mult, op1=ALU.add).then_inc(S_sb, 1)
                if t >= 1:
                    v.wait_ge(A_mm, t)
                    if t >= 3:
                        v.wait_ge(o_mm, t - 2)
                    k.step(v.tensor_tensor(AT[:, (t - 1) % 2], bank[2 + (t - 1) % 2][:, 0:P], later[:], ALU.mult))
                    v.tensor_tensor(AT[:, (t - 1) % 2], AT[:, (t - 1) % 2], band[:, 0:P], ALU.add).then_inc(A_sb, 1)
            v.wait_ge(hi_w, 2)
            v.tensor_tensor(w1_lo[:].rearrange("p c f -> p (c f)"), w1_32[:],
                            w1_hi[:].bitcast(F32).rearrange("p c f -> p (c f)"), ALU.subtract).then_inc(w_lo_ok, 1)
            v.tensor_tensor(w2_lo[:].rearrange("p c f -> p (c f)"), w2_32,
                            w2_hi[:].bitcast(F32).rearrange("p c f -> p (c f)"), ALU.subtract).then_inc(w_lo_ok, 1)
            def add_residual(c):
                for t in range(c * TPC, (c + 1) * TPC):
                    v.wait_ge(h2_mm, t + 1)
                    v.wait_ge(xb_ok, t + 1)
                    v.tensor_tensor(h2[:, t], bank[PROJ_BANKS[t % 4]][:, 0:D], h2[:, t], ALU.add).then_inc(h2_sb, 1)

            def second_norm(c):
                sl = slice(c * TPC, (c + 1) * TPC)
                v.wait_ge(squares, NT + (c + 1) * TPC)
                k.step(v.tensor_scalar(ss[:, sl], ss[:, sl], 1.0 / D, EPS_RMS, ALU.mult, ALU.add))
                rsqrt_steps(v, k, rs[:, sl], ss[:, sl], tmp[:, 0:TPC])
                if c >= 2:
                    v.wait_ge(hT_mm, DH * (c - 1))
                for j in range(TPC):
                    t = c * TPC + j
                    v.tensor_scalar(n2[:, c % 2, j], h2[:, t], rs[:, t:t + 1], None, ALU.mult).then_inc(n2_ok, 1)

            add_residual(0)
            add_residual(1)
            second_norm(0)
            add_residual(2)
            add_residual(3)
            low_part(v, 0)
            second_norm(1)
            second_norm(2)
            low_part(v, 1)
            second_norm(3)
            for c in range(NC):
                for f in range(FT):
                    n = c * FT + f
                    v.wait_ge(gelu_ok, n + 1)
                    if c >= 1:
                        v.wait_ge(y_mm, TPC * c)
                    k.step(v.tensor_copy(g_hi[:, f], g32[:, f % 2]))
                    v.tensor_tensor(g_lo[:, f], g32[:, f % 2], g_hi[:, f].bitcast(F32), ALU.subtract).then_inc(g_ok, 1)
                    if f == 6 and c + 2 < NC:
                        low_part(v, c + 2)
                for t in range(c * TPC, (c + 1) * TPC):
                    v.wait_ge(y_mm, t + 1)
                    v.wait_ge(res_ok, t + 1)
                    v.tensor_tensor(hn[:, t], bank[t % 2][:, 0:D], hn[:, t], ALU.add).then_inc(z_ok, 1)
                    v.wait_ge(z_ok, t + 1)
                    k.step(v.bn_stats(stats[:, t], hn[:, t]))
                    k.step(v.bn_aggr(mv[:, t], stats[:, t]))
                sl = slice(c * TPC, (c + 1) * TPC)
                k.step(v.tensor_scalar(ss[:, sl], mv[:, sl, 1], EPS_LN, None, ALU.add))
                rsqrt_steps(v, k, rs[:, sl], ss[:, sl], tmp[:, 0:TPC])
                for t in range(c * TPC, (c + 1) * TPC):
                    last = v.tensor_scalar(h2[:, t], hn[:, t], mv[:, t, 0:1], rs[:, t:t + 1], ALU.subtract, ALU.mult)
                last.then_inc(x1_ok, 1)

        @block.tensor
        def _(pe):
            pe.wait_ge(ld_xT, 16)
            pe.wait_ge(uv_ok, 2)
            for g in range(2):
                for j in range(NT // 2):
                    for h in range(DH):
                        last = pe.matmul(bank[7 - g][:, j * 2 * R:(j + 1) * 2 * R], xT[:, h, tile(g * NT // 2 + j)], uv[:, h],
                                         start=(h == 0), stop=(h == DH - 1))
                last.then_inc(qk_mm, 1)
            pe.wait_ge(consts, 1)
            pe.wait_ge(cats, 1)
            for t in range(NT + 2):
                if t == 0:
                    pe.wait_ge(cats, 2)
                if t < NT:
                    if t >= 2:
                        pe.wait_ge(turned_sb, t - 1)
                    pe.transpose(bank[t % 2][0:96, 0:P], qcat[:, t].rearrange("p s r -> p (s r)"), ident[:])
                    pe.transpose(bank[t % 2][0:96, P:2 * P], kcat[:, t].rearrange("p s r -> p (s r)"),
                                 ident[:]).then_inc(turned, 1)
                    pe.wait_ge(hn_ok, t + 1)
                    if t >= 2:
                        pe.wait_ge(S_sb, t - 1)
                    pe.matmul(bank[6 + t % 2][64:64 + R + KTAP - 1, 0:D],
                              kcat[:, t].rearrange("p s r -> p (s r)")[:, 64:64 + R + KTAP - 1], hn[:, t],
                              start=True, stop=True).then_inc(S_mm, 1)
                if 1 <= t <= NT:
                    pe.wait_ge(turned_sb, t)
                    if t >= 3:
                        pe.wait_ge(A_sb, t - 2)
                    u = (t - 1) % 3
                    pe.matmul(bank[2 + (t - 1) % 2][:, 0:P], qkT[0:64, u, P:2 * P], qkT[0:64, u, 0:P],
                              start=True, stop=True).then_inc(A_mm, 1)
                if t >= 2:
                    u = t - 2
                    pe.wait_ge(A_sb, u + 1)
                    if u >= 1:
                        pe.wait_ge(S_sb, u)
                    if u >= 2:
                        pe.wait_ge(o_sb, u - 1)
                    for h in range(DH):
                        out = bank[4 + u % 2][:, h * P:(h + 1) * P]
                        pe.matmul(out, hn[:, u, h * P:(h + 1) * P], AT[:, u % 2], start=True, stop=False)
                        last = pe.matmul(out, S[64:64 + R + KTAP - 1, u % 4, h * P:(h + 1) * P],
                                         qkT[64:64 + R + KTAP - 1, u % 3, 0:P], start=False, stop=True)
                    last.then_inc(o_mm, 1)
            def project(c):
                for t in range(c * TPC, (c + 1) * TPC):
                    pe.wait_ge(o_sb, t + 1)
                    if t >= 4:
                        pe.wait_ge(h2_sb, t - 3)
                    for h in range(DH):
                        last = pe.matmul(bank[PROJ_BANKS[t % 4]][:, 0:D], oT[:, h, tile(t)], projT[:, h], start=(h == 0), stop=(h == DH - 1))
                    last.then_inc(h2_mm, 1)

            def turn_n2(c):
                if c >= 2:
                    pe.wait_ge(hT_lo_ok, DH * (c - 1))
                pe.wait_ge(n2_ok, (c + 1) * TPC)
                for h in range(DH):
                    for j in range(TPC):
                        last = pe.transpose(bank[2 + (c % 2) * 2 + h][:, j * P:(j + 1) * P],
                                            n2[:, c % 2, j, h * P:(h + 1) * P], ident[:])
                    last.then_inc(hT_mm, 1)

            def turn_x1(c):
                if c >= 2:
                    pe.wait_ge(x1_sb, DH * (c - 1))
                else:
                    pe.wait_ge(hT_lo_ok, DH * (c + 3))
                pe.wait_ge(x1_ok, c + 1)
                for h in range(DH):
                    for j in range(TPC):
                        last = pe.transpose(bank[2 + (c % 2) * 2 + h][:, j * P:(j + 1) * P],
                                            h2[:, c * TPC + j, h * P:(h + 1) * P], ident[:])
                    last.then_inc(x1_mm, 1)

            pe.wait_ge(S_sb, NT)
            for c in range(NC):
                project(c)
            pe.wait_ge(o_sb, NT)
            turn_n2(0)
            pe.wait_ge(h2_sb, NT)
            pe.wait_ge(w_lo_ok, 2)
            for c in range(NC):
                pe.wait_ge(hT_lo_ok, DH * (c + 1))
                for f in range(FT):
                    n = c * FT + f
                    if n >= 2:
                        pe.wait_ge(gelu_ok, n - 1)
                    fs = slice(f * P, (f + 1) * P)
                    for h in range(DH):
                        last = three_pass(pe, bank[6 + f % 2][:], w1_hi[:, h, fs], w1_lo[:, h, fs],
                                          hT_hi[:, h, chunk(c % 3)], hT_lo[:, h, chunk(c % 3)], h == 0, h == DH - 1)
                    last.then_inc(up_mm, 1)
                    if f == 1 and c == 0:
                        turn_n2(1)
                    if f == 4 and c + 2 < NC:
                        turn_n2(c + 2)
                    if f == 5 and c >= 2:
                        turn_x1(c - 2)
                for j in range(TPC):
                    t = c * TPC + j
                    if t >= 2:
                        pe.wait_ge(z_ok, t - 1)
                    for f in range(FT):
                        pe.wait_ge(g_ok, c * FT + f + 1)
                        last = three_pass(pe, bank[t % 2][:, 0:D], g_hi[:, f, j * P:(j + 1) * P], g_lo[:, f, j * P:(j + 1) * P],
                                          w2_hi[:, f], w2_lo[:, f], f == 0, f == FT - 1)
                    last.then_inc(y_mm, 1)
            turn_x1(NC - 2)
            turn_x1(NC - 1)


def cross_attention(nc, io, shared):
    ident, ones, sT = shared["ident"], shared["ones"], shared["sT"]
    HALF = T // 2
    G = 3 * D
    V_STEPS, v_steps = NC * (1 + RSQRT_STEPS) + MT * (NC + 2) + 2 + NC * DH * 2, []
    with ExitStack() as ctx:
        def sb(name, shape, dt=F32, stack=ctx):
            return stack.enter_context(nc.sbuf_tensor(name, shape, dt))

        def sem(name, stack=ctx):
            return stack.enter_context(nc.semaphore("x_" + name))

        psum = ctx.enter_context(nc.psum_tensor("x_psum", [P, 8, CH], F32))
        bank = [psum[:, i] for i in range(8)]

        w1 = shared["w1"] = nc.alloc_sbuf_tensor_at("w1", [P, NE, DH, F], F32, offset=-(-nc.sbuf_base // 32) * 32)
        kq_hi = sb("x_kq_hi", [P, DH, M], F32R)
        kq_lo = sb("x_kq_lo", [P, DH, M], F32R)
        v_hi = sb("x_v_hi", [P, MT, D], F32R)
        v_lo = sb("x_v_lo", [P, MT, D], F32R)
        E_beside = NE * DH * F // HALF - -(-2 * (DH * M + MT * D) // HALF)
        E_first = sb("x_E_first", [P, E_beside, HALF])
        sb("x_gap", [P, NE * DH * F - 2 * (DH * M + MT * D) - E_beside * HALF])
        wi_hi = sb("x_wi_hi", [P, DH, G], F32R)
        wi_lo = sb("x_wi_lo", [P, DH, G], F32R)
        wh_hi = sb("x_wh_hi", [P, DH, G], F32R)
        wh_lo = sb("x_wh_lo", [P, DH, G], F32R)
        rs16 = sb("x_rs16", [P, MT])
        bias = sb("x_bias", [P, 4 * DH])

        def hs(h):
            return slice(h * P, (h + 1) * P)

        def chunk(c):
            return slice(c * CH, (c + 1) * CH)

        sn_hi = sb("x_sn_hi", [P, DH, T], F32R)
        sn_lo = sb("x_sn_lo", [P, DH, T], F32R)
        diag = sb("x_diag", [P, 2, CH])
        st = sb("x_st", [P, 3, NT])

        (sq_ok, sum_ok, stat_mm, diag_ok, bc_mm, prod_ok, sn_hi_ok, sn_lo_ok, s_ok, vchain) = (
            sem(n) for n in ("sq_ok", "sum_ok", "stat_mm", "diag_ok", "bc_mm", "prod_ok", "sn_hi_ok", "sn_lo_ok", "s_ok", "vchain"))

        def factors(v, values, slot, counted, tiles):
            for j, t in enumerate(tiles):
                last = v.tensor_scalar(diag[:, slot, j * P:(j + 1) * P], ident[:], values[:, t:t + 1], None, ALU.mult)
            last.then_inc(counted, 1)

        class SlotNorm:

            def __init__(self, sq, u32, first=False):
                self.sq, self.u32, self.first = sq, u32, first

            def reused(self, c):
                return not (self.first and c < 2)

            def squares(self, act, g, c):
                if self.reused(c):
                    act.wait_ge(stat_mm, g - 1)
                act.activation(self.sq[c % 2], sT[:, :, chunk(c)], ACT.Square).then_inc(sq_ok, 1)

            def add_squares(self, pool, g, c):
                sq = self.sq[c % 2]
                pool.wait_ge(sq_ok, g + 1)
                pool.tensor_tensor(sq[:, 0], sq[:, 0], sq[:, 1], ALU.add).then_inc(sum_ok, 1)

            def square_sums(self, pe, g, c):
                pe.wait_ge(sum_ok, g + 1)
                if self.reused(c):
                    pe.wait_ge(diag_ok, g - 1)
                for j in range(TPC):
                    last = pe.matmul(bank[4 + c % 2][:, j:j + 1], self.sq[c % 2][:, 0, j * P:(j + 1) * P], ones[:, 0:1],
                                     start=True, stop=True)
                last.then_inc(stat_mm, 1)

            def rms(self, v, k, g, c):
                tiles = slice(c * TPC, (c + 1) * TPC)
                v.wait_ge(stat_mm, g + 1)
                k.step(v.tensor_scalar(st[:, 0, tiles], bank[4 + c % 2][:, 0:TPC], 1.0 / D, EPS_RMS, ALU.mult, ALU.add))
                rsqrt_steps(v, k, st[:, 1, tiles], st[:, 0, tiles], st[:, 2, tiles])
                if self.reused(c):
                    v.wait_ge(bc_mm, g - 1)
                factors(v, st[:, 1], c % 2, diag_ok, range(c * TPC, (c + 1) * TPC))

            def broadcast(self, pe, g, c):
                pe.wait_ge(diag_ok, g + 1)
                if self.reused(c):
                    pe.wait_ge(prod_ok, g - 1)
                pe.matmul(bank[6 + c % 2], ones[:], diag[:, c % 2], start=True, stop=True).then_inc(bc_mm, 1)

            def normed(self, v, g, c):
                v.wait_ge(bc_mm, g + 1)
                if self.reused(c):
                    v.wait_ge(sn_hi_ok, g - 1)
                    v.wait_ge(sn_lo_ok, g - 1)
                v.tensor_tensor(self.u32[c % 2], sT[:, :, chunk(c)], bc(bank[6 + c % 2], 1, DH), ALU.mult).then_inc(prod_ok, 1)

            def normed_hi(self, act, g, c):
                act.wait_ge(prod_ok, g + 1)
                act.activation(sn_hi[:, :, chunk(c)], self.u32[c % 2], ACT.Copy).then_inc(sn_hi_ok, 1)

            def normed_lo(self, v, g, c):
                v.wait_ge(sn_hi_ok, g + 1)
                v.tensor_tensor(sn_lo[:, :, chunk(c)], self.u32[c % 2], sn_hi[:, :, chunk(c)].bitcast(F32),
                                ALU.subtract).then_inc(sn_lo_ok, 1)

        with ExitStack() as pre:
            first_sq = sb("y_sq", [P, 2, DH, CH], stack=pre)
            first_u32 = sb("y_u32", [P, 2, DH, CH], stack=pre)
            first = SlotNorm([first_sq[:, i] for i in range(2)], [first_u32[:, i] for i in range(2)], first=True)
            dest = dict(kq_hi=kq_hi, kq_lo=kq_lo, v_hi=v_hi, v_lo=v_lo, wi_hi=wi_hi, wi_lo=wi_lo, wh_hi=wh_hi,
                        wh_lo=wh_lo, rs16=rs16, bias=bias, norm=first, st=st, s_ok=s_ok, prod_ok=prod_ok, vchain=vchain)
            prepare_context(nc, io, pre, bank, dest)

        E_rest = sb("x_E_rest", [P, MT - E_beside, HALF])
        E = [E_first[:, m] for m in range(E_beside)] + [E_rest[:, m] for m in range(MT - E_beside)]
        e = sb("x_e", [P, 2, HALF])
        p_hi = sb("x_p_hi", [P, 2, HALF], F32R)
        p_lo = sb("x_p_lo", [P, 2, HALF], F32R)
        acc = sb("x_acc", [P, T])
        rw = sb("x_rw", [P, NT])
        mx = sb("x_mx", [P, 2, NC + 2])
        inv = sb("x_inv", [P, MT, 3])
        room = E_rest[:].rearrange("p m (a n) -> p (m a) n", n=CH)
        gates = [room[:, 4 + 4 * i:8 + 4 * i] for i in range(2)]
        sq = [room[:, 12 + DH * i:12 + DH * (i + 1)] for i in range(2)]
        u32 = [room[:, 16 + DH * i:16 + DH * (i + 1)] for i in range(2)]
        U = [e[:, c].rearrange("p (h n) -> p h n", h=DH) for c in range(2)] + [room[:, DH * c:DH * (c + 1)] for c in range(2)]
        u_hi = [p_hi[:, i].rearrange("p (h n) -> p h n", h=DH) for i in range(2)]
        u_lo = [p_lo[:, i].rearrange("p (h n) -> p h n", h=DH) for i in range(2)]

        norm = SlotNorm(sq, u32)

        (score_mm, neg_ok, exp_ok, inv_ok, p_hi_ok, p_lo_ok, acc_ok, upd_mm) = (
            sem(n) for n in ("score_mm", "neg_ok", "exp_ok", "inv_ok", "p_hi_ok", "p_lo_ok", "acc_ok", "upd_mm"))
        (U_ok, s_hi_ok, s_lo_ok, row_mm, rdiag_ok, rbc_mm, u_ok, u_hi_ok, u_lo_ok) = (
            sem(n) for n in ("U_ok", "s_hi_ok", "s_lo_ok", "row_mm", "rdiag_ok", "rbc_mm", "u_ok", "u_hi_ok", "u_lo_ok"))
        (r_mm, z_mm, hn_mm, in_mm, r_ok, z_ok, hr_ok, arg_ok, n_ok) = (
            sem(n) for n in ("r_mm", "z_mm", "hn_mm", "in_mm", "r_ok", "z_ok", "hr_ok", "arg_ok", "n_ok"))

        GH = NC * DH
        Q = 2 * MT

        def turn(q):
            if q < MT - 1:
                return 0, q
            return {MT - 1: (1, 0), MT: (0, MT - 1)}.get(q, (1, q - MT))

        block = ctx.enter_context(nc.Block())

        @block.scalar
        def _(act):
            with act.Fori(0, ITERS) as it:
                def weights_hi(q):
                    half, m = turn(q)
                    n = MROWS[m]
                    src = e[0:n, m % 2] if half == 0 else E[m][0:n]
                    if q >= 2:
                        act.wait_ge(upd_mm, it * Q + q - 1)
                    act.activation(p_hi[0:n, q % 2], src, ACT.Copy, scale=inv[0:n, m, 2:3]).then_inc(p_hi_ok, 1)

                def slots_hi(c):
                    act.activation(sn_hi[:, :, chunk(c)], sT[:, :, chunk(c)], ACT.Copy).then_inc(s_hi_ok, 1)

                def take_updates(c):
                    b = 4 + DH * c if c < 2 else DH * (c - 2)
                    act.activation(U[c], psum[:, b:b + DH], ACT.Copy).then_inc(U_ok, 1)

                def updates_hi(c):
                    act.wait_ge(u_ok, it * NC + c + 1)
                    if c >= 2:
                        act.wait_ge(in_mm, it * GH + DH * (c - 1))
                    act.activation(u_hi[c % 2], U[c], ACT.Copy).then_inc(u_hi_ok, 1)

                act.wait_ge(s_ok, it * GH + 1)
                norm.squares(act, it * NC + NC - 1, NC - 1)
                norm.normed_hi(act, it * NC + NC - 1, NC - 1)
                for m in range(MT):
                    n = MROWS[m]
                    if m == MT - 1:
                        weights_hi(MT - 1)
                    act.wait_ge(neg_ok, it * MT + m + 1)
                    if m == 0:
                        act.wait_ge(sn_lo_ok, it * NC + NC)
                    for half in range(2):
                        if half == 0 and m >= 2:
                            act.wait_ge(acc_ok, it * MT * NC + (m - 2) * NC + 2)
                            act.wait_ge(p_lo_ok, it * Q + m - 1)
                        out = e[0:n, m % 2] if half == 0 else E[m][0:n]
                        act.activation(out, psum[0:n, 2 * half:2 * half + 2].rearrange("p a n -> p (a n)"), ACT.Exp,
                                       bias=inv[0:n, m, 0:1], scale=rs16[0:n, m:m + 1],
                                       accum_out=mx[0:n, m % 2, NC + half:NC + half + 1]).then_inc(exp_ok, 1)
                    act.wait_ge(inv_ok, it * MT + m + 1)
                    weights_hi(m if m < MT - 1 else MT)
                for m in range(1, MT):
                    weights_hi(MT + m)
                    if m == 2:
                        act.wait_ge(upd_mm, it * Q + MT + 1)
                        act.wait_ge(acc_ok, (it + 1) * MT * NC)
                        act.wait_ge(p_lo_ok, it * Q + MT + 1)
                    if 2 <= m < 4:
                        take_updates(m - 2)
                    elif 4 <= m < 4 + NC:
                        slots_hi(m - 4)
                act.wait_ge(upd_mm, (it + 1) * Q)
                act.wait_ge(p_lo_ok, (it + 1) * Q)
                take_updates(2)
                take_updates(3)
                updates_hi(0)
                for c in range(NC):
                    after = (it + 1) * NC + c - 1
                    if c + 1 < NC:
                        updates_hi(c + 1)
                    if c >= 1:
                        act.wait_ge(s_ok, it * GH + DH * c + 1)
                        norm.squares(act, after, c - 1)
                    for h in range(DH):
                        i = c * DH + h
                        r, z, arg, new = (gates[i % 2][:, j] for j in range(4))
                        act.wait_ge(r_mm, it * GH + i + 1)
                        if i >= 2:
                            act.wait_ge(s_ok, it * GH + i)
                        act.activation(r, bank[1], ACT.Sigmoid, bias=bias[:, h:h + 1]).then_inc(r_ok, 1)
                        if c >= 1 and h == 1:
                            norm.normed_hi(act, after, c - 1)
                        act.wait_ge(z_mm, it * GH + i + 1)
                        act.activation(z, bank[2], ACT.Sigmoid, bias=bias[:, DH + h:DH + h + 1]).then_inc(z_ok, 1)
                        act.wait_ge(arg_ok, it * GH + i + 1)
                        act.activation(new, arg, ACT.Tanh, bias=bias[:, 2 * DH + h:2 * DH + h + 1]).then_inc(n_ok, 1)

        @block.vector
        def _(v):
            with v.Fori(0, ITERS) as it:
                k = Chain(v, vchain, it * V_STEPS + dest["steps"])

                def add_weights(m, c):
                    n = MROWS[m]
                    src = e[0:n, m % 2, chunk(c)] if c < 2 else E[m][0:n, chunk(c - 2)]
                    if m == 0:
                        v.tensor_scalar(acc[0:n, chunk(c)], src, inv[0:n, m, 2:3], None, ALU.mult).then_inc(acc_ok, 1)
                    else:
                        v.wait_ge(acc_ok, it * MT * NC + (m - 1) * NC + c + 1)
                        v.scalar_tensor_tensor(out=acc[0:n, chunk(c)], in0=src, scalar=inv[0:n, m, 2:3],
                                               in1=acc[0:n, chunk(c)], op0=ALU.mult, op1=ALU.add).then_inc(acc_ok, 1)

                def weights_lo(q):
                    half, m = turn(q)
                    n = MROWS[m]
                    src = e[0:n, m % 2] if half == 0 else E[m][0:n]
                    v.wait_ge(p_hi_ok, it * Q + q + 1)
                    if q >= 2:
                        v.wait_ge(upd_mm, it * Q + q - 1)
                    v.scalar_tensor_tensor(out=p_lo[0:n, q % 2], in0=src, scalar=inv[0:n, m, 2:3],
                                           in1=p_hi[0:n, q % 2].bitcast(F32), op0=ALU.mult,
                                           op1=ALU.subtract).then_inc(p_lo_ok, 1)

                norm.rms(v, k, it * NC + NC - 1, NC - 1)
                for m in range(MT):
                    n = MROWS[m]
                    for c in range(NC):
                        if m == 0 and c == 1:
                            norm.normed(v, it * NC + NC - 1, NC - 1)
                        if m == 0 and c == 2:
                            norm.normed_lo(v, it * NC + NC - 1, NC - 1)
                        v.wait_ge(score_mm, it * MT * NC + m * NC + c + 1)
                        mark = k.mark(v.tensor_reduce(mx[0:n, m % 2, c:c + 1], bank[c][0:n], AX_X, ALU.max))
                        if c == 0 and m >= 1:
                            weights_lo(m - 1)
                        if c == 1 and m == MT - 1:
                            weights_lo(MT - 1)
                    v.wait_ge(vchain, mark)
                    k.step(v.tensor_reduce(inv[0:n, m, 0:1], mx[0:n, m % 2, 0:NC], AX_X, ALU.max))
                    v.tensor_scalar(inv[0:n, m, 0:1], inv[0:n, m, 0:1], rs16[0:n, m:m + 1], -1.0,
                                    ALU.mult, ALU.mult).then_inc(neg_ok, 1)
                    if m >= 1:
                        for c in range(NC):
                            add_weights(m - 1, c)
                    v.wait_ge(exp_ok, it * Q + 2 * m + 2)
                    k.step(v.tensor_tensor(inv[0:n, m, 1:2], mx[0:n, m % 2, NC:NC + 1], mx[0:n, m % 2, NC + 1:NC + 2], ALU.add))
                    v.reciprocal(inv[0:n, m, 2:3], inv[0:n, m, 1:2]).then_inc(inv_ok, 1)
                weights_lo(MT)

                def norm_updates(c):
                    v.wait_ge(U_ok, it * NC + c + 1)
                    v.wait_ge(rbc_mm, it * NC + c + 1)
                    v.tensor_tensor(U[c], U[c], bc(bank[4 + c], 1, DH), ALU.mult).then_inc(u_ok, 1)

                def slots_lo(c):
                    v.wait_ge(s_hi_ok, it * NC + c + 1)
                    v.tensor_tensor(sn_lo[:, :, chunk(c)], sT[:, :, chunk(c)], sn_hi[:, :, chunk(c)].bitcast(F32),
                                    ALU.subtract).then_inc(s_lo_ok, 1)

                for m in range(1, MT):
                    weights_lo(MT + m)
                    if m == 1:
                        for c in range(NC):
                            add_weights(MT - 1, c)
                    if 4 <= m < 4 + NC:
                        slots_lo(m - 4)
                    if m == 7:
                        v.wait_ge(row_mm, it + 1)
                        k.step(v.tensor_scalar(rw[:], bank[4][:, 0:NT], EPS_RMS, None, ALU.add))
                        k.step(v.reciprocal(rw[:], rw[:]))
                        factors(v, rw, 0, rdiag_ok, range(0, TPC))
                    if m in (8, 10, 11):
                        c = {8: 1, 10: 2, 11: 3}[m]
                        if c >= 2:
                            v.wait_ge(rbc_mm, it * NC + c - 1)
                        factors(v, rw, c % 2, rdiag_ok, range(c * TPC, (c + 1) * TPC))
                    if m in (11, 12):
                        norm_updates(m - 11)

                def updates_lo(c):
                    v.wait_ge(u_hi_ok, it * NC + c + 1)
                    v.tensor_tensor(u_lo[c % 2], U[c], u_hi[c % 2].bitcast(F32), ALU.subtract).then_inc(u_lo_ok, 1)

                updates_lo(0)
                norm_updates(2)
                norm_updates(3)
                for c in range(NC):
                    after = (it + 1) * NC + c - 1
                    if c + 1 < NC:
                        updates_lo(c + 1)
                    for h in range(DH):
                        i = c * DH + h
                        r, z, arg, new = (gates[i % 2][:, j] for j in range(4))
                        s = sT[:, h, chunk(c)]
                        v.wait_ge(hn_mm, it * GH + i + 1)
                        v.wait_ge(r_ok, it * GH + i + 1)
                        v.scalar_tensor_tensor(out=arg, in0=bank[0], scalar=bias[:, 3 * DH + h:3 * DH + h + 1], in1=r,
                                               op0=ALU.add, op1=ALU.mult).then_inc(hr_ok, 1)
                        if c >= 1 and h == 1:
                            norm.normed_lo(v, after, c - 1)
                        if c >= 1 and h == 0:
                            norm.rms(v, k, after, c - 1)
                        v.wait_ge(hr_ok, it * GH + i + 1)
                        v.wait_ge(in_mm, it * GH + i + 1)
                        v.tensor_tensor(arg, arg, bank[3], ALU.add).then_inc(arg_ok, 1)
                        v.wait_ge(n_ok, it * GH + i + 1)
                        k.step(v.tensor_tensor(s, s, new, ALU.subtract))
                        k.step(v.tensor_tensor(s, s, z, ALU.mult))
                        v.tensor_tensor(s, s, new, ALU.add).then_inc(s_ok, 1)
                        if c >= 1 and h == 0:
                            norm.normed(v, after, c - 1)
                v_steps.append(k.n)

        @block.sync
        def _(sp):
            sp.wait_ge(upd_mm, ITERS * Q)
            sp.wait_ge(p_lo_ok, ITERS * Q)
            sp.wait_ge(acc_ok, ITERS * MT * NC)
            for e in range(NE):
                sp.dma_start(w1[:, e], io["w1"][e].rearrange("(c p) f -> p c f", p=P)).then_inc(shared["ld_e"], 16)

        @block.gpsimd
        def _(pool):
            with pool.Fori(0, ITERS) as it:
                norm.add_squares(pool, it * NC + NC - 1, NC - 1)
                for c in range(NC - 1):
                    norm.add_squares(pool, (it + 1) * NC + c, c)

        @block.tensor
        def _(pe):
            with pe.Fori(0, ITERS) as it:
                def update(q):
                    half, m = turn(q)
                    n = MROWS[m]
                    pe.wait_ge(p_lo_ok, it * Q + q + 1)
                    for c in range(2):
                        for h in range(DH):
                            b = (4 if half == 0 else 0) + DH * c + h
                            last = three_pass(pe, bank[b], v_hi[0:n, m, hs(h)], v_lo[0:n, m, hs(h)],
                                              p_hi[0:n, q % 2, chunk(c)], p_lo[0:n, q % 2, chunk(c)], m == 0, m == MT - 1)
                    last.then_inc(upd_mm, 1)

                for m in range(MT):
                    n = MROWS[m]
                    ks = slice(m * P, m * P + n)
                    for c in range(NC):
                        if m == 0:
                            if c == 1:
                                norm.square_sums(pe, it * NC + NC - 1, NC - 1)
                            if c == 2:
                                norm.broadcast(pe, it * NC + NC - 1, NC - 1)
                            pe.wait_ge(sn_lo_ok, it * NC + c + 1)
                        elif c % 2 == 0:
                            pe.wait_ge(exp_ok, it * Q + 2 * (m - 1) + c // 2 + 1)
                        for h in range(DH):
                            last = three_pass(pe, bank[c][0:n], kq_hi[:, h, ks], kq_lo[:, h, ks],
                                              sn_hi[:, h, chunk(c)], sn_lo[:, h, chunk(c)], h == 0, h == DH - 1)
                        last.then_inc(score_mm, 1)
                    if m >= 1:
                        update(m - 1)
                pe.wait_ge(exp_ok, (it + 1) * Q)
                update(MT - 1)
                update(MT)

                def row_broadcast(c):
                    pe.wait_ge(rdiag_ok, it * NC + c + 1)
                    pe.matmul(bank[4 + c], ones[:], diag[:, c % 2], start=True, stop=True).then_inc(rbc_mm, 1)

                for m in range(1, MT):
                    update(MT + m)
                    if m == 5:
                        pe.wait_ge(acc_ok, (it + 1) * MT * NC)
                        pe.wait_ge(U_ok, it * NC + 2)
                        for t in range(NT):
                            last = pe.matmul(bank[4][:, t:t + 1], acc[:, t * P:(t + 1) * P], ones[:, 0:1], start=True, stop=True)
                        last.then_inc(row_mm, 1)
                    if m in (8, 9, 11, 12):
                        row_broadcast((8, 9, 11, 12).index(m))

                def gate(b, e_from, h, c, parts, counted):
                    cols = slice(e_from * D + h * P, e_from * D + (h + 1) * P)
                    slots = [(wh_hi, wh_lo, sn_hi[:, k, chunk(c)], sn_lo[:, k, chunk(c)], k) for k in range(DH)]
                    updates = [(wi_hi, wi_lo, u_hi[c % 2][:, k], u_lo[c % 2][:, k], k) for k in range(DH)]
                    steps = slots * ("s" in parts) + updates * ("u" in parts)
                    for i, (w_hi, w_lo, x_hi, x_lo, k) in enumerate(steps):
                        if x_hi is updates[0][2]:
                            pe.wait_ge(u_lo_ok, it * NC + c + 1)
                        last = three_pass(pe, bank[b], w_hi[:, k, cols], w_lo[:, k, cols], x_hi, x_lo,
                                          i == 0, i == len(steps) - 1)
                    last.then_inc(counted, 1)

                for c in range(NC):
                    after = (it + 1) * NC + c - 1
                    pe.wait_ge(s_lo_ok, it * NC + c + 1)
                    for h in range(DH):
                        i = c * DH + h
                        if i == 0:
                            pe.wait_ge(U_ok, (it + 1) * NC)
                        else:
                            pe.wait_ge(hr_ok, it * GH + i)
                        gate(0, 2, h, c, "s", hn_mm)
                        if i > 0:
                            pe.wait_ge(r_ok, it * GH + i)
                        gate(1, 0, h, c, "su", r_mm)
                        if c >= 1 and h == 1:
                            norm.broadcast(pe, after, c - 1)
                        if i > 0:
                            pe.wait_ge(z_ok, it * GH + i)
                        gate(2, 1, h, c, "su", z_mm)
                        if c >= 1 and h == 0:
                            norm.square_sums(pe, after, c - 1)
                        if i > 0:
                            pe.wait_ge(arg_ok, it * GH + i)
                        gate(3, 2, h, c, "u", in_mm)
                pe.wait_ge(z_ok, (it + 1) * GH)
                pe.wait_ge(arg_ok, (it + 1) * GH)

    assert v_steps == [V_STEPS], v_steps


def prepare_context(nc, io, ctx, bank, dest):
    kq_hi, kq_lo, v_hi, v_lo = (dest[n] for n in ("kq_hi", "kq_lo", "v_hi", "v_lo"))
    wi_hi, wi_lo, wh_hi, wh_lo, rs16, bias = (dest[n] for n in ("wi_hi", "wi_lo", "wh_hi", "wh_lo", "rs16", "bias"))
    G = 3 * D

    def sb(name, shape, dt=F32):
        return ctx.enter_context(nc.sbuf_tensor("y_" + name, shape, dt))

    def sem(name):
        return ctx.enter_context(nc.semaphore("y_" + name))

    cx = sb("cx", [P, MT, D])
    cxT = sb("cxT", [P, DH, M])
    v32 = sb("v32", [P, MT, D])
    wq, wk, wv = (sb(n, [P, DH, D]) for n in ("wq", "wk", "wv"))
    wiT = sb("wiT", [P, DH, G])
    whT = sb("whT", [P, DH, G])
    wkq = sb("wkq", [P, DH, D])
    cols = sb("cols", [P, 2 * DH])
    bi = sb("bi", [P, 2 * 3 * DH])
    junk = sb("junk", [P, 2, D])
    ss, rs, tmp = sb("ss", [P, MT]), sb("rs", [P, MT]), sb("tmp", [P, MT])
    ld_w, ld_c, ld_cT, ld_g, zeroed = sem("ld_w"), sem("ld_c"), sem("ld_cT"), sem("ld_g"), sem("zeroed")
    squares, v32_ok, v_hi_ok = sem("squares"), sem("v32_ok"), sem("v_hi_ok")
    norm, st, s_ok, prod_ok, vchain = (dest[n] for n in ("norm", "st", "s_ok", "prod_ok", "vchain"))
    FIRST = NC - 1
    KEY_BANKS, DEEP = (2, 3, 0, 1), 4
    VG = (slice(0, 8), slice(8, MT))
    wkq_mm, wkq_ok, kq_mm, kq_hi_ok, kq_lo_ok = (sem(n) for n in ("wkq_mm", "wkq_ok", "kq_mm", "kq_hi_ok", "kq_lo_ok"))
    wi_mm, wi_hi_ok, wi_lo_ok, wh_hi_ok, wh_lo_ok = sem("wi_mm"), sem("wi_hi_ok"), sem("wi_lo_ok"), sem("wh_hi_ok"), sem("wh_lo_ok")
    FULL = MT - 1
    keys = [(h, c) for c in range(-(-M // CH)) for h in range(DH)]
    gru = [(h, n0, min(CH, G - n0)) for h in range(DH) for n0 in range(0, G, CH)]

    with nc.Block() as block:
        @block.sync
        def _(sp):
            for t, name in ((wq, "Wq"), (wk, "Wk"), (wv, "Wv")):
                sp.dma_start(t[:], io[name].rearrange("(c p) f -> p c f", p=P)).then_inc(ld_w, 16)
            sp.dma_start(cols[:], io["x_cols"]).then_inc(ld_w, 16)
            sp.dma_start(cxT[:], io["ctxT"].rearrange("(c p) t -> p c t", p=P)).then_inc(ld_cT, 16)
            sp.wait_ge(zeroed, 1)
            sp.dma_start(cx[:, 0:FULL], io["ctx"][0:FULL * P].rearrange("(t p) d -> p t d", p=P)).then_inc(ld_c, 16)
            sp.dma_start(cx[0:MROWS[-1], FULL], io["ctx"][FULL * P:]).then_inc(ld_c, 16)
            sp.dma_start(wiT[:], io["gru_wiT"].rearrange("(c p) f -> p c f", p=P)).then_inc(ld_g, 16)
            sp.dma_start(whT[:], io["gru_whT"].rearrange("(c p) f -> p c f", p=P)).then_inc(ld_g, 16)
            sp.dma_start(bi[:], io["gru_cols"]).then_inc(ld_g, 16)

        @block.gpsimd
        def _(pool):
            for c in range(FIRST):
                norm.add_squares(pool, c, c)
            pool.wait_ge(wh_hi_ok, 1)
            pool.tensor_tensor(wh_lo[:], whT[:], wh_hi[:].bitcast(F32), ALU.subtract).then_inc(wh_lo_ok, 1)
            pool.wait_ge(v_hi_ok, 2)
            pool.tensor_tensor(v_lo[:, VG[1]], v32[:, VG[1]], v_hi[:, VG[1]].bitcast(F32), ALU.subtract).then_inc(wh_lo_ok, 1)
            pool.wait_ge(wh_lo_ok, 2)

        @block.scalar
        def _(act):
            norm.squares(act, 0, 0)
            norm.squares(act, 1, 1)
            norm.normed_hi(act, 0, 0)
            norm.squares(act, 2, 2)

            def keys_hi(i):
                h, c = keys[i]
                n = min(CH, M - c * CH)
                act.wait_ge(kq_mm, i + 1)
                act.activation(kq_hi[:, h, c * CH:c * CH + n], bank[KEY_BANKS[i % DEEP]][:, 0:n], ACT.Copy,
                               scale=cols[:, DH + h:DH + h + 1]).then_inc(kq_hi_ok, 1)

            keys_hi(0)
            norm.normed_hi(act, 1, 1)
            keys_hi(1)
            act.wait_ge(ld_c, 32)
            for m in range(MT):
                if m >= 2:
                    act.wait_ge(squares, m - 1)
                act.activation(junk[:, m % 2], cx[:, m], ACT.Square, accum_out=ss[:, m:m + 1]).then_inc(squares, 1)
            keys_hi(2)
            norm.normed_hi(act, 2, 2)
            keys_hi(3)
            for i in range(4, len(keys)):
                keys_hi(i)
            act.wait_ge(ld_g, 48)
            act.activation(wh_hi[:], whT[:], ACT.Copy).then_inc(wh_hi_ok, 1)
            act.wait_ge(v32_ok, MT)
            for g in range(2):
                act.activation(v_hi[:, VG[g]], v32[:, VG[g]], ACT.Copy).then_inc(v_hi_ok, 1)
            for i, (h, n0, n) in enumerate(gru):
                act.wait_ge(wi_mm, i + 1)
                act.activation(wi_hi[:, h, n0:n0 + n], bank[4 + i][:, 0:n], ACT.Copy,
                               scale=cols[:, h:h + 1]).then_inc(wi_hi_ok, 1)

        @block.vector
        def _(v):
            k = Chain(v, vchain)
            v.memset(cx[:, FULL], 0.0).then_inc(zeroed, 1)
            v.memset(st[:], 0.0).then_inc(s_ok, 1)
            v.wait_ge(s_ok, 1)
            norm.rms(v, k, 0, 0)
            norm.rms(v, k, 1, 1)
            v.wait_ge(ld_w, 64)
            for h in range(DH):
                v.wait_ge(wkq_mm, h + 1)
                v.tensor_scalar(wkq[:, h], bank[h][:, 0:D], cols[:, h:h + 1], None, ALU.mult).then_inc(wkq_ok, 1)

            def keys_lo(i):
                h, c = keys[i]
                n = min(CH, M - c * CH)
                v.wait_ge(kq_hi_ok, i + 1)
                v.scalar_tensor_tensor(out=kq_lo[:, h, c * CH:c * CH + n], in0=bank[KEY_BANKS[i % DEEP]][:, 0:n],
                                       scalar=cols[:, DH + h:DH + h + 1],
                                       in1=kq_hi[:, h, c * CH:c * CH + n].bitcast(F32),
                                       op0=ALU.mult, op1=ALU.subtract).then_inc(kq_lo_ok, 1)

            norm.normed(v, 0, 0)
            norm.normed_lo(v, 0, 0)
            norm.rms(v, k, 2, 2)
            keys_lo(0)
            norm.normed(v, 1, 1)
            norm.normed_lo(v, 1, 1)
            keys_lo(1)
            keys_lo(2)
            norm.normed(v, 2, 2)
            norm.normed_lo(v, 2, 2)
            keys_lo(3)
            v.wait_ge(squares, MT)
            k.step(v.tensor_scalar(ss[:], ss[:], 1.0 / D, EPS_RMS, ALU.mult, ALU.add))
            rsqrt_steps(v, k, rs[:], ss[:], tmp[:])
            for m in range(MT):
                v.tensor_scalar(v32[:, m], cx[:, m], rs[:, m:m + 1], None, ALU.mult).then_inc(v32_ok, 1)
            k.step(v.tensor_scalar(rs16[:], rs[:], float(D) ** -0.5, None, ALU.mult))
            for i in range(4, len(keys)):
                keys_lo(i)
            v.wait_ge(v_hi_ok, 1)
            k.mark(v.tensor_tensor(v_lo[:, VG[0]], v32[:, VG[0]], v_hi[:, VG[0]].bitcast(F32), ALU.subtract))
            for i, (h, n0, n) in enumerate(gru):
                v.wait_ge(wi_hi_ok, i + 1)
                v.scalar_tensor_tensor(out=wi_lo[:, h, n0:n0 + n], in0=bank[4 + i][:, 0:n], scalar=cols[:, h:h + 1],
                                       in1=wi_hi[:, h, n0:n0 + n].bitcast(F32), op0=ALU.mult,
                                       op1=ALU.subtract).then_inc(wi_lo_ok, 1)
            k.mark(v.tensor_tensor(bias[:, 0:2 * DH], bi[:, 0:2 * DH], bi[:, 3 * DH:5 * DH], ALU.add))
            k.mark(v.tensor_copy(bias[:, 2 * DH:3 * DH], bi[:, 2 * DH:3 * DH]))
            k.step(v.tensor_copy(bias[:, 3 * DH:], bi[:, 5 * DH:]))
            dest["steps"] = k.n

        @block.tensor
        def _(pe):
            norm.square_sums(pe, 0, 0)
            norm.square_sums(pe, 1, 1)
            pe.wait_ge(ld_w, 64)
            for h in range(DH):
                for k in range(DH):
                    last = pe.matmul(bank[h][:, 0:D], wk[:, k, h * P:(h + 1) * P], wq[:, k], start=(k == 0), stop=(k == DH - 1))
                last.then_inc(wkq_mm, 1)
            norm.broadcast(pe, 0, 0)
            norm.square_sums(pe, 2, 2)
            pe.wait_ge(wkq_ok, DH)
            pe.wait_ge(ld_cT, 16)
            for i, (h, c) in enumerate(keys):
                if i == 1 or i == 3:
                    norm.broadcast(pe, (i + 1) // 2, (i + 1) // 2)
                n = min(CH, M - c * CH)
                if i >= DEEP:
                    pe.wait_ge(kq_lo_ok, i - DEEP + 1)
                for k in range(DH):
                    last = pe.matmul(bank[KEY_BANKS[i % DEEP]][:, 0:n], wkq[:, k, h * P:(h + 1) * P], cxT[:, k, c * CH:c * CH + n],
                                     start=(k == 0), stop=(k == DH - 1))
                last.then_inc(kq_mm, 1)
            pe.wait_ge(ld_g, 48)
            pe.wait_ge(prod_ok, FIRST)
            for i, (h, n0, n) in enumerate(gru):
                for k in range(DH):
                    last = pe.matmul(bank[4 + i][:, 0:n], wv[:, k, h * P:(h + 1) * P], wiT[:, k, n0:n0 + n],
                                     start=(k == 0), stop=(k == DH - 1))
                last.then_inc(wi_mm, 1)


SLOTS = 256
SH = SLOTS // P
TOP = 2
TILES = T * TOP // SLOTS + NE - 1
ROWS = TILES * SLOTS
PLACES = ROWS // P
assert PLACES <= P
SHIFT = SLOTS.bit_length() - 1


def layer_norm_factors(v, k, tiles, z, stats, mv, rs, tmp, nb, counted):
    sl = slice(tiles[0], tiles[-1] + 1)
    for t in tiles:
        mark = k.mark(v.bn_stats(stats[:, t], z[:, t]))
    v.wait_ge(k.sem, mark)
    for t in tiles:
        mark = k.mark(v.bn_aggr(mv[:, t], stats[:, t]))
    v.wait_ge(k.sem, mark)
    k.step(v.tensor_scalar(nb[:, sl], mv[:, sl, 1], EPS_LN, None, ALU.add))
    rsqrt_steps(v, k, rs[:, sl], nb[:, sl], tmp[:, sl])
    v.scalar_tensor_tensor(out=nb[:, sl], in0=mv[:, sl, 0], scalar=-1.0, in1=rs[:, sl], op0=ALU.mult,
                           op1=ALU.mult).then_inc(counted, 1)


def route(nc, io, shared):
    ident, ones, sT = shared["ident"], shared["ones"], shared["sT"]
    emap, token_of, row_of, gate = shared["emap"], shared["token_of"], shared["row_of"], shared["gate"]
    w2, b1, b2, ld_e = (shared[n] for n in ("w2", "b1", "b2", "ld_e"))
    KT = TOP * NT

    def quarter(g):
        return slice(g * KT // 4, (g + 1) * KT // 4)

    with ExitStack() as ctx:
        def sb(name, shape, dt=F32):
            return ctx.enter_context(nc.sbuf_tensor("r_" + name, shape, dt))

        def sem(name):
            return ctx.enter_context(nc.semaphore("r_" + name))

        bank = [ctx.enter_context(nc.psum_tensor(f"r_bank{i}", [P, CH], F32)) for i in range(8)]
        TURN_BANKS = (0, 1, 6, 7)
        x2 = sb("x2", [P, NT, D])
        x2T = sb("x2T", [P, 4, DH, P])
        stats, mv = sb("stats", [P, NT, 6]), sb("mv", [P, NT, 2])
        nb, rs, tmp = sb("nb", [P, NT]), sb("rs", [P, NT]), sb("tmp", [P, NT])
        rw = sb("rw", [P, DH, NE])
        rb = sb("rb", [P, 2, NE])
        tri = sb("tri", [P, P])
        earlier_i = sb("earlier_i", [P, NE], I32)
        tile_no = sb("tile_no", [P, TILES], I32)
        lane_i = sb("lane_i", [P, P], I32)
        row_i = sb("row_i", [P, TOP, NT], I32)
        spare_i = sb("spare_i", [P, PLACES], I32)
        earlier, tile_f, lane, row, spare = (sb(n, t.shape) for n, t in (
            ("earlier", earlier_i), ("tile_f", tile_no), ("lane", lane_i), ("row", row_i), ("spare", spare_i)))
        lg = sb("lg", [P, NT, NE])
        warm = sb("warm", [P, 1])
        red = sb("red", [P, NT])
        pr = sb("pr", [P, NT, NE])
        left = sb("left", [P, NT, NE])
        equal = sb("equal", [P, NT, NE])
        chosen = [sb(f"chosen{k}", [P, NT, NE]) for k in range(TOP)]
        sel = sb("sel", [P, NT, NE])
        place = sb("place", [P, NT, NE])
        cum = sb("cum", [P, 2, NT + NT // 2, NE])
        end = sb("end", [P, 2, NE + NE // 2])
        cnt = sb("cnt", [P, NE], I32)
        ntile, start = sb("ntile", [P, NE]), sb("start", [P, NE])
        emf = sb("emf", [P, TILES, NE])
        emr = sb("emr", [P, TILES])
        pf = sb("pf", [P, TOP, NT])
        pi, hi_i, lo_i = (sb(n, [P, KT], I32) for n in ("pi", "hi_i", "lo_i"))
        hi_f, lo_f = sb("hi_f", [P, KT]), sb("lo_f", [P, KT])
        lane_is = sb("lane_is", [P, 4, KT // 4, P], F32R)
        in_column = sb("in_column", [P, KT, PLACES])
        column_is = sb("column_is", [P, KT, PLACES], F32R)
        found, empty = sb("found", [P, PLACES]), sb("empty", [P, PLACES])
        found_i = sb("found_i", [P, PLACES], I32)

        loaded = shared["loaded"]
        ld_r, consts, gchain, vchain = (sem(n) for n in ("ld_r", "consts", "gchain", "vchain"))
        turn_mm, z_ok, norm_ok, x2_ok, x2T_mm, x2T_ok, lg_mm, sub_ok, exp_ok = (
            sem(n) for n in ("turn_mm", "z_ok", "norm_ok", "x2_ok", "x2T_mm", "x2T_ok", "lg_mm", "sub_ok", "exp_ok"))
        sel_ok, pos_mm, in_column_ok, column_ok, lane_ok, found_mm, kept = (
            sem(n) for n in ("sel_ok", "pos_mm", "in_column_ok", "column_ok", "lane_ok", "found_mm", "kept"))

        block = ctx.enter_context(nc.Block())

        @block.sync
        def _(sp):
            x1 = io["x1"].rearrange("(t p) d -> p t d", p=P)
            for c in range(NC):
                ts = slice(c * TPC, (c + 1) * TPC)
                sp.dma_start(x2[:, ts], x1[:, ts]).then_inc(loaded[c], 16)
            sp.dma_start(rw[:], io["router_w"].rearrange("(c p) e -> p c e", p=P)).then_inc(ld_r, 16)
            sp.dma_start(rb[:, 0], io["router_b"].partition_broadcast(P)).then_inc(ld_r, 16)
            sp.dma_start(rb[:, 1], io["expert_bias"].partition_broadcast(P)).then_inc(ld_r, 16)
            sp.dma_start(b1[:], io["b1_cols"]).then_inc(ld_e, 16)
            sp.dma_start(b2[:], io["b2"].rearrange("e d -> (e d)").partition_broadcast(P)).then_inc(ld_e, 16)
            for e in range(NE):
                sp.dma_start(w2[:, e], io["w2"][e].rearrange("(c p) f -> p c f", p=P)).then_inc(ld_e, 16)
            sp.wait_ge(x2_ok, NT)
            sp.dma_start(io["x2"].rearrange("(t p) d -> p t d", p=P), x2[:]).then_inc(kept, 16)
            sp.wait_ge(kept, 16)

        @block.gpsimd
        def _(pool):
            g = Chain(pool, gchain)
            g.step(pool.memset(tri[:], 1.0))
            g.step(pool.affine_select(out=tri[:], in_=tri[:], compare_op=ALU.is_ge, fill=0.0,
                                      base=-1, pattern=[[1, P]], channel_multiplier=-1))
            pool.iota(tile_no[:], pattern=[[1, TILES]], base=0, channel_multiplier=0).then_inc(consts, 1)
            pool.iota(earlier_i[:], pattern=[[-1, NE]], base=NE, channel_multiplier=0).then_inc(consts, 1)
            pool.iota(lane_i[:], pattern=[[1, P]], base=0, channel_multiplier=0).then_inc(consts, 1)
            pool.iota(row_i[:], pattern=[[T, TOP], [P, NT]], base=1, channel_multiplier=1).then_inc(consts, 1)
            pool.iota(spare_i[:], pattern=[[P, PLACES]], base=TOP * T + 1, channel_multiplier=1).then_inc(consts, 1)
            pool.memset(cum[:], 0.0).then_inc(consts, 1)
            pool.memset(end[:], 0.0).then_inc(consts, 1)
            pool.wait_ge(consts, 7)
            for to, i in ((tile_f, tile_no), (earlier, earlier_i), (lane, lane_i), (row, row_i), (spare, spare_i)):
                pool.tensor_copy(to[:], i[:]).then_inc(consts, 1)
            pool.wait_ge(consts, 12)
            row_kt = row[:].rearrange("p k t -> p (k t)")
            for q in range(4):
                ks = quarter(q)
                pool.wait_ge(in_column_ok, q + 1)
                pool.tensor_tensor(column_is[:, ks], in_column[:, ks], bc(row_kt[:, ks], 2, PLACES), ALU.mult).then_inc(column_ok, 1)

        @block.scalar
        def _(act):
            def apply(c):
                act.wait_ge(norm_ok, c + 1)
                for t in range(c * TPC, (c + 1) * TPC):
                    act.activation(x2[:, t], x2[:, t], ACT.Identity, bias=nb[:, t:t + 1], scale=rs[:, t:t + 1]).then_inc(x2_ok, 1)

            def take_turned(c):
                for t in range(c * TPC, (c + 1) * TPC):
                    act.wait_ge(x2T_mm, t + 1)
                    if t >= 4:
                        act.wait_ge(lg_mm, t - 3)
                    act.activation(x2T[:, t % 4].rearrange("p h n -> p (h n)"), bank[2 + t % 2][:, 0:D], ACT.Copy).then_inc(x2T_ok, 1)

            act.activation(warm[:], ones[:, 0:1], ACT.Exp)
            for c in range(NC):
                apply(c)
                take_turned(c)
            act.wait_ge(sub_ok, 1)
            act.activation(pr[:], lg[:], ACT.Exp).then_inc(exp_ok, 1)

        @block.vector
        def _(v):
            k = Chain(v, vchain)
            for c in range(NC):
                tiles = list(range(c * TPC, (c + 1) * TPC))
                v.wait_ge(loaded[c], 16)
                for t in tiles:
                    v.wait_ge(turn_mm, t + 1)
                    v.tensor_tensor(x2[:, t], bank[TURN_BANKS[t % 4]][:, 0:D], x2[:, t], ALU.add).then_inc(z_ok, 1)
                v.wait_ge(z_ok, tiles[-1] + 1)
                layer_norm_factors(v, k, tiles, x2, stats, mv, rs, tmp, nb, norm_ok)
            v.wait_ge(lg_mm, NT)
            v.wait_ge(ld_r, 48)
            k.step(v.tensor_tensor(lg[:], bank[4][:, 0:NT * NE].rearrange("p (t e) -> p t e", e=NE), bc(rb[:, 0], 1, NT), ALU.add))
            k.step(v.tensor_tensor(lg[:], lg[:], bc(rb[:, 1], 1, NT), ALU.add))
            k.step(v.tensor_reduce(red[:], lg[:], AX_X, ALU.max))
            v.tensor_tensor(lg[:], lg[:], bc(red[:], 2, NE), ALU.subtract).then_inc(sub_ok, 1)
            v.wait_ge(exp_ok, 1)
            k.step(v.tensor_reduce(red[:], pr[:], AX_X, ALU.add))
            k.step(v.reciprocal(red[:], red[:]))
            k.step(v.tensor_tensor(pr[:], pr[:], bc(red[:], 2, NE), ALU.mult))
            v.wait_ge(consts, 12)
            for i in range(TOP):
                options = pr if i == 0 else left
                k.step(v.tensor_reduce(gate[:, i], options[:], AX_X, ALU.max))
                k.step(v.tensor_tensor(equal[:], options[:], bc(gate[:, i], 2, NE), ALU.is_equal))
                k.step(v.tensor_tensor(equal[:], equal[:], bc(earlier[:], 1, NT), ALU.mult))
                k.step(v.tensor_reduce(red[:], equal[:], AX_X, ALU.max))
                k.step(v.tensor_tensor(chosen[i][:], equal[:], bc(red[:], 2, NE), ALU.is_equal))
                if i == 0:
                    k.step(v.scalar_tensor_tensor(out=left[:], in0=chosen[0][:], scalar=-2.0, in1=pr[:], op0=ALU.mult, op1=ALU.add))
            v.tensor_tensor(sel[:], chosen[0][:], chosen[1][:], ALU.add).then_inc(sel_ok, 1)
            k.step(v.tensor_tensor(red[:], gate[:, 0], gate[:, 1], ALU.add))
            k.step(v.tensor_scalar(red[:], red[:], 1e-9, None, ALU.add))
            k.step(v.reciprocal(red[:], red[:]))
            for i in range(TOP):
                k.step(v.tensor_tensor(gate[:, i], gate[:, i], red[:], ALU.mult))
            v.wait_ge(pos_mm, 1)
            Z = NT // 2
            k.step(v.tensor_copy(cum[:, 0, Z:], bank[6][:, 0:NT * NE].rearrange("p (t e) -> p t e", e=NE)))
            at = 0
            for step in (1, 2, 4, 8):
                k.step(v.tensor_tensor(cum[:, 1 - at, Z:], cum[:, at, Z:], cum[:, at, Z - step:Z + NT - step], ALU.add))
                at = 1 - at
            k.step(v.tensor_scalar(cnt[:], cum[:, at, Z + NT - 1], float(SLOTS - 1), None, ALU.add))
            k.step(v.tensor_scalar(cnt[:], cnt[:], SHIFT, None, ALU.arith_shift_right))
            k.step(v.tensor_copy(ntile[:], cnt[:]))
            Y = NE // 2
            k.step(v.tensor_copy(end[:, 0, Y:], ntile[:]))
            to = 0
            for step in (1, 2, 4):
                k.step(v.tensor_tensor(end[:, 1 - to, Y:], end[:, to, Y:], end[:, to, Y - step:Y + NE - step], ALU.add))
                to = 1 - to
            k.step(v.tensor_tensor(start[:], end[:, to, Y:], ntile[:], ALU.subtract))
            k.step(v.tensor_scalar(start[:], start[:], float(SLOTS), None, ALU.mult))
            k.step(v.tensor_tensor(place[:], bank[5][:, 0:NT * NE].rearrange("p (t e) -> p t e", e=NE),
                                   cum[:, at, Z - 1:Z + NT - 1], ALU.add))
            k.step(v.tensor_tensor(place[:], place[:], bc(start[:], 1, NT), ALU.add))
            for i in range(TOP):
                k.step(v.tensor_tensor(equal[:], place[:], chosen[i][:], ALU.mult))
                k.step(v.tensor_reduce(pf[:, i], equal[:], AX_X, ALU.add))
            k.step(v.tensor_copy(pi[:], pf[:].rearrange("p k t -> p (k t)")))
            k.step(v.tensor_scalar(hi_i[:], pi[:], P.bit_length() - 1, None, ALU.arith_shift_right))
            k.step(v.tensor_scalar(lo_i[:], pi[:], P - 1, None, ALU.bitwise_and))
            k.step(v.tensor_copy(hi_f[:], hi_i[:]))
            k.step(v.tensor_copy(lo_f[:], lo_i[:]))
            for g in range(4):
                ks = quarter(g)
                v.tensor_tensor(in_column[:, ks], bc(lane[:, 0:PLACES], 1, KT // 4), bc(hi_f[:, ks], 2, PLACES), ALU.is_equal).then_inc(in_column_ok, 1)
                v.tensor_tensor(lane_is[:, g], bc(lane[:], 1, KT // 4), bc(lo_f[:, quarter(g)], 2, P), ALU.is_equal).then_inc(lane_ok, 1)
            k.step(v.tensor_tensor(emf[:], bc(tile_f[:], 2, NE), bc(end[:, to, Y:], 1, TILES), ALU.is_ge))
            k.step(v.tensor_reduce(emr[:], emf[:], AX_X, ALU.add))
            k.step(v.tensor_scalar(emap[:], emr[:], float(NE - 1), None, ALU.min))
            v.wait_ge(found_mm, 1)
            k.step(v.tensor_scalar(found[:], bank[7][:, 0:PLACES], -1.0, None, ALU.add))
            k.step(v.tensor_scalar(empty[:], bank[7][:, 0:PLACES], 0.0, None, ALU.is_equal))
            k.step(v.tensor_tensor(empty[:], empty[:], spare[:], ALU.mult))
            k.step(v.tensor_copy(found_i[:], found[:]))
            k.step(v.tensor_scalar(token_of[:], found_i[:], T - 1, None, ALU.bitwise_and))
            k.step(v.tensor_tensor(row_of[:], found[:], empty[:], ALU.add))

        @block.tensor
        def _(pe):
            def turn(t):
                if t >= 4:
                    pe.wait_ge(z_ok, t - 3)
                for h in range(DH):
                    last = pe.transpose(bank[TURN_BANKS[t % 4]][:, h * P:(h + 1) * P], sT[:, h, t * P:(t + 1) * P], ident[:])
                last.then_inc(turn_mm, 1)

            def turn_x2(t):
                pe.wait_ge(x2_ok, t + 1)
                if t >= 2:
                    pe.wait_ge(x2T_ok, t - 1)
                for h in range(DH):
                    last = pe.transpose(bank[2 + t % 2][:, h * P:(h + 1) * P], x2[:, t, h * P:(h + 1) * P], ident[:])
                last.then_inc(x2T_mm, 1)

            def logits(t):
                pe.wait_ge(x2T_ok, t + 1)
                if t == 0:
                    pe.wait_ge(ld_r, 48)
                for h in range(DH):
                    last = pe.matmul(bank[4][:, t * NE:(t + 1) * NE], x2T[:, t % 4, h], rw[:, h],
                                     start=(h == 0), stop=(h == DH - 1))
                last.then_inc(lg_mm, 1)

            for t in range(TPC):
                turn(t)
            for t in range(NT + 2):
                if t % TPC == 0 and t + TPC < NT:
                    for u in range(t + TPC, t + 2 * TPC):
                        turn(u)
                if t < NT:
                    turn_x2(t)
                if t >= 2:
                    logits(t - 2)
            pe.wait_ge(consts, 12)
            pe.wait_ge(sel_ok, 1)
            pe.matmul(bank[5][:, 0:NT * NE], tri[:], sel[:].rearrange("p t e -> p (t e)"), start=True, stop=True)
            pe.matmul(bank[6][:, 0:NT * NE], ones[:], sel[:].rearrange("p t e -> p (t e)"), start=True,
                      stop=True).then_inc(pos_mm, 1)
            for i in range(KT):
                pe.wait_ge(lane_ok, i // (KT // 4) + 1)
                pe.wait_ge(column_ok, i // (KT // 4) + 1)
                last = pe.matmul(bank[7][:, 0:PLACES], lane_is[:, i // (KT // 4), i % (KT // 4)], column_is[:, i],
                                 start=(i == 0), stop=(i == KT - 1))
            last.then_inc(found_mm, 1)


def experts(nc, io, shared):
    ident, sT, emap = shared["ident"], shared["sT"], shared["emap"]
    token_of, row_of = shared["token_of"], shared["row_of"]
    w1, w2, b1, b2, ld_e = (shared[n] for n in ("w1", "w2", "b1", "b2", "ld_e"))
    FP = FT // 2
    with ExitStack() as ctx:
        def sb(name, shape, dt=F32):
            return ctx.enter_context(nc.sbuf_tensor("e_" + name, shape, dt))

        def sem(name):
            return ctx.enter_context(nc.semaphore("e_" + name))

        bank = [ctx.enter_context(nc.psum_tensor(f"e_bank{i}", [P, CH], F32)) for i in range(8)]
        w1_hi, w1_lo = sb("w1_hi", [P, DH, F], F32R), sb("w1_lo", [P, DH, F], F32R)
        w2_hi, w2_lo = sb("w2_hi", [P, FT, D], F32R), sb("w2_lo", [P, FT, D], F32R)
        xT_hi, xT_lo = sb("xT_hi", [P, 2, DH, SLOTS], F32R), sb("xT_lo", [P, 2, DH, SLOTS], F32R)
        g_hi, g_lo = sb("g_hi", [P, FT, SLOTS], F32R), sb("g_lo", [P, FT, SLOTS], F32R)
        room = sT[:].rearrange("p c (a n) -> p (c a) n", n=CH)
        xg = [room[:, i].rearrange("p (s d) -> p s d", s=SH) for i in range(2)]
        y = [room[:, 2 + i].rearrange("p (s d) -> p s d", s=SH) for i in range(2)]
        g32 = [room[:, 4 + i].rearrange("p (f n) -> p f n", f=2) for i in range(2)]

        tokens, rows = sb("tokens", [P, 2 * SH], I32), sb("rows", [P, 2 * SH], I32)
        tokens_ok, rows_ok = sem("tokens_ok"), sem("rows_ok")
        passed = sem("passed")

        ld_x, y_out = [sem("ld_x0"), sem("ld_x1")], [sem("y_out0"), sem("y_out1")]
        xT_mm, xT_hi_ok, xT_lo_ok, w1_hi_ok, w1_lo_ok, w2_hi_ok, w2_hi_last, w2_lo_ok = (
            sem(n) for n in ("xT_mm", "xT_hi_ok", "xT_lo_ok", "w1_hi_ok", "w1_lo_ok", "w2_hi_ok", "w2_hi_last", "w2_lo_ok"))
        up_mm, g32_ok, g_hi_ok, g_lo_ok, y_mm, y_ok = (
            sem(n) for n in ("up_mm", "g32_ok", "g_hi_ok", "g_lo_ok", "y_mm", "y_ok"))
        block = ctx.enter_context(nc.Block())

        @block.sync
        def _(sp):
            sp.wait_ge(w1_hi_ok, TILES * FP)
            sp.wait_ge(w1_lo_ok, TILES * FP)
            sp.dma_start(shared["rows_back"], io["x2"].rearrange("(t p) d -> p t d", p=P)).then_inc(shared["ld_back"], 16)

        @block.gpsimd
        def _(pool):
            def take(i, slot, first=False):
                if not first:
                    pool.wait_ge(xT_mm, i - 1)
                pool.tensor_copy(tokens[:, slot * SH:(slot + 1) * SH], token_of[:, bass.ds(i * SH, SH)]).then_inc(tokens_ok, 1)
                pool.wait_ge(tokens_ok, i + 1)
                pool.sem_inc(passed, 1)
                for s in range(SH):
                    pool.indirect_dma_start(out=xg[slot][:, s], out_offset=None, in_=io["x2"],
                                            in_offset=bass.IndirectOffsetOnAxis(tokens[:, slot * SH + s:slot * SH + s + 1], 0)).then_inc(ld_x[slot], 16)

            def give(i, slot):
                pool.wait_ge(y_ok, SH * i + 1)
                pool.tensor_copy(rows[:, slot * SH:(slot + 1) * SH], row_of[:, bass.ds(i * SH, SH)]).then_inc(rows_ok, 1)
                pool.wait_ge(rows_ok, i + 1)
                for s in range(SH):
                    pool.wait_ge(y_ok, SH * i + s + 1)
                    pool.sem_inc(passed, 1)
                    pool.indirect_dma_start(out=io["results"], out_offset=bass.IndirectOffsetOnAxis(rows[:, slot * SH + s:slot * SH + s + 1], 0),
                                            in_=y[slot][:, s], in_offset=None).then_inc(y_out[slot], 16)

            def weights(i, first=False):
                ex = pool.value_load(emap[0:1, bass.ds(i, 1)], min_val=0, max_val=NE - 1)
                if not first:
                    pool.wait_ge(y_mm, i * SH)
                for f in range(FP - 1):
                    pool.tensor_copy(w2_hi[:, 2 * f:2 * f + 2], w2[:, bass.ds(ex, 1), 2 * f:2 * f + 2].rearrange("p e c f -> p (e c) f")).then_inc(w2_hi_ok, 1)

            take(0, 0, first=True)
            take(1, 1, first=True)
            pool.wait_ge(ld_e, 16 * (2 * NE + 2))
            weights(0, first=True)
            take(2, 0)
            weights(1)
            take(3, 1)
            give(0, 0)
            with pool.Fori(1, TILES // 2 - 1) as it:
                for slot in range(2):
                    i = it * 2 + slot
                    weights(i)
                    take(i + 2, slot)
                    give(i - 1, 1 - slot)
            weights(TILES - 3)
            take(TILES - 1, 0)
            give(TILES - 4, 1)
            for i in range(TILES - 2, TILES):
                weights(i)
                give(i - 1, (i - 1) % 2)
            give(TILES - 1, 0)
            pool.wait_ge(y_out[0], 16 * SH * (TILES // 2 + 1))
            pool.wait_ge(y_out[1], 16 * SH * (TILES // 2))

        @block.scalar
        def _(act):
            act.wait_ge(ld_e, 16 * (2 * NE + 2))

            def turn(i, slot):
                act.wait_ge(xT_mm, i + 1)
                act.activation(xT_hi[:, slot].rearrange("p c n -> p (c n)"), bank[0][:], ACT.Copy).then_inc(xT_hi_ok, 1)

            def w1_high(i, ex, f):
                cols = slice(f * 2 * P, (f + 1) * 2 * P)
                act.activation(w1_hi[:, :, cols], w1[:, bass.ds(ex, 1), :, cols].rearrange("p e c f -> p (e c) f"), ACT.Copy).then_inc(w1_hi_ok, 1)

            def body(i, slot, n, first=False, last=False):
                ex = act.value_load(emap[0:1, bass.ds(i, 1)], min_val=0, max_val=NE - 1)
                if not last:
                    nx = act.value_load(emap[0:1, bass.ds(i + 1, 1)], min_val=0, max_val=NE - 1)
                if not first:
                    act.wait_ge(y_mm, i * SH)
                act.activation(w2_hi[:, FT - 2:], w2[:, bass.ds(ex, 1), FT - 2:].rearrange("p e c f -> p (e c) f"), ACT.Copy).then_inc(w2_hi_last, 1)
                for f in range(FP):
                    act.wait_ge(up_mm, i * FP + f + 1)
                    if not (first and f < 2):
                        act.wait_ge(g_lo_ok, i * FP + f - 1)
                    for a in range(2):
                        act.activation(g32[f % 2][:, a], bank[1 + f % 2][:, a * SLOTS:(a + 1) * SLOTS], ACT.Gelu,
                                       bias=b1[:, bass.ds(ex * FT + (2 * f + a), 1)]).then_inc(g32_ok, 1)
                    act.wait_ge(g32_ok, (i * FP + f + 1) * 2)
                    if not first:
                        act.wait_ge(y_mm, i * SH)
                    act.activation(g_hi[:, 2 * f:2 * f + 2], g32[f % 2], ACT.Copy).then_inc(g_hi_ok, 1)
                    if f == FP - 1 and not last:
                        turn(i + 1, 1 - slot)
                if not last:
                    for f in range(FP):
                        w1_high(i + 1, nx, f)

            ex0 = act.value_load(emap[0:1, 0:1], min_val=0, max_val=NE - 1)
            for f in range(FP):
                w1_high(0, ex0, f)
            turn(0, 0)
            body(0, 0, 0, first=True)
            body(1, 1, 0)
            with act.Fori(1, TILES // 2) as it:
                body(it * 2, 0, it)
                body(it * 2 + 1, 1, it)
            body(TILES - 1, 0, TILES // 2, last=True)

        @block.vector
        def _(v):
            v.wait_ge(ld_e, 16 * (2 * NE + 2))

            def turn(i, slot):
                v.wait_ge(xT_hi_ok, i + 1)
                v.tensor_tensor(xT_lo[:, slot].rearrange("p c n -> p (c n)"), bank[0][:],
                                xT_hi[:, slot].bitcast(F32).rearrange("p c n -> p (c n)"), ALU.subtract).then_inc(xT_lo_ok, 1)

            def split_w1(i, ex, f):
                cols = slice(f * 2 * P, (f + 1) * 2 * P)
                v.wait_ge(w1_hi_ok, i * FP + f + 1)
                v.tensor_tensor(w1_lo[:, :, cols], w1[:, bass.ds(ex, 1), :, cols].rearrange("p e c f -> p (e c) f"),
                                w1_hi[:, :, cols].bitcast(F32), ALU.subtract).then_inc(w1_lo_ok, 1)

            def split_w2(i, ex, f):
                if f == FP - 1:
                    v.wait_ge(w2_hi_last, i + 1)
                else:
                    v.wait_ge(w2_hi_ok, i * (FP - 1) + f + 1)
                v.tensor_tensor(w2_lo[:, 2 * f:2 * f + 2], w2[:, bass.ds(ex, 1), 2 * f:2 * f + 2].rearrange("p e c f -> p (e c) f"),
                                w2_hi[:, 2 * f:2 * f + 2].bitcast(F32), ALU.subtract).then_inc(w2_lo_ok, 1)

            def body(i, slot, n, warm_up=False, last=False):
                ex = v.value_load(emap[0:1, bass.ds(i, 1)], min_val=0, max_val=NE - 1)
                if not last:
                    nx = v.value_load(emap[0:1, bass.ds(i + 1, 1)], min_val=0, max_val=NE - 1)
                for f in range(FP):
                    split_w2(i, ex, (f - 1) % FP)
                    v.wait_ge(g_hi_ok, i * FP + f + 1)
                    v.tensor_tensor(g_lo[:, 2 * f:2 * f + 2], g32[f % 2], g_hi[:, 2 * f:2 * f + 2].bitcast(F32),
                                    ALU.subtract).then_inc(g_lo_ok, 1)
                    if f == FP - 1 and not last:
                        turn(i + 1, 1 - slot)
                for s in range(SH):
                    if not last:
                        split_w1(i + 1, nx, 2 * s)
                        split_w1(i + 1, nx, 2 * s + 1)
                    v.wait_ge(y_mm, i * SH + s + 1)
                    if s == 0 and not warm_up:
                        v.wait_ge(y_out[slot], 16 * SH * n)
                    v.tensor_tensor(y[slot][:, s], bank[3 + s][:, 0:D], b2[:, bass.ds(ex * D, D)], ALU.add).then_inc(y_ok, 1)

            ex0 = v.value_load(emap[0:1, 0:1], min_val=0, max_val=NE - 1)
            for f in range(FP):
                split_w1(0, ex0, f)
            turn(0, 0)
            body(0, 0, 0, warm_up=True)
            body(1, 1, 0, warm_up=True)
            with v.Fori(1, TILES // 2) as it:
                body(it * 2, 0, it)
                body(it * 2 + 1, 1, it)
            body(TILES - 1, 0, TILES // 2, last=True)

        @block.tensor
        def _(pe):
            def turn(i, slot, n):
                pe.wait_ge(ld_x[slot], 16 * SH * (n + 1))
                for h in range(DH):
                    for s in range(SH):
                        last = pe.transpose(bank[0][:, (h * SH + s) * P:(h * SH + s + 1) * P], xg[slot][:, s, h * P:(h + 1) * P], ident[:])
                last.then_inc(xT_mm, 1)

            def body(i, slot, n, first=False, last=False):
                pe.wait_ge(xT_lo_ok, i + 1)
                for f in range(FP):
                    pe.wait_ge(w1_lo_ok, i * FP + f + 1)
                    if not (first and f < 2):
                        pe.wait_ge(g32_ok, (i * FP + f - 1) * 2)
                    for a in range(2):
                        fs = slice((2 * f + a) * P, (2 * f + a + 1) * P)
                        for h in range(DH):
                            mm = three_pass(pe, bank[1 + f % 2][:, a * SLOTS:(a + 1) * SLOTS], w1_hi[:, h, fs], w1_lo[:, h, fs],
                                            xT_hi[:, slot, h], xT_lo[:, slot, h], h == 0, h == DH - 1)
                    mm.then_inc(up_mm, 1)
                    if f == FP - 1 and not last:
                        turn(i + 1, 1 - slot, n + slot)
                for s in range(SH):
                    if not first:
                        pe.wait_ge(y_ok, (i - 1) * SH + s + 1)
                    for f in range(FT):
                        if s == 0 and f % 2 == 0:
                            pe.wait_ge(w2_lo_ok, i * FP + min(f // 2 + 2, FP))
                            pe.wait_ge(g_lo_ok, i * FP + f // 2 + 1)
                        ss = slice(s * P, (s + 1) * P)
                        mm = three_pass(pe, bank[3 + s][:, 0:D], g_hi[:, f, ss], g_lo[:, f, ss], w2_hi[:, f], w2_lo[:, f],
                                        f == 0, f == FT - 1)
                    mm.then_inc(y_mm, 1)

            turn(0, 0, 0)
            body(0, 0, 0, first=True)
            body(1, 1, 0)
            with pe.Fori(1, TILES // 2) as it:
                body(it * 2, 0, it)
                body(it * 2 + 1, 1, it)
            body(TILES - 1, 0, TILES // 2, last=True)


def combine(nc, io, shared):
    gate, x2, yk, ld_back = shared["gate"], shared["rows_back"], shared["results_back"], shared["ld_back"]
    with ExitStack() as ctx:
        def sb(name, shape, dt=F32):
            return ctx.enter_context(nc.sbuf_tensor("c_" + name, shape, dt))

        def sem(name):
            return ctx.enter_context(nc.semaphore("c_" + name))

        stats, mv = sb("stats", [P, NT, 6]), sb("mv", [P, NT, 2])
        nb, rs, tmp = sb("nb", [P, NT]), sb("rs", [P, NT]), sb("tmp", [P, NT])
        vchain, gated, summed, norm_ok, out_ok, stored = (sem(n) for n in ("vchain", "gated", "summed", "norm_ok", "out_ok", "stored"))
        loaded, BEFORE = shared["loaded"], 16
        block = ctx.enter_context(nc.Block())

        def chunk(c):
            return slice(c * TPC, (c + 1) * TPC)

        @block.sync
        def _(sp):
            for c in range(NC):
                for k in range(TOP):
                    results = io["results"][k * T:(k + 1) * T].rearrange("(t p) d -> p t d", p=P)
                    sp.dma_start(yk[:, k, chunk(c)], results[:, chunk(c)]).then_inc(loaded[c], 16)
            out = io["out"].rearrange("(t p) d -> p t d", p=P)
            for c in range(NC):
                sp.wait_ge(out_ok, (c + 1) * TPC)
                sp.dma_start(out[:, chunk(c)], x2[:, chunk(c)]).then_inc(stored, 16)
            sp.wait_ge(stored, 16 * NC)

        @block.scalar
        def _(act):
            def weigh(c):
                act.wait_ge(loaded[c], BEFORE + 16 * TOP)
                for t in range(c * TPC, (c + 1) * TPC):
                    act.activation(yk[:, 0, t], yk[:, 0, t], ACT.Copy, scale=gate[:, 0, t:t + 1]).then_inc(gated, 1)

            weigh(0)
            for c in range(NC):
                if c + 1 < NC:
                    weigh(c + 1)
                act.wait_ge(norm_ok, c + 1)
                for t in range(c * TPC, (c + 1) * TPC):
                    act.activation(x2[:, t], x2[:, t], ACT.Identity, bias=nb[:, t:t + 1], scale=rs[:, t:t + 1]).then_inc(out_ok, 1)

        @block.gpsimd
        def _(pool):
            pool.wait_ge(ld_back, 16)
            for c in range(NC):
                for t in range(c * TPC, (c + 1) * TPC):
                    pool.wait_ge(gated, t + 1)
                    pool.tensor_tensor(x2[:, t], x2[:, t], yk[:, 0, t], ALU.add).then_inc(summed, 1)

        @block.vector
        def _(v):
            k = Chain(v, vchain)
            for c in range(NC):
                tiles = list(range(c * TPC, (c + 1) * TPC))
                v.wait_ge(loaded[c], BEFORE + 16 * TOP)
                for t in tiles:
                    v.wait_ge(summed, t + 1)
                    mark = k.mark(v.scalar_tensor_tensor(out=x2[:, t], in0=yk[:, 1, t], scalar=gate[:, 1, t:t + 1],
                                                         in1=x2[:, t], op0=ALU.mult, op1=ALU.add))
                v.wait_ge(vchain, mark)
                layer_norm_factors(v, k, tiles, x2, stats, mv, rs, tmp, nb, norm_ok)



def program(nc, io):
    with ExitStack() as ctx:
        def sb(name, shape, dt=F32):
            return ctx.enter_context(nc.sbuf_tensor(name, shape, dt))

        shared = {"ident": sb("ident", [P, P]), "ones": sb("ones", [P, P]), "sT": sb("sT", [P, DH, T])}
        shared["loaded"] = [ctx.enter_context(nc.semaphore(f"loaded{c}")) for c in range(NC)]
        decay_attention_and_mlp(nc, io, shared)
        shared |= {"ld_e": ctx.enter_context(nc.semaphore("ld_e"))}
        cross_attention(nc, io, shared)
        sb("w1_place", [P, NE, DH, F])
        w1 = shared["w1"]
        w2, b1, b2 = sb("w2", [P, NE, FT, D]), sb("b1", [P, NE * FT]), sb("b2", [P, NE * D])
        place_of_w1 = w1[:].rearrange("p e c f -> p (e c f)")
        shared |= {"emap": sb("emap", [P, TILES], I32), "token_of": sb("token_of", [P, PLACES], I32),
                   "row_of": sb("row_of", [P, PLACES], I32), "gate": sb("gate", [P, TOP, NT]), "w2": w2, "b1": b1, "b2": b2,
                   "rows_back": place_of_w1[:, 0:NT * D].rearrange("p (t d) -> p t d", t=NT),
                   "results_back": place_of_w1[:, NT * D:3 * NT * D].rearrange("p (k t d) -> p k t d", k=TOP, t=NT),
                   "ld_back": ctx.enter_context(nc.semaphore("ld_back"))}
        route(nc, io, shared)
        experts(nc, io, shared)
        combine(nc, io, shared)


def kernel(**inputs):
    import numpy as np
    import concourse.bacc as bacc
    from concourse.bass_utils import run_bass_kernel_spmd

    a = {name: np.asarray(value) for name, value in inputs.items()}

    def turned(x):
        return np.ascontiguousarray(x.T)

    def columns(*names):
        return np.ascontiguousarray(np.concatenate([a[n].reshape(-1, P).T for n in names], axis=1))

    x, context = a["x"][0], a["ctx_1024"][0]
    send = {
        "x": x, "xT": turned(x), "u": a["L0_attn_u"], "v": a["L0_attn_v"],
        "decay": a["L0_attn_decay_logit"], "alpha": a["L0_attn_alpha_logit"],
        "gate": a["L0_attn_k_base_gate_logit"].reshape(1), "taps": a["L0_attn_k_base_kernel"],
        "projT": turned(a["L0_attn_proj_w"]), "proj_b": a["L0_attn_proj_b"], "norm1_w": a["L0_attn_norm1_w"],
        "mlp_w1": a["L0_attn_mlp_w1"], "mlp_w2": a["L0_attn_mlp_w2"], "mlp_b2": a["L0_attn_mlp_b2"],
        "a_cols": columns("L0_attn_norm1_w", "L0_attn_norm2_w", "L0_attn_mlp_b1"),
        "ctx": context, "ctxT": turned(context),
        "Wq": a["L0_xattn_Wq"], "Wk": a["L0_xattn_Wk"], "Wv": a["L0_xattn_Wv"],
        "gru_wiT": turned(a["L0_xattn_gru_wi"]), "gru_whT": turned(a["L0_xattn_gru_wh"]),
        "x_cols": columns("L0_xattn_input_norm_w", "L0_xattn_slot_norm_w"),
        "gru_cols": columns("L0_xattn_gru_bi", "L0_xattn_gru_bh"),
        "router_w": a["L0_ffn_router_w"], "router_b": a["L0_ffn_router_b"], "expert_bias": a["L0_ffn_expert_bias"],
        "w1": a["L0_ffn_w1"], "w2": a["L0_ffn_w2"], "b1_cols": columns("L0_ffn_b1"), "b2": a["L0_ffn_b2"],
    }
    nc = bacc.Bacc("TRN2", target_bir_lowering=False, num_devices=1, dynamic_dma_scratch_size=4096)
    io = {k: nc.dram_tensor(f"in_{k}", v.shape, F32, kind="ExternalInput").ap() for k, v in send.items()}
    for name, shape in (("x1", (T, D)), ("x2", (T, D)), ("results", (TOP * T + ROWS, D))):
        io[name] = nc.dram_tensor(f"scratch_{name}", shape, F32).ap()
    io["out"] = nc.dram_tensor("out", (T, D), F32, kind="ExternalOutput").ap()
    program(nc, io)
    r = run_bass_kernel_spmd(nc, [{f"in_{k}": v for k, v in send.items()}], core_ids=[0])
    return r.results[0]["out"].reshape(1, T, D)
```
